# Optimizing a Trainium2 kernel written in Bass

```python
import numpy as np
import jax
import jax.numpy as jnp

def _softmax(x, axis=-1):
    return jax.nn.softmax(x, axis=axis)

def _gelu(x):
    return jax.nn.gelu(x, approximate=True)

def _silu(x):
    return jax.nn.silu(x)

def _sigmoid(x):
    return jax.nn.sigmoid(x)

def _layernorm(x, axis=-1, eps=1e-05):
    m = jnp.mean(x, axis=axis, keepdims=True)
    v = jnp.var(x, axis=axis, keepdims=True)
    return (x - m) / jnp.sqrt(v + eps)

def _scatter_add(tgt, idx, src, axis=0):
    return tgt.at[idx].add(src)

def _segment_sum(src, seg, n):
    return jax.ops.segment_sum(src, seg, n)
kernel_name = 'mk_gnn_ffn_d2_gnn_r32_a31397'

def setup_inputs(seed: int=0):
    np.random.seed(seed)
    _w = jnp.asarray

    def _rec_inputs():
        import jax
        import jax.numpy as jnp
        _gk = jax.random.key(seed)
        x = -0.0002117 + 1 * jax.random.normal(jax.random.fold_in(_gk, 1), (10000, 512), jnp.float32)
        src = jax.random.randint(jax.random.fold_in(_gk, 2), (10000,), 0, 10000, jnp.int32)
        dst = jax.random.randint(jax.random.fold_in(_gk, 3), (10000,), 0, 10000, jnp.int32)
        _o = jnp.argsort(dst, stable=True)
        src = src[_o]
        dst = dst[_o]
        return (x, src, dst)
    x, src, dst = _rec_inputs()

    def _L0_gnn_setup():
        import jax, jax.numpy as jnp
        import numpy as np
        N = 50000
        E = 25000
        F_IN = 512
        F_OUT = 512
        key = jax.random.key(seed)
        k_feat, k_src, k_dst, k_w1, k_b1, k_w2, k_b2 = jax.random.split(key, 7)
        feat = jax.random.normal(k_feat, (N, F_IN), dtype=jnp.float32)
        src_idx = jax.random.randint(k_src, (E,), 0, N, dtype=jnp.int32)
        dst_idx = jax.random.randint(k_dst, (E,), 0, N, dtype=jnp.int32)
        deg = jax.ops.segment_sum(jnp.ones((E,), jnp.float32), dst_idx, num_segments=N)
        in_deg = jnp.maximum(deg, 1.0)
        stdv = 1.0 / np.sqrt(F_IN)
        W1 = jax.random.uniform(k_w1, (F_OUT, F_IN), jnp.float32, -stdv, stdv)
        b1 = jax.random.uniform(k_b1, (F_OUT,), jnp.float32, -stdv, stdv)
        W2 = jax.random.uniform(k_w2, (F_OUT, F_IN), jnp.float32, -stdv, stdv)
        b2 = jax.random.uniform(k_b2, (F_OUT,), jnp.float32, -stdv, stdv)
        return {'feat': feat, 'src_idx': src_idx, 'dst_idx': dst_idx, 'in_deg': in_deg, 'W1': W1, 'b1': b1, 'W2': W2, 'b2': b2}
    _L0_gnn_all = _L0_gnn_setup()
    _L0_gnn_in = {k: v for k, v in _L0_gnn_all.items() if k in ('W1', 'b1', 'W2', 'b2')}
    del _L0_gnn_all

    def _L0_ffn_setup():
        import jax, jax.numpy as jnp
        import numpy as np
        B, S, D, F, E, NS, K = (2, 64, 512, 64, 8, 2, 2)
        key = jax.random.key(seed)
        ks = jax.random.split(key, 6)
        scale = 0.02

        def p(k, shape):
            return jax.random.normal(k, shape, jnp.float32) * scale
        return {'x': jax.random.normal(ks[0], (B, S, D), jnp.float32), 'gate_w': p(ks[1], (E, D)), 'gate_b': jnp.zeros((E,), jnp.float32), 'sw1': p(ks[2], (NS, F, D)), 'sb1': jnp.zeros((NS, F), jnp.float32), 'sw2': p(ks[3], (NS, D, F)), 'sb2': jnp.zeros((NS, D), jnp.float32), 'rw1': p(ks[4], (E, F, D)), 'rb1': jnp.zeros((E, F), jnp.float32), 'rw2': p(ks[5], (E, D, F)), 'rb2': jnp.zeros((E, D), jnp.float32)}
    _L0_ffn_all = _L0_ffn_setup()
    _L0_ffn_in = {k: v for k, v in _L0_ffn_all.items() if k in ('gate_w', 'gate_b', 'sw1', 'sb1', 'sw2', 'sb2', 'rw1', 'rb1', 'rw2', 'rb2')}
    del _L0_ffn_all

    def _L1_gnn_setup():
        import jax, jax.numpy as jnp
        import numpy as np
        N_NODES = 10000
        N_EDGES = 5000
        D = 512
        key = jax.random.key(seed)
        k_h, k_e, k_w1, k_w2 = jax.random.split(key, 4)
        h = jax.random.normal(k_h, (N_NODES, D), dtype=jnp.float32)
        edge_index = jax.random.randint(k_e, (2, N_EDGES), 0, N_NODES, dtype=jnp.int64)
        scale = 1.0 / np.sqrt(D)
        W1 = jax.random.normal(k_w1, (D, D), dtype=jnp.float32) * scale
        b1 = jnp.zeros((D,), dtype=jnp.float32)
        W2 = jax.random.normal(k_w2, (D, D), dtype=jnp.float32) * scale
        b2 = jnp.zeros((D,), dtype=jnp.float32)
        return {'h': h, 'edge_index': edge_index, 'W1': W1, 'b1': b1, 'W2': W2, 'b2': b2}
    _L1_gnn_all = _L1_gnn_setup()
    _L1_gnn_in = {k: v for k, v in _L1_gnn_all.items() if k in ('W1', 'b1', 'W2', 'b2')}
    del _L1_gnn_all

    def _L1_ffn_setup():
        import jax, jax.numpy as jnp
        import numpy as np
        E, TOPK, H, DK, DV, D = (4, 2, 8, 64, 64, 512)
        B, L = (4, 1024)
        VDIM = H * DV

        def _silu(x):
            return x * jax.nn.sigmoid(x)

        def _l2norm(x):
            return x * jax.lax.rsqrt(jnp.sum(x * x, axis=-1, keepdims=True) + 1e-06)

        def _forward(h, Wq, Wgate, Wk, Wv, Wb, Wa, A_log, dt_bias, Wg, o_norm_weight, Wo):
            Bs, Ls, _ = h.shape
            scores = jax.nn.softmax((h @ Wgate).astype(jnp.float32), axis=-1)
            rw, sel = jax.lax.top_k(scores, TOPK)
            rw = rw / jnp.sum(rw, axis=-1, keepdims=True)
            bi = jnp.arange(Bs)[:, None, None]
            li = jnp.arange(Ls)[None, :, None]
            w_full = jnp.zeros((Bs, Ls, E), jnp.float32).at[bi, li, sel].set(rw)
            m = jnp.transpose(w_full > 0, (2, 0, 1))
            q = _l2norm(_silu(h @ Wq).reshape(Bs, Ls, H, DK))
            k = _l2norm(_silu(h @ Wk).reshape(Bs, Ls, H, DK))
            v = _silu(h @ Wv).reshape(Bs, Ls, H, DV)
            beta = jax.nn.sigmoid(h @ Wb)
            g = -jnp.exp(A_log) * jax.nn.softplus((h @ Wa).astype(jnp.float32) + dt_bias)
            beta_e = beta[None] * m[..., None]
            g_e = jnp.where(m[..., None], g[None], 0.0)
            scale = DK ** (-0.5)
            xs = (jnp.moveaxis(q, 1, 0), jnp.moveaxis(k, 1, 0), jnp.moveaxis(v, 1, 0), jnp.moveaxis(beta_e, 2, 0), jnp.moveaxis(g_e, 2, 0))

            def step(S, x):
                qt, kt, vt, bt, gt = x
                S = S * jnp.exp(gt)[..., None, None]
                kv = jnp.einsum('bhk,ebhkv->ebhv', kt, S)
                delta = (vt[None] - kv) * bt[..., None]
                S = S + kt[None, :, :, :, None] * delta[..., None, :]
                ot = jnp.einsum('bhk,ebhkv->ebhv', qt * scale, S)
                return (S, ot)
            S0 = jnp.zeros((E, Bs, H, DK, DV), jnp.float32)
            _, o = jax.lax.scan(step, S0, xs)
            o = jnp.moveaxis(o, 0, 2)
            core = jnp.einsum('ble,eblhv->blhv', w_full, o)
            gate = _silu((h @ Wg).reshape(Bs, Ls, H, DV))
            core = core * jax.lax.rsqrt(jnp.mean(core * core, axis=-1, keepdims=True) + 1e-05)
            core = core * o_norm_weight * gate
            return core.reshape(Bs, Ls, VDIM) @ Wo
        key = jax.random.key(seed)
        ks = jax.random.split(key, 12)
        std = 0.02
        h = jax.random.normal(ks[0], (B, L, D), jnp.float32)
        Wq = jax.random.normal(ks[1], (D, H * DK), jnp.float32) * std
        Wgate = jax.random.normal(ks[2], (D, E), jnp.float32) * std
        Wk = jax.random.normal(ks[3], (D, H * DK), jnp.float32) * std
        Wv = jax.random.normal(ks[4], (D, VDIM), jnp.float32) * std
        Wb = jax.random.normal(ks[5], (D, H), jnp.float32) * std
        Wa = jax.random.normal(ks[6], (D, H), jnp.float32) * std
        Wg = jax.random.normal(ks[7], (D, VDIM), jnp.float32) * std
        Wo = jax.random.normal(ks[8], (VDIM, D), jnp.float32) * std
        A = jax.random.uniform(ks[9], (H,), jnp.float32, 0.0001, 16.0)
        A_log = jnp.log(A)
        dt = jnp.exp(jax.random.uniform(ks[10], (H,), jnp.float32) * (np.float32(np.log(0.1)) - np.float32(np.log(0.001))) + np.float32(np.log(0.001)))
        dt = jnp.maximum(dt, 0.0001)
        dt_bias = dt + jnp.log(-jnp.expm1(-dt))
        o_norm_weight = jnp.ones((DV,), jnp.float32)
        return {'hidden_states': h, 'Wq': Wq, 'Wgate': Wgate, 'Wk': Wk, 'Wv': Wv, 'Wb': Wb, 'Wa': Wa, 'A_log': A_log, 'dt_bias': dt_bias, 'Wg': Wg, 'o_norm_weight': o_norm_weight, 'Wo': Wo}
    _L1_ffn_all = _L1_ffn_setup()
    _L1_ffn_in = {k: v for k, v in _L1_ffn_all.items() if k in ('Wq', 'Wgate', 'Wk', 'Wv', 'Wb', 'Wa', 'A_log', 'dt_bias', 'Wg', 'o_norm_weight', 'Wo')}
    del _L1_ffn_all
    return {'x': x, 'src': src, 'dst': dst, 'L0_gnn_W1': _L0_gnn_in['W1'], 'L0_gnn_b1': _L0_gnn_in['b1'], 'L0_gnn_W2': _L0_gnn_in['W2'], 'L0_gnn_b2': _L0_gnn_in['b2'], 'L0_ffn_gate_w': _L0_ffn_in['gate_w'], 'L0_ffn_gate_b': _L0_ffn_in['gate_b'], 'L0_ffn_sw1': _L0_ffn_in['sw1'], 'L0_ffn_sb1': _L0_ffn_in['sb1'], 'L0_ffn_sw2': _L0_ffn_in['sw2'], 'L0_ffn_sb2': _L0_ffn_in['sb2'], 'L0_ffn_rw1': _L0_ffn_in['rw1'], 'L0_ffn_rb1': _L0_ffn_in['rb1'], 'L0_ffn_rw2': _L0_ffn_in['rw2'], 'L0_ffn_rb2': _L0_ffn_in['rb2'], 'L1_gnn_W1': _L1_gnn_in['W1'], 'L1_gnn_b1': _L1_gnn_in['b1'], 'L1_gnn_W2': _L1_gnn_in['W2'], 'L1_gnn_b2': _L1_gnn_in['b2'], 'L1_ffn_Wq': _L1_ffn_in['Wq'], 'L1_ffn_Wgate': _L1_ffn_in['Wgate'], 'L1_ffn_Wk': _L1_ffn_in['Wk'], 'L1_ffn_Wv': _L1_ffn_in['Wv'], 'L1_ffn_Wb': _L1_ffn_in['Wb'], 'L1_ffn_Wa': _L1_ffn_in['Wa'], 'L1_ffn_A_log': _L1_ffn_in['A_log'], 'L1_ffn_dt_bias': _L1_ffn_in['dt_bias'], 'L1_ffn_Wg': _L1_ffn_in['Wg'], 'L1_ffn_o_norm_weight': _L1_ffn_in['o_norm_weight'], 'L1_ffn_Wo': _L1_ffn_in['Wo']}

def reference(x, src, dst, L0_gnn_W1, L0_gnn_b1, L0_gnn_W2, L0_gnn_b2, L0_ffn_gate_w, L0_ffn_gate_b, L0_ffn_sw1, L0_ffn_sb1, L0_ffn_sw2, L0_ffn_sb2, L0_ffn_rw1, L0_ffn_rb1, L0_ffn_rw2, L0_ffn_rb2, L1_gnn_W1, L1_gnn_b1, L1_gnn_W2, L1_gnn_b2, L1_ffn_Wq, L1_ffn_Wgate, L1_ffn_Wk, L1_ffn_Wv, L1_ffn_Wb, L1_ffn_Wa, L1_ffn_A_log, L1_ffn_dt_bias, L1_ffn_Wg, L1_ffn_o_norm_weight, L1_ffn_Wo):
    import jax
    import jax.numpy as jnp

    def _L0_gnn_ref(feat, src_idx, dst_idx, in_deg, W1, b1, W2, b2):
        import jax, jax.numpy as jnp
        import numpy as np
        N = 50000
        E = 25000
        F_IN = 512
        F_OUT = 512
        num_dst = in_deg.shape[0]
        agg = jax.ops.segment_sum(feat[src_idx], dst_idx, num_segments=num_dst)
        ah = agg / in_deg[:, None]
        out = jnp.einsum('nf,of->no', feat[:num_dst], W1) + b1 + jnp.einsum('nf,of->no', ah, W2) + b2
        return out

    def _L0_ffn_ref(x, gate_w, gate_b, sw1, sb1, sw2, sb2, rw1, rb1, rw2, rb2):
        import jax, jax.numpy as jnp
        import numpy as np
        B, S, D, F, E, NS, K = (2, 64, 512, 64, 8, 2, 2)
        b, s, d = x.shape
        t = x.reshape(-1, d)
        T = t.shape[0]
        hs = jax.nn.gelu(jnp.einsum('td,nfd->ntf', t, sw1) + sb1[:, None, :], approximate=False)
        shared = jnp.einsum('ntf,ndf->td', hs, sw2) + sb2.sum(axis=0)
        logits = t @ gate_w.T + gate_b
        probs = jax.nn.softmax(logits, axis=-1)
        top_v, top_i = jax.lax.top_k(probs, K)
        cw = jnp.zeros_like(probs).at[jnp.arange(T)[:, None], top_i].add(top_v)
        hr = jax.nn.gelu(jnp.einsum('td,efd->etf', t, rw1) + rb1[:, None, :], approximate=False)
        oe = jnp.einsum('etf,edf->etd', hr, rw2) + rb2[:, None, :]
        routed = jnp.einsum('etd,te->td', oe, cw)
        return (shared + routed).reshape(b, s, d)

    def _L1_gnn_ref(h, edge_index, W1, b1, W2, b2):
        import jax, jax.numpy as jnp
        import numpy as np
        N_NODES = 10000
        N_EDGES = 5000
        D = 512
        send, rec = (edge_index[0], edge_index[1])
        agg = jax.ops.segment_sum(h[send], rec, num_segments=h.shape[0])
        x = h + agg
        x = jax.nn.relu(x @ W1 + b1)
        x = x @ W2 + b2
        return x

    def _L1_ffn_ref(hidden_states, Wq, Wgate, Wk, Wv, Wb, Wa, A_log, dt_bias, Wg, o_norm_weight, Wo):
        import jax, jax.numpy as jnp
        import numpy as np
        E, TOPK, H, DK, DV, D = (4, 2, 8, 64, 64, 512)
        B, L = (4, 1024)
        VDIM = H * DV

        def _silu(x):
            return x * jax.nn.sigmoid(x)

        def _l2norm(x):
            return x * jax.lax.rsqrt(jnp.sum(x * x, axis=-1, keepdims=True) + 1e-06)

        def _forward(h, Wq, Wgate, Wk, Wv, Wb, Wa, A_log, dt_bias, Wg, o_norm_weight, Wo):
            Bs, Ls, _ = h.shape
            scores = jax.nn.softmax((h @ Wgate).astype(jnp.float32), axis=-1)
            rw, sel = jax.lax.top_k(scores, TOPK)
            rw = rw / jnp.sum(rw, axis=-1, keepdims=True)
            bi = jnp.arange(Bs)[:, None, None]
            li = jnp.arange(Ls)[None, :, None]
            w_full = jnp.zeros((Bs, Ls, E), jnp.float32).at[bi, li, sel].set(rw)
            m = jnp.transpose(w_full > 0, (2, 0, 1))
            q = _l2norm(_silu(h @ Wq).reshape(Bs, Ls, H, DK))
            k = _l2norm(_silu(h @ Wk).reshape(Bs, Ls, H, DK))
            v = _silu(h @ Wv).reshape(Bs, Ls, H, DV)
            beta = jax.nn.sigmoid(h @ Wb)
            g = -jnp.exp(A_log) * jax.nn.softplus((h @ Wa).astype(jnp.float32) + dt_bias)
            beta_e = beta[None] * m[..., None]
            g_e = jnp.where(m[..., None], g[None], 0.0)
            scale = DK ** (-0.5)
            xs = (jnp.moveaxis(q, 1, 0), jnp.moveaxis(k, 1, 0), jnp.moveaxis(v, 1, 0), jnp.moveaxis(beta_e, 2, 0), jnp.moveaxis(g_e, 2, 0))

            def step(S, x):
                qt, kt, vt, bt, gt = x
                S = S * jnp.exp(gt)[..., None, None]
                kv = jnp.einsum('bhk,ebhkv->ebhv', kt, S)
                delta = (vt[None] - kv) * bt[..., None]
                S = S + kt[None, :, :, :, None] * delta[..., None, :]
                ot = jnp.einsum('bhk,ebhkv->ebhv', qt * scale, S)
                return (S, ot)
            S0 = jnp.zeros((E, Bs, H, DK, DV), jnp.float32)
            _, o = jax.lax.scan(step, S0, xs)
            o = jnp.moveaxis(o, 0, 2)
            core = jnp.einsum('ble,eblhv->blhv', w_full, o)
            gate = _silu((h @ Wg).reshape(Bs, Ls, H, DV))
            core = core * jax.lax.rsqrt(jnp.mean(core * core, axis=-1, keepdims=True) + 1e-05)
            core = core * o_norm_weight * gate
            return core.reshape(Bs, Ls, VDIM) @ Wo
        return _forward(hidden_states, Wq, Wgate, Wk, Wv, Wb, Wa, A_log, dt_bias, Wg, o_norm_weight, Wo)
    edge_index = jnp.stack([src, dst])
    deg = jnp.maximum(jax.ops.segment_sum(jnp.ones(dst.shape, jnp.float32), dst, num_segments=10000), 1.0)
    x = x + _L0_gnn_ref(_layernorm(x, axis=-1), src, dst, deg, L0_gnn_W1, L0_gnn_b1, L0_gnn_W2, L0_gnn_b2)
    x = x + _L0_ffn_ref(_layernorm(x, axis=-1)[None], L0_ffn_gate_w, L0_ffn_gate_b, L0_ffn_sw1, L0_ffn_sb1, L0_ffn_sw2, L0_ffn_sb2, L0_ffn_rw1, L0_ffn_rb1, L0_ffn_rw2, L0_ffn_rb2)[0]
    x = x + _L1_gnn_ref(_layernorm(x, axis=-1), edge_index, L1_gnn_W1, L1_gnn_b1, L1_gnn_W2, L1_gnn_b2)
    x = x + _L1_ffn_ref(_layernorm(x, axis=-1)[None], L1_ffn_Wq, L1_ffn_Wgate, L1_ffn_Wk, L1_ffn_Wv, L1_ffn_Wb, L1_ffn_Wa, L1_ffn_A_log, L1_ffn_dt_bias, L1_ffn_Wg, L1_ffn_o_norm_weight, L1_ffn_Wo)[0]
    return x

_drawn_inputs = setup_inputs


def setup_inputs(seed=0):
    import zlib

    import numpy as np

    out = dict(_drawn_inputs(seed))
    spreads = {'L0_ffn_gate_b': (0.0, 0.677),
     'L0_ffn_sb1': (0.0, 0.685),
     'L0_ffn_sb2': (0.0, 0.1),
     'L0_ffn_rb1': (0.0, 0.8),
     'L0_ffn_rb2': (0.0, 0.316),
     'L1_gnn_b1': (0.0, 0.1),
     'L1_gnn_b2': (0.0, 0.1),
     'L1_ffn_o_norm_weight': (1.0, 0.6)}
    factors = {'L0_ffn_rw1': 5.825,
     'L0_ffn_rw2': 5.445,
     'L1_ffn_Wb': 6.039,
     'L1_ffn_Wa': 8.0,
     'L1_ffn_A_log': 4.281,
     'L1_ffn_dt_bias': 3.285}
    for name, (base, spread) in spreads.items():
        noise = np.random.default_rng([zlib.crc32(name.encode()), seed]).standard_normal(out[name].shape)
        drawn = base * np.exp(spread * noise) if base else spread * noise
        out[name] = jnp.asarray(drawn.astype(out[name].dtype))
    for name, factor in factors.items():
        out[name] = (out[name] * factor).astype(out[name].dtype)
    return out
```

```python
from contextlib import ExitStack
import concourse.bass as bass
from concourse import mybir

F32 = mybir.dt.float32
I32 = mybir.dt.int32
ALU = mybir.AluOpType
ACT = mybir.ActivationFunctionType
AX = mybir.AxisListType

N = 10000
D = 512
KC = D // 128
R = 125
T = N // R
G = 4
GR = G * R
NG = N // GR
ER = 8
HF = 640
HC = HF // 128
E4 = 4
H = 8
DK = 64
CH = 128
NCH = 2 * N // CH + E4
NP = NCH * CH
ROW = 3 * D + 2 * H
RSQRT_SEED = 0x5F3759DF


class Consts:
    pass


class Pools:

    def __init__(self, nc, ctx, tag):
        self.nc, self.ctx, self.tag = nc, ctx, tag
        self.held = []
        ctx.callback(self.release)

    def release(self):
        self.nc.clear_and_free_semaphores(self.held)
        self.nc.all_engine_barrier()

    def sb(self, name, shape, dt=F32):
        return self.ctx.enter_context(self.nc.sbuf_tensor(f"{self.tag}_{name}", shape, dt))

    def ps(self, name, shape, dt=F32):
        return self.ctx.enter_context(self.nc.psum_tensor(f"{self.tag}_{name}", shape, dt))

    def sem(self, name):
        self.held.append(self.nc.alloc_semaphore(name=f"{self.tag}_{name}"))
        return self.held[-1]

    def sems(self, name, n=2):
        return [self.sem(f"{name}{i}") for i in range(n)]


def hold(pool, K, sem, value):
    pool.wait_ge(sem, value)
    pool.nop().then_inc(K.passed, 1)


def rsqrt(dve, y, v, tmp):
    dve.tensor_scalar(y.bitcast(I32), v.bitcast(I32), 1, None, ALU.arith_shift_right)
    dve.drain()
    dve.tensor_scalar(y.bitcast(I32), y.bitcast(I32), -1.0, float(RSQRT_SEED), ALU.mult, ALU.add)
    dve.drain()
    for _ in range(3):
        dve.tensor_tensor(tmp, y, y, ALU.mult)
        dve.drain()
        dve.scalar_tensor_tensor(tmp, tmp, -0.5, v, ALU.mult, ALU.mult)
        dve.drain()
        dve.scalar_tensor_tensor(y, tmp, 1.5, y, ALU.add, ALU.mult)
        dve.drain()


def moments(dve, rows, n, stats, mv):
    for g in range(n):
        dve.bn_stats(stats[0:R, g, :], rows[0:R, g, 0:D])
    dve.drain()
    for g in range(n):
        dve.bn_aggr(mv[0:R, g, :], stats[0:R, g, :])
    dve.drain()


def layernorm(dve, out, rows, n, stats, mv, rstd, var, tmp):
    moments(dve, rows, n, stats, mv)
    dve.tensor_scalar(var[0:R, 0:n], mv[0:R, 0:n, 1], 1e-5, None, ALU.add)
    dve.drain()
    rsqrt(dve, rstd[0:R, 0:n], var[0:R, 0:n], tmp[0:R, 0:n])
    for g in range(n):
        dve.tensor_scalar(out[0:R, g, 0:D], rows[0:R, g, 0:D], mv[0:R, g, 0:1], rstd[0:R, g:g + 1],
                          ALU.subtract, ALU.mult)


def constants(nc, K):
    K.ident = K.pool.sb("ident", [128, 128])
    K.later = K.pool.sb("later", [128, 128])
    K.upto = K.pool.sb("upto", [128, 128])
    K.before = K.pool.sb("before", [128, 128])
    K.ones = K.pool.sb("ones", [128, 128])
    K.zero = K.pool.sb("zero", [128, ROW])
    K.dump = K.pool.sb("dump", [128, 1])
    K.dumpi = K.pool.sb("dumpi", [128, 1], I32)
    filled, K.passed = K.pool.sem("filled"), K.pool.sem("passed")
    with nc.Block() as block:
        @block.gpsimd
        def _(pool):
            pool.memset(K.ident[:], 0.0)
            pool.memset(K.ones[:], 1.0)
            pool.memset(K.zero[:], 0.0)
            pool.iota(K.dumpi[:], pattern=[[0, 1]], base=N, channel_multiplier=1).then_inc(filled, 1)
            pool.wait_ge(filled, 1)
            pool.affine_select(out=K.ident[:], in_=K.ident[:], compare_op=ALU.not_equal, fill=1.0, base=0,
                               pattern=[[-1, 128]], channel_multiplier=1)
            pool.affine_select(out=K.later[:], in_=K.ones[:], compare_op=ALU.is_gt, fill=0.0, base=0,
                               pattern=[[-1, 128]], channel_multiplier=1)
            pool.affine_select(out=K.upto[:], in_=K.ones[:], compare_op=ALU.is_ge, fill=0.0, base=0,
                               pattern=[[1, 128]], channel_multiplier=-1)
            pool.affine_select(out=K.before[:], in_=K.ones[:], compare_op=ALU.is_gt, fill=0.0, base=0,
                               pattern=[[1, 128]], channel_multiplier=-1)
            pool.tensor_copy(K.dump[:], K.dumpi[:]).then_inc(filled, 1)
            pool.wait_ge(filled, 2)


def aggregate(nc, K, tag, src, dst, rows, table, first):
    W = D + 1 if first else D
    with ExitStack() as ctx:
        P = Pools(nc, ctx, tag)
        srcix = [P.sb(f"srcix{u}", [R, 1], I32) for u in range(2)]
        dstcol = [P.sb(f"dstcol{u}", [R, 1], I32) for u in range(2)]
        dstrow = [P.sb(f"dstrow{u}", [R, R], I32) for u in range(2)]
        rowf = [P.sb(f"rowf{u}", [R, R]) for u in range(2)]
        eq = [P.sb(f"eq{u}", [R, R]) for u in range(2)]
        colf = [P.sb(f"colf{u}", [R, 1]) for u in range(2)]
        scr = P.sb("scr", [R, R])
        earlier = P.sb("earlier", [R, 1])
        move = P.sb("move", [R, 1])
        degree = [P.sb(f"degree{u}", [R, 1]) for u in range(2)]
        sidx = [P.sb(f"sidx{u}", [R, 1], I32) for u in range(2)]
        gath = [P.sb(f"gath{u}", [R, 1, D]) for u in range(2)]
        comb = [P.sb(f"comb{u}", [R, W]) for u in range(2)]
        stats, mv = P.sb("stats", [R, 1, 6]), P.sb("mv", [R, 1, 2])
        rstd, var, tmp = P.sb("rstd", [R, 1]), P.sb("var", [R, 1]), P.sb("tmp", [R, 1])
        total = [P.ps(f"total{u}", [R, 512]) for u in range(2)]
        zeroed = P.sem("zeroed")
        src_in, dst_in, row_in = P.sems("src_in"), P.sems("dst_in"), P.sems("row_in")
        tile_done = P.sem("tile_done")
        gathered, added = P.sems("gathered"), P.sems("added")
        landed = P.sem("landed")
        gath_ready, summed, comb_ready = P.sem("gath_ready"), P.sem("summed"), P.sem("comb_ready")

        with nc.Block() as block:
            @block.sync
            def _(sp):
                sp.dma_start(table[0:N, :].rearrange("(p t) w -> p t w", p=R),
                             K.zero[0:R, 0:W].unsqueeze(1).to_broadcast([R, T, W])).then_inc(zeroed, 16)
                sp.wait_ge(zeroed, 16)
                sp.dma_start(table[N:N + R, :], K.zero[0:R, 0:W]).then_inc(zeroed, 16)
                with sp.Fori(0, T // 2) as i:
                    for u in range(2):
                        sp.wait_ge(tile_done, i * 2 + u + 1)
                        t = i * 2 + u
                        sp.dma_start(srcix[u][:], src[bass.ds(t, 1), :].rearrange("a r -> r a")).then_inc(src_in[u], 16)
                        sp.dma_start(dstcol[u][:], dst[bass.ds(t, 1), :].rearrange("a r -> r a")).then_inc(dst_in[u], 16)
                        sp.dma_start(dstrow[u][:], dst[bass.ds(t, 1), :].to_broadcast([R, R])).then_inc(row_in[u], 16)

            @block.gpsimd
            def _(pool):
                def gather(i, u):
                    hold(pool, K, src_in[u], (i + 1) * 16)
                    hold(pool, K, summed, i * 2 + u + 1)
                    pool.indirect_dma_start(gath[u][:, 0, :], None, rows,
                                            bass.IndirectOffsetOnAxis(ap=srcix[u][:, 0:1], axis=0),
                                            bounds_check=N - 1, oob_is_err=True).then_inc(gathered[u], 16)

                def add(i, u):
                    hold(pool, K, comb_ready, i * 2 + u + 1)
                    pool.indirect_dma_start(table, bass.IndirectOffsetOnAxis(ap=sidx[u][:, 0:1], axis=0),
                                            comb[u][:], None, bounds_check=N + R - 1, oob_is_err=True,
                                            compute_op=ALU.add).then_inc(added[u], 16)

                def land(i, u):
                    hold(pool, K, added[u], (i + 1) * 16)
                    pool.nop().then_inc(landed, 1)

                pool.wait_ge(zeroed, 32)
                gather(0, 0)
                gather(0, 1)
                add(0, 0)
                with pool.Fori(0, T // 2 - 1) as i:
                    gather(i + 1, 0)
                    land(i, 0)
                    add(i, 1)
                    gather(i + 1, 1)
                    land(i, 1)
                    add(i + 1, 0)
                land(T // 2 - 1, 0)
                add(T // 2 - 1, 1)
                land(T // 2 - 1, 1)

            @block.vector
            def _(dve):
                dve.drain().then_inc(tile_done, 2)
                dve.drain().then_inc(landed, 2)
                dve.drain().then_inc(summed, 2)
                with dve.Fori(0, T // 2) as i:
                    for u in range(2):
                        dve.wait_ge(dst_in[u], (i + 1) * 16)
                        dve.wait_ge(row_in[u], (i + 1) * 16)
                        dve.wait_ge(summed, i * 2 + u + 1)
                        dve.wait_ge(landed, i * 2 + u + 1)
                        dve.tensor_copy(rowf[u][:], dstrow[u][:])
                        dve.tensor_copy(colf[u][:], dstcol[u][:])
                        dve.drain()
                        dve.tensor_scalar(eq[u][:], rowf[u][:], colf[u][:, 0:1], None, ALU.is_equal)
                        dve.drain()
                        dve.tensor_tensor(scr[:], eq[u][:], K.later[0:R, 0:R], ALU.mult)
                        dve.tensor_reduce(degree[u][:], eq[u][:], AX.X, ALU.add)
                        dve.drain()
                        dve.tensor_reduce(earlier[:], scr[:], AX.X, ALU.add)
                        dve.tensor_tensor(move[:], K.dump[0:R, :], colf[u][:], ALU.subtract)
                        dve.drain()
                        dve.tensor_scalar(earlier[:], earlier[:], 1.0, None, ALU.min)
                        dve.drain()
                        dve.tensor_tensor(move[:], move[:], earlier[:], ALU.mult)
                        dve.drain()
                        dve.tensor_tensor(sidx[u][:], move[:], colf[u][:], ALU.add)
                        dve.drain()
                        dve.wait_ge(gathered[u], (i + 1) * 16)
                        if first:
                            layernorm(dve, gath[u], gath[u], 1, stats, mv, rstd, var, tmp)
                            dve.drain()
                        dve.nop().then_inc(gath_ready, 1)
                        dve.drain().then_inc(tile_done, 1)

            @block.tensor
            def _(pe):
                with pe.Fori(0, T // 2) as i:
                    for u in range(2):
                        pe.wait_ge(gath_ready, i * 2 + u + 1)
                        pe.matmul(total[u][:, :], eq[u][:], gath[u][:, 0, :], start=True, stop=True)\
                            .then_inc(summed, 1)

            @block.scalar
            def _(act):
                with act.Fori(0, T // 2) as i:
                    for u in range(2):
                        act.wait_ge(summed, i * 2 + u + 3)
                        act.wait_ge(landed, i * 2 + u + 1)
                        if first:
                            act.activation(comb[u][:, D:W], degree[u][:], ACT.Copy)
                        act.activation(comb[u][:, 0:D], total[u][:, :], ACT.Copy).then_inc(comb_ready, 1)


def first_layer(nc, K, x, table, w, x2, h2, rows):
    GPB = 2
    with ExitStack() as ctx:
        P = Pools(nc, ctx, "b")
        w1, w2 = P.sb("w1", [128, KC, D]), P.sb("w2", [128, KC, D])
        wup, wgate = P.sb("wup", [128, KC, HF]), P.sb("wgate", [128, KC, ER])
        wdown = P.sb("wdown", [128, HC, D])
        bup, bdown = P.sb("bup", [128, HC]), P.sb("bdown", [ER + 2, D])
        spread = P.sb("spread", [ER + 2, ER // 2, 128])
        bias1, bias2, gbias = P.sb("bias1", [R, D]), P.sb("bias2", [R, D]), P.sb("gbias", [R, G, ER])
        desc = P.sb("desc", [R, G, ER])
        desci = P.sb("desci", [R, G, ER], I32)
        xin = [P.sb(f"xin{u}", [R, G, D]) for u in range(GPB)]
        agg = [P.sb(f"agg{u}", [R, G, D + 1]) for u in range(GPB)]
        xn = P.sb("xn", [R, G, D])
        featA = P.sb("featA", [128, KC, GR])
        featB = P.sb("featB", [128, KC, GR])
        hid = P.sb("hid", [128, HC, GR])
        stats, mv = P.sb("stats", [R, G, 6]), P.sb("mv", [R, G, 2])
        rstd, var, tmp = P.sb("rstd", [R, G]), P.sb("var", [R, G]), P.sb("tmp", [R, G])
        recip = P.sb("recip", [R, G])
        lg, pr, ta, tb = (P.sb(n, [R, G, ER]) for n in ("lg", "pr", "ta", "tb"))
        cw = P.sb("cw", [R, G, ER + 2])
        cwT = P.sb("cwT", [ER + 2, GR])
        red = P.sb("red", [R, G])
        turned = [P.ps(f"turned{u}", [128, 512]) for u in range(2)]
        acc = [P.ps(f"acc{u}", [128, 512]) for u in range(2)]
        up = [P.ps(f"up{u}", [128, 512]) for u in range(2)]
        small = P.ps("small", [128, 512])
        wide = P.ps("wide", [128, 512])
        wld, wready, counted, xn_free = P.sem("wld"), P.sem("wready"), P.sem("counted"), P.sem("xn_free")
        x_in, a_in = P.sems("x_in"), P.sems("a_in")
        xn_ready, an_ready = P.sem("xn_ready"), P.sem("an_ready")
        tfull, tfree = P.sem("tfull"), P.sem("tfree")
        afull, afree = P.sem("afull"), P.sem("afree")
        hfull, hfree = P.sem("hfull"), P.sem("hfree")
        x1n_ready = P.sem("x1n_ready")
        gates_full, cw_ready, cwT_full, cwT_ready = P.sem("gates_full"), P.sem("cw_ready"), P.sem("cwT_full"), P.sem("cwT_ready")
        exp_in, exp_out = P.sem("exp_in"), P.sem("exp_out")
        wfull, wfree = P.sem("wfull"), P.sem("wfree")
        hid_ready = P.sem("hid_ready")
        x2_ready, h2_ready = P.sem("x2_ready"), P.sem("h2_ready")
        z_out, z_rest = P.sems("z_out"), P.sem("z_rest")
        x2_out, h2_out = P.sems("x2_out"), P.sems("h2_out")
        xrows = x.rearrange("(n r) d -> r n d", r=R)
        trows = table[0:N, :].rearrange("(n r) d -> r n d", r=R)
        x2rows = x2.rearrange("(n r) d -> r n d", r=R)
        h2rows = h2.rearrange("(n r) d -> r n d", r=R)

        with nc.Block() as block:
            @block.sync
            def _(sp):
                loads = [(w1, w["g1"].rearrange("(k p) n -> p k n", p=128)), (w2, w["g2"].rearrange("(k p) n -> p k n", p=128)),
                         (wup, w["up"].rearrange("(k p) n -> p k n", p=128)), (wgate, w["gate"].rearrange("(k p) n -> p k n", p=128)),
                         (wdown, w["down"].rearrange("(k p) n -> p k n", p=128)), (bup, w["bup"]), (bdown, w["bdown"]),
                         (bias1, w["gb1"].to_broadcast([R, D])), (bias2, w["gb2"].to_broadcast([R, D]))]
                for t, a in loads:
                    sp.dma_start(t[:], a).then_inc(wld, 16)
                for g in range(G):
                    sp.dma_start(gbias[:, g, :], w["gateb"].to_broadcast([R, ER])).then_inc(wld, 16)
                sp.wait_ge(wld, 16 * (len(loads) + G))
                sp.nop().then_inc(wready, 1)

                def load(i, u):
                    t = (i * GPB + u) * G
                    sp.dma_start(xin[u][:], xrows[:, bass.ds(t, G), :]).then_inc(x_in[u], 16)
                    sp.dma_start(agg[u][:], trows[:, bass.ds(t, G), :]).then_inc(a_in[u], 16)

                def leave(i, u, more):
                    t = (i * GPB + u) * G
                    sp.wait_ge(x2_ready, i * GPB + u + 1)
                    sp.dma_start(x2rows[:, bass.ds(t, G), :], xin[u][:]).then_inc(x2_out[u], 16)
                    sp.wait_ge(h2_ready, i * GPB + u + 1)
                    sp.dma_start(h2rows[:, bass.ds(t, G), :], xn[:]).then_inc(h2_out[u], 16)
                    sp.wait_ge(x2_out[u], (i + 1) * 16)
                    if more:
                        load(i + 1, u)
                    sp.wait_ge(h2_out[u], (i + 1) * 16)
                    sp.nop().then_inc(xn_free, 1)

                for u in range(GPB):
                    load(0, u)
                with sp.Fori(0, NG // GPB - 1) as i:
                    for u in range(GPB):
                        leave(i, u, True)
                for u in range(GPB):
                    leave(NG // GPB - 1, u, False)

            @block.gpsimd
            def _(pool):
                pool.memset(cw[:], 1.0)
                pool.memset(spread[:], 1.0)
                pool.iota(desci[:], pattern=[[0, G], [-1, ER]], base=ER, channel_multiplier=0).then_inc(counted, 1)
                pool.wait_ge(counted, 1)
                pool.tensor_copy(desc[:], desci[:])
                pool.affine_select(out=spread[:], in_=spread[:], compare_op=ALU.is_ge, fill=0.0, base=0,
                                   pattern=[[128, ER // 2], [1, 128]], channel_multiplier=-64)
                pool.drain()
                pool.affine_select(out=spread[:], in_=spread[:], compare_op=ALU.is_ge, fill=0.0, base=63,
                                   pattern=[[-128, ER // 2], [-1, 128]], channel_multiplier=64)
                pool.drain()
                pool.wait_ge(wready, 1)
                pool.tensor_tensor(bias1[:], bias1[:], bias2[:], ALU.add).then_inc(wready, 1)

            @block.tensor
            def _(pe):
                pe.wait_ge(wready, 2)

                def turn(ti, j, srcs):
                    for k in range(KC):
                        n = j * KC + k
                        pe.wait_ge(tfree, ti + n + 1)
                        for g in range(G):
                            m = pe.transpose(turned[n % 2][:, g * R:(g + 1) * R], srcs[:, g, k * 128:(k + 1) * 128], K.ident[0:R, 0:R])
                        m.then_inc(tfull, 1)

                with pe.Fori(0, NG // GPB) as i:
                    for u in range(GPB):
                        ig = i * GPB + u
                        pe.wait_ge(xn_ready, ig + 1)
                        turn(ig * 3 * KC, 0, xn)
                        pe.wait_ge(an_ready, ig + 1)
                        turn(ig * 3 * KC, 1, agg[u])
                        pe.wait_ge(tfree, ig * 3 * KC + 2 * KC + 2)
                        for g in range(G):
                            pe.wait_ge(afree, ig * 2 * G + g + 1)
                            for k in range(KC):
                                pe.matmul(acc[g % 2][0:R, :], featA[:, k, g * R:(g + 1) * R], w1[:, k, :], start=(k == 0), stop=False)
                            for k in range(KC):
                                m = pe.matmul(acc[g % 2][0:R, :], featB[:, k, g * R:(g + 1) * R], w2[:, k, :], start=False, stop=(k == KC - 1))
                            m.then_inc(afull, 1)
                        pe.wait_ge(x1n_ready, ig + 1)
                        turn(ig * 3 * KC, 2, xn)
                        pe.wait_ge(tfree, ig * 3 * KC + 3 * KC + 2)
                        for g in range(G):
                            for k in range(KC):
                                m = pe.matmul(small[0:R, g * ER:(g + 1) * ER], featA[:, k, g * R:(g + 1) * R], wgate[:, k, :], start=(k == 0), stop=(k == KC - 1))
                        m.then_inc(gates_full, 1)
                        for c in range(HC):
                            pe.wait_ge(hfree, ig * HC + c + 1)
                            for k in range(KC):
                                m = pe.matmul(up[c % 2][:, 0:GR], wup[:, k, c * 128:(c + 1) * 128], featA[:, k, :], start=(k == 0), stop=(k == KC - 1))
                            m.then_inc(hfull, 1)
                        pe.wait_ge(cw_ready, ig + 1)
                        for g in range(G):
                            m = pe.transpose(wide[0:ER + 2, g * R:(g + 1) * R], cw[:, g, :], K.ident[0:R, 0:R])
                        m.then_inc(cwT_full, 1)
                        pe.wait_ge(cwT_ready, ig + 1)
                        for c in range(ER // 2):
                            pe.wait_ge(wfree, ig * (ER // 2) + c + 1)
                            pe.matmul(wide[:, 0:GR], spread[:, c, :], cwT[:], start=True, stop=True).then_inc(wfull, 1)
                        pe.wait_ge(hid_ready, ig + 1)
                        for g in range(G):
                            pe.wait_ge(afree, ig * 2 * G + G + g + 1)
                            for c in range(HC):
                                pe.matmul(acc[g % 2][0:R, :], hid[:, c, g * R:(g + 1) * R], wdown[:, c, :], start=(c == 0), stop=False)
                            pe.matmul(acc[g % 2][0:R, :], cwT[:, g * R:(g + 1) * R], bdown[:], start=False, stop=True).then_inc(afull, 1)

            @block.scalar
            def _(act):
                act.wait_ge(wready, 2)

                def evict(base, j, dst):
                    for k in range(KC):
                        n = j * KC + k
                        act.wait_ge(tfull, base + n + 1)
                        act.activation(dst[:, k, :], turned[n % 2][:, 0:GR], ACT.Copy).then_inc(tfree, 1)

                PR = (NP + 128) // 128
                zrows = rows.rearrange("(p t) w -> p t w", p=128)
                part = (PR - 1) // NG
                act.dma_start(zrows[:, PR - 1, :], K.zero[:]).then_inc(z_rest, 16)
                with act.Fori(0, NG // GPB) as i:
                    for u in range(GPB):
                        ig = i * GPB + u
                        act.dma_start(zrows[:, bass.ds(ig * part, part), :], K.zero[:].unsqueeze(1).to_broadcast([128, part, ROW])).then_inc(z_out[u], 16)
                        evict(ig * 3 * KC, 0, featA)
                        evict(ig * 3 * KC, 1, featB)
                        evict(ig * 3 * KC, 2, featA)
                        for c in range(HC):
                            act.wait_ge(hfull, ig * HC + c + 1)
                            act.activation(hid[:, c, :], up[c % 2][:, 0:GR], ACT.Gelu, bias=bup[:, c:c + 1]).then_inc(hfree, 1)
                        act.wait_ge(exp_in, ig + 1)
                        act.activation(pr[:], lg[:], ACT.Exp).then_inc(exp_out, 1)
                act.wait_ge(z_rest, 16)
                for u in range(GPB):
                    act.wait_ge(z_out[u], 16 * (NG // GPB))

            @block.vector
            def _(dve):
                dve.wait_ge(wready, 2)
                for s, n in ((xn_free, 1), (tfree, 2), (afree, 2), (hfree, 2), (wfree, 1)):
                    dve.drain().then_inc(s, n)

                def topk_onehot(dst, p, m):
                    dve.tensor_reduce(red[:], p, AX.X, ALU.max)
                    dve.drain()
                    dve.tensor_tensor(dst, p, red[:].unsqueeze(2).to_broadcast([R, G, ER]), ALU.is_equal)
                    dve.drain()
                    dve.tensor_tensor(dst, dst, desc[:], ALU.mult)
                    dve.drain()
                    dve.tensor_reduce(red[:], dst, AX.X, ALU.max)
                    dve.drain()
                    dve.tensor_tensor(dst, desc[:], red[:].unsqueeze(2).to_broadcast([R, G, ER]), ALU.is_equal)
                    dve.drain()

                with dve.Fori(0, NG // GPB) as i:
                    for u in range(GPB):
                        ig = i * GPB + u
                        dve.wait_ge(x_in[u], (i + 1) * 16)
                        dve.wait_ge(a_in[u], (i + 1) * 16)
                        dve.wait_ge(xn_free, ig + 1)
                        layernorm(dve, xn, xin[u], G, stats, mv, rstd, var, tmp)
                        dve.tensor_scalar(recip[:], agg[u][:, :, D], 1.0, None, ALU.max)
                        dve.drain().then_inc(xn_ready, 1)
                        dve.reciprocal(recip[:], recip[:])
                        dve.drain()
                        for g in range(G):
                            dve.tensor_scalar(agg[u][:, g, 0:D], agg[u][:, g, 0:D], recip[:, g:g + 1], None, ALU.mult)
                        dve.drain().then_inc(an_ready, 1)
                        for g in range(G):
                            dve.tensor_tensor(xin[u][:, g, :], xin[u][:, g, :], bias1[:], ALU.add)
                        dve.drain()
                        for g in range(G):
                            dve.wait_ge(afull, ig * 2 * G + g + 1)
                            dve.tensor_tensor(xin[u][:, g, :], acc[g % 2][0:R, :], xin[u][:, g, :], ALU.add).then_inc(afree, 1)
                        dve.drain()
                        layernorm(dve, xn, xin[u], G, stats, mv, rstd, var, tmp)
                        dve.drain().then_inc(x1n_ready, 1)
                        dve.wait_ge(gates_full, ig + 1)
                        dve.tensor_tensor(lg[:], small[0:R, 0:G * ER].rearrange("p (g e) -> p g e", g=G), gbias[:], ALU.add)
                        dve.drain()
                        dve.tensor_reduce(red[:], lg[:], AX.X, ALU.max)
                        dve.drain()
                        dve.tensor_tensor(lg[:], lg[:], red[:].unsqueeze(2).to_broadcast([R, G, ER]), ALU.subtract)
                        dve.drain().then_inc(exp_in, 1)
                        dve.wait_ge(exp_out, ig + 1)
                        dve.tensor_reduce(red[:], pr[:], AX.X, ALU.add)
                        dve.drain()
                        dve.reciprocal(red[:], red[:])
                        dve.drain()
                        dve.tensor_tensor(pr[:], pr[:], red[:].unsqueeze(2).to_broadcast([R, G, ER]), ALU.mult)
                        dve.drain()
                        topk_onehot(ta[:], pr[:], red)
                        dve.scalar_tensor_tensor(lg[:], ta[:], -2.0, pr[:], ALU.mult, ALU.add)
                        dve.drain()
                        topk_onehot(tb[:], lg[:], red)
                        dve.tensor_tensor(ta[:], ta[:], tb[:], ALU.add)
                        dve.drain()
                        dve.tensor_tensor(cw[:, :, 0:ER], ta[:], pr[:], ALU.mult)
                        dve.drain().then_inc(cw_ready, 1)
                        dve.wait_ge(cwT_full, ig + 1)
                        dve.tensor_copy(cwT[:], wide[0:ER + 2, 0:GR])
                        dve.drain().then_inc(cwT_ready, 1)
                        dve.wait_ge(hfree, ig * HC + HC + 2)
                        for c in range(ER // 2):
                            dve.wait_ge(wfull, ig * (ER // 2) + c + 1)
                            hc = HC - ER // 2 + c
                            dve.tensor_tensor(hid[:, hc, :], wide[:, 0:GR], hid[:, hc, :], ALU.mult).then_inc(wfree, 1)
                        dve.drain().then_inc(hid_ready, 1)
                        for g in range(G):
                            dve.wait_ge(afull, ig * 2 * G + G + g + 1)
                            dve.tensor_tensor(xin[u][:, g, :], acc[g % 2][0:R, :], xin[u][:, g, :], ALU.add).then_inc(afree, 1)
                        dve.drain().then_inc(x2_ready, 1)
                        layernorm(dve, xn, xin[u], G, stats, mv, rstd, var, tmp)
                        dve.drain().then_inc(h2_ready, 1)


NL = E4 + 2 * H


def second_gnn(nc, K, h2, table, x2, w, x3, h3T, logits):
    GPB = 2
    with ExitStack() as ctx:
        P = Pools(nc, ctx, "d")
        w1, w2 = P.sb("w1", [128, KC, D]), P.sb("w2", [128, KC, D])
        wl = P.sb("wl", [128, KC, NL])
        b1, b2 = P.sb("b1", [128, KC]), P.sb("b2", [R, D])
        hin = [P.sb(f"hin{u}", [R, G, D]) for u in range(GPB)]
        xin = [P.sb(f"xin{u}", [R, G, D]) for u in range(GPB)]
        agg = P.sb("agg", [R, G, D])
        featA, hid = P.sb("featA", [128, KC, GR]), P.sb("hid", [128, KC, GR])
        featB = [P.sb(f"featB{u}", [128, KC, GR]) for u in range(GPB)]
        stats, mv = P.sb("stats", [R, G, 6]), P.sb("mv", [R, G, 2])
        rstd, var, tmp = P.sb("rstd", [R, G]), P.sb("var", [R, G]), P.sb("tmp", [R, G])
        turned = [P.ps(f"turned{u}", [128, 512]) for u in range(2)]
        acc = [P.ps(f"acc{u}", [128, 512]) for u in range(2)]
        up = [P.ps(f"up{u}", [128, 512]) for u in range(2)]
        small = P.ps("small", [128, 512])
        wld, wready = P.sem("wld"), P.sem("wready")
        h_in, x_in, a_in = P.sems("h_in"), P.sems("x_in"), P.sem("a_in")
        agg_free, fb_free = P.sem("agg_free"), P.sem("fb_free")
        s_ready, h3_ready = P.sem("s_ready"), P.sem("h3_ready")
        tfull, tfree, afull, afree = P.sem("tfull"), P.sem("tfree"), P.sem("afull"), P.sem("afree")
        hfull, hfree = P.sem("hfull"), P.sem("hfree")
        lfull, lfree = P.sem("lfull"), P.sem("lfree")
        x3_ready = P.sem("x3_ready")
        x3_out, fb_out = P.sems("x3_out"), P.sems("fb_out")
        hrows, xrows, x3rows = (a.rearrange("(n r) d -> r n d", r=R) for a in (h2, x2, x3))
        trows = table[0:N, :].rearrange("(n r) d -> r n d", r=R)
        NB = NG // GPB

        with nc.Block() as block:
            @block.sync
            def _(sp):
                loads = [(w1, w["n1"].rearrange("(k p) n -> p k n", p=128)), (w2, w["n2"].rearrange("(k p) n -> p k n", p=128)),
                         (wl, w["wl"].rearrange("(k p) n -> p k n", p=128)), (b1, w["nb1"]), (b2, w["nb2"].to_broadcast([R, D]))]
                for t, a in loads:
                    sp.dma_start(t[:], a).then_inc(wld, 16)
                sp.wait_ge(wld, 16 * len(loads))
                sp.nop().then_inc(wready, 1)

                def load(i, u):
                    t = (i * GPB + u) * G
                    sp.dma_start(hin[u][:], hrows[:, bass.ds(t, G), :]).then_inc(h_in[u], 16)
                    sp.dma_start(xin[u][:], xrows[:, bass.ds(t, G), :]).then_inc(x_in[u], 16)

                def load_agg(i, u):
                    t = (i * GPB + u) * G
                    sp.wait_ge(agg_free, i * GPB + u + 1)
                    sp.dma_start(agg[:], trows[:, bass.ds(t, G), :]).then_inc(a_in, 16)

                def leave(i, u, more):
                    ig = i * GPB + u
                    if u == 0:
                        load_agg(i, 1)
                    elif more:
                        load_agg(i + 1, 0)
                    sp.wait_ge(x3_ready, ig + 1)
                    sp.dma_start(x3rows[:, bass.ds(ig * G, G), :], xin[u][:]).then_inc(x3_out[u], 16)
                    sp.wait_ge(tfree, ig * 2 * KC + 2 * KC + 2)
                    sp.dma_start(h3T[bass.ds(ig, 1), :, :].rearrange("a p n -> p (a n)"), featB[u][:].rearrange("p k n -> p (k n)")).then_inc(fb_out[u], 16)
                    sp.wait_ge(x3_out[u], (i + 1) * 16)
                    if more:
                        load(i + 1, u)
                    sp.wait_ge(fb_out[u], (i + 1) * 16)
                    sp.nop().then_inc(fb_free, 1)

                for u in range(GPB):
                    load(0, u)
                load_agg(0, 0)
                with sp.Fori(0, NB - 1) as i:
                    for u in range(GPB):
                        leave(i, u, True)
                for u in range(GPB):
                    leave(NB - 1, u, False)

            @block.tensor
            def _(pe):
                pe.wait_ge(wready, 1)

                def turn(ti, j, srcs):
                    for k in range(KC):
                        n = j * KC + k
                        pe.wait_ge(tfree, ti + n + 1)
                        for g in range(G):
                            m = pe.transpose(turned[n % 2][:, g * R:(g + 1) * R], srcs[:, g, k * 128:(k + 1) * 128], K.ident[0:R, 0:R])
                        m.then_inc(tfull, 1)

                with pe.Fori(0, NB) as i:
                    for u in range(GPB):
                        ig = i * GPB + u
                        pe.wait_ge(s_ready, ig + 1)
                        turn(ig * 2 * KC, 0, hin[u])
                        pe.wait_ge(tfree, ig * 2 * KC + KC + 2)
                        for c in range(KC):
                            pe.wait_ge(hfree, ig * KC + c + 1)
                            for k in range(KC):
                                m = pe.matmul(up[c % 2][:, 0:GR], w1[:, k, c * 128:(c + 1) * 128], featA[:, k, :], start=(k == 0), stop=(k == KC - 1))
                            m.then_inc(hfull, 1)
                        pe.wait_ge(hfree, ig * KC + KC + 2)
                        for g in range(G):
                            pe.wait_ge(afree, ig * G + g + 1)
                            for k in range(KC):
                                m = pe.matmul(acc[g % 2][0:R, :], hid[:, k, g * R:(g + 1) * R], w2[:, k, :], start=(k == 0), stop=(k == KC - 1))
                            m.then_inc(afull, 1)
                        pe.wait_ge(h3_ready, ig + 1)
                        turn(ig * 2 * KC, 1, hin[u])
                        pe.wait_ge(tfree, ig * 2 * KC + 2 * KC + 2)
                        pe.wait_ge(lfree, ig + 1)
                        for g in range(G):
                            for k in range(KC):
                                m = pe.matmul(small[0:R, g * NL:(g + 1) * NL], featB[u][:, k, g * R:(g + 1) * R], wl[:, k, :], start=(k == 0), stop=(k == KC - 1))
                        m.then_inc(lfull, 1)

            @block.scalar
            def _(act):
                act.wait_ge(wready, 1)

                def evict(base, j, dst):
                    for k in range(KC):
                        n = j * KC + k
                        act.wait_ge(tfull, base + n + 1)
                        act.activation(dst[:, k, :], turned[n % 2][:, 0:GR], ACT.Copy).then_inc(tfree, 1)

                with act.Fori(0, NB) as i:
                    for u in range(GPB):
                        ig = i * GPB + u
                        evict(ig * 2 * KC, 0, featA)
                        for c in range(KC):
                            act.wait_ge(hfull, ig * KC + c + 1)
                            act.activation(hid[:, c, :], up[c % 2][:, 0:GR], ACT.Relu, bias=b1[:, c:c + 1]).then_inc(hfree, 1)
                        act.wait_ge(fb_free, ig + 1)
                        evict(ig * 2 * KC, 1, featB[u])

            @block.vector
            def _(dve):
                dve.wait_ge(wready, 1)
                for s, n in ((tfree, 2), (afree, 2), (hfree, 2), (lfree, 1), (agg_free, 1), (fb_free, GPB)):
                    dve.drain().then_inc(s, n)
                with dve.Fori(0, NB) as i:
                    for u in range(GPB):
                        ig = i * GPB + u
                        dve.wait_ge(h_in[u], (i + 1) * 16)
                        dve.wait_ge(a_in, (ig + 1) * 16)
                        for g in range(G):
                            dve.tensor_tensor(hin[u][:, g, :], hin[u][:, g, :], agg[:, g, :], ALU.add)
                        dve.drain().then_inc(s_ready, 1)
                        dve.nop().then_inc(agg_free, 1)
                        dve.wait_ge(x_in[u], (i + 1) * 16)
                        for g in range(G):
                            dve.tensor_tensor(xin[u][:, g, :], xin[u][:, g, :], b2[:], ALU.add)
                        dve.drain()
                        for g in range(G):
                            dve.wait_ge(afull, ig * G + g + 1)
                            dve.tensor_tensor(xin[u][:, g, :], acc[g % 2][0:R, :], xin[u][:, g, :], ALU.add).then_inc(afree, 1)
                        dve.drain().then_inc(x3_ready, 1)
                        layernorm(dve, hin[u], xin[u], G, stats, mv, rstd, var, tmp)
                        dve.drain().then_inc(h3_ready, 1)
                        dve.wait_ge(lfull, ig + 1)
                        dve.tensor_copy(logits[:, bass.ds(ig * G, G), :], small[0:R, 0:G * NL].rearrange("p (g e) -> p g e", g=G)).then_inc(lfree, 1)


def route(nc, K, logits, w, weights, pos, beta, decay, keep):
    S = [R, T, E4]
    with ExitStack() as ctx:
        P = Pools(nc, ctx, "r")
        p, e1, e2, m, desc, allpos = (P.sb(n, S) for n in ("p", "e1", "e2", "m", "desc", "allpos"))
        desci = P.sb("desci", S, I32)
        red, w1, w2, any2, at1, at2 = (P.sb(n, [R, T]) for n in ("red", "w1", "w2", "any2", "at1", "at2"))
        tot, run = P.sb("tot", [128, E4, T]), P.sb("run", [128, E4, T])
        onesT = P.sb("onesT", [128, T])
        cnt, cnti, start = P.sb("cnt", [128, E4]), P.sb("cnti", [128, E4], I32), P.sb("start", [128, E4])
        SB = [R, T, H]
        y, z, z2, s, den = (P.sb(n, SB) for n in ("y", "z", "z2", "s", "den"))
        dtb, alog = P.sb("dtb", [R, H]), P.sb("alog", [R, H])
        chunki, chunk, hit = P.sb("chunki", [128, NCH + 1], I32), P.sb("chunk", [128, NCH + 1]), P.sb("hit", [128, NCH + 1])
        dumpno = P.sb("dumpno", [128, 1])
        dumpi = P.sb("dumpi", [128, 1], I32)
        before, total = P.ps("before", [R, T * E4]), P.ps("total", [128, T * E4])
        made, ld, a_go, a_done, g_go, g_done, pre = (P.sem(n) for n in ("made", "ld", "a_go", "a_done", "g_go", "g_done", "pre"))
        bc = lambda a: a.unsqueeze(2).to_broadcast(S)
        bh = lambda a: a.unsqueeze(1).to_broadcast(SB)
        with nc.Block() as block:
            @block.sync
            def _(sp):
                sp.dma_start(dtb[:], w["dtb"].to_broadcast([R, H])).then_inc(ld, 16)
                sp.dma_start(alog[:], w["alog"].to_broadcast([R, H])).then_inc(ld, 16)

            @block.gpsimd
            def _(pool):
                pool.iota(desci[:], pattern=[[0, T], [-1, E4]], base=E4, channel_multiplier=0)
                pool.iota(chunki[:], pattern=[[CH, NCH + 1]], base=0, channel_multiplier=0)
                pool.iota(dumpi[:], pattern=[[0, 1]], base=NP, channel_multiplier=1)
                pool.drain()
                pool.tensor_copy(desc[:], desci[:])
                pool.tensor_copy(chunk[:], chunki[:])
                pool.tensor_copy(dumpno[:], dumpi[:]).then_inc(made, 1)

            @block.scalar
            def _(act):
                act.wait_ge(a_go, 1)
                act.activation(p[:], p[:], ACT.Exp).then_inc(a_done, 1)
                act.wait_ge(a_go, 2)
                act.activation(z[:], z[:], ACT.Exp)
                act.activation(alog[:], alog[:], ACT.Exp).then_inc(a_done, 1)
                act.wait_ge(a_go, 3)
                act.activation(beta[:], beta[:], ACT.Sigmoid).then_inc(a_done, 1)

            @block.tensor
            def _(pe):
                pe.wait_ge(g_go, 1)
                mm = m[:].rearrange("p t e -> p (t e)")
                pe.matmul(before[:], K.before[0:R, 0:R], mm, start=True, stop=True)
                pe.matmul(total[:], K.ones[0:R, 0:128], mm, start=True, stop=True).then_inc(g_done, 1)

            @block.vector
            def _(dve):
                d = dve.drain

                def first_largest(dst, src):
                    dve.tensor_reduce(red[:], src, AX.X, ALU.max); d()
                    dve.tensor_tensor(dst, src, bc(red[:]), ALU.is_equal); d()
                    dve.tensor_tensor(dst, dst, desc[:], ALU.mult); d()
                    dve.tensor_reduce(red[:], dst, AX.X, ALU.max); d()
                    dve.tensor_tensor(dst, desc[:], bc(red[:]), ALU.is_equal); d()

                def weigh(dst, onehot, vals):
                    dve.tensor_tensor(m[:], onehot, vals, ALU.mult); d()
                    dve.tensor_reduce(dst, m[:], AX.X, ALU.add); d()

                dve.wait_ge(made, 1)
                dve.wait_ge(ld, 32)
                dve.tensor_reduce(red[:], logits[:, :, 0:E4], AX.X, ALU.max); d()
                dve.tensor_tensor(p[:], logits[:, :, 0:E4], bc(red[:]), ALU.subtract)
                d().then_inc(a_go, 1)
                dve.tensor_tensor(y[:], logits[:, :, E4 + H:NL], bh(dtb[:]), ALU.add); d()
                dve.tensor_scalar(z[:], y[:], -1.0, None, ALU.mult); d()
                dve.tensor_tensor(z[:], z[:], y[:], ALU.min)
                d().then_inc(a_go, 1)
                dve.tensor_copy(beta[:], logits[:, :, E4:E4 + H])
                d().then_inc(a_go, 1)
                dve.wait_ge(a_done, 1)
                dve.tensor_reduce(red[:], p[:], AX.X, ALU.add); d()
                dve.reciprocal(red[:], red[:]); d()
                dve.tensor_tensor(p[:], p[:], bc(red[:]), ALU.mult); d()
                first_largest(e1[:], p[:])
                weigh(w1[:], e1[:], p[:])
                dve.scalar_tensor_tensor(allpos[:], e1[:], -2.0, p[:], ALU.mult, ALU.add); d()
                first_largest(e2[:], allpos[:])
                weigh(w2[:], e2[:], p[:])
                dve.tensor_tensor(red[:], w1[:], w2[:], ALU.add); d()
                dve.reciprocal(red[:], red[:]); d()
                dve.tensor_tensor(weights[:, 0, :], w1[:], red[:], ALU.mult)
                dve.tensor_tensor(weights[:, 1, :], w2[:], red[:], ALU.mult); d()
                dve.tensor_scalar(any2[:], weights[:, 1, :], 0.0, None, ALU.is_gt); d()
                dve.tensor_tensor(e2[:], e2[:], bc(any2[:]), ALU.mult); d()
                dve.tensor_tensor(m[:], e1[:], e2[:], ALU.add)
                d().then_inc(g_go, 1)
                dve.wait_ge(g_done, 1)
                dve.tensor_copy(tot[:], total[:].rearrange("p (t e) -> p e t", e=E4))
                dve.memset(onesT[:], 1.0); d()
                for e in range(E4):
                    dve.tensor_tensor_scan(run[:, e, :], onesT[:], tot[:, e, :], 0.0, ALU.mult, ALU.add)
                d()
                dve.tensor_copy(cnt[:], run[:, :, T - 1]); d()
                dve.tensor_tensor(run[:], run[:], tot[:], ALU.subtract)
                dve.tensor_scalar(cnti[:], cnt[:], float(CH - 1), None, ALU.add); d()
                dve.tensor_scalar(cnti[:], cnti[:], 7, 7, ALU.arith_shift_right, ALU.arith_shift_left); d()
                dve.tensor_copy(cnt[:], cnti[:])
                dve.memset(start[:], 0.0); d()
                for e in range(1, E4):
                    dve.tensor_tensor(start[:, e:e + 1], start[:, e - 1:e], cnt[:, e - 1:e], ALU.add); d()
                dve.tensor_tensor(allpos[:], before[:].rearrange("p (t e) -> p t e", e=E4), run[0:R].rearrange("p e t -> p t e"), ALU.add); d()
                dve.tensor_tensor(allpos[:], allpos[:], start[0:R, :].unsqueeze(1).to_broadcast(S), ALU.add); d()
                weigh(at1[:], e1[:], allpos[:])
                weigh(at2[:], e2[:], allpos[:])
                dve.tensor_copy(pos[:, 0, :], at1[:])
                dve.tensor_scalar(any2[:], any2[:], -1.0, 1.0, ALU.mult, ALU.add); d()
                dve.tensor_tensor(any2[:], any2[:], dumpno[0:R, 0:1].to_broadcast([R, T]), ALU.mult); d()
                dve.tensor_tensor(pos[:, 1, :], at2[:], any2[:], ALU.add)
                dve.wait_ge(a_done, 2)
                dve.tensor_scalar(den[:], z[:], 2.0, None, ALU.add); d()
                dve.reciprocal(den[:], den[:]); d()
                dve.tensor_tensor(s[:], z[:], den[:], ALU.mult); d()
                dve.tensor_tensor(z2[:], s[:], s[:], ALU.mult); d()
                dve.tensor_scalar(den[:], z2[:], 1.0 / 17, 1.0 / 15, ALU.mult, ALU.add); d()
                for n in (13, 11, 9, 7, 5, 3, 1):
                    dve.tensor_tensor(den[:], den[:], z2[:], ALU.mult); d()
                    dve.tensor_scalar(den[:], den[:], 1.0 / n, None, ALU.add); d()
                dve.tensor_tensor(den[:], den[:], s[:], ALU.mult); d()
                dve.tensor_scalar(y[:], y[:], 0.0, None, ALU.max); d()
                dve.scalar_tensor_tensor(den[:], den[:], 2.0, y[:], ALU.mult, ALU.add); d()
                dve.tensor_tensor(den[:], den[:], bh(alog[:]), ALU.mult); d()
                dve.tensor_scalar(decay[:], den[:], -1.0, -3.0e38, ALU.mult, ALU.max)
                dve.wait_ge(a_done, 3)
                dve.memset(keep[:], 1.0); d()
                for e in range(E4):
                    dve.tensor_scalar(hit[:], chunk[:], start[:, e:e + 1], None, ALU.not_equal); d()
                    dve.tensor_tensor(keep[:], keep[:], hit[:], ALU.mult); d()


def project(nc, K, h3T, w, pos, beta, decay, rows):
    QK = 2 * D
    NR = 4
    with ExitStack() as ctx:
        P = Pools(nc, ctx, "e")
        wt = P.sb("w", [128, 3, KC, D])
        feat = [P.sb(f"feat{u}", [128, KC, GR]) for u in range(2)]
        row = [P.sb(f"row{v}", [R, ROW]) for v in range(NR)]
        ix = [[P.sb(f"ix{v}{s}", [R, 1], I32) for s in range(2)] for v in range(NR)]
        sq = P.sb("sq", [R, QK])
        ss, inv, tmp = P.sb("ss", [R, 2 * H]), P.sb("inv", [R, 2 * H]), P.sb("tmp", [R, 2 * H])
        proj = [[P.ps(f"proj{v}{j}", [R, 512]) for j in range(3)] for v in range(2)]
        wld = P.sem("wld")
        f_in, f_used = P.sems("f_in"), P.sem("f_used")
        pfull, silu, row_ready, row_free = P.sem("pfull"), P.sem("silu"), P.sem("row_ready"), P.sem("row_free")
        sent = [[P.sem(f"sent{v}{s}") for s in range(2)] for v in range(NR)]
        NB = NG // 2
        with nc.Block() as block:
            @block.sync
            def _(sp):
                for j, n in enumerate(("wk", "wq", "wv")):
                    sp.dma_start(wt[:, j], w[n].rearrange("(k p) n -> p k n", p=128)).then_inc(wld, 16)

                def load(ig, u):
                    sp.dma_start(feat[u][:].rearrange("p k n -> p (k n)"), h3T[bass.ds(ig, 1), :, :].rearrange("a p n -> p (a n)")).then_inc(f_in[u], 16)
                load(0, 0)
                load(1, 1)
                with sp.Fori(0, NB - 1) as i:
                    for u in range(2):
                        sp.wait_ge(f_used, i * 2 + u + 1)
                        load(i * 2 + u + 2, u)

            @block.tensor
            def _(pe):
                pe.wait_ge(wld, 48)
                with pe.Fori(0, NB) as i:
                    for u in range(2):
                        pe.wait_ge(f_in[u], (i + 1) * 16)
                        for g in range(G):
                            t = (i * 2 + u) * G + g
                            pe.wait_ge(silu, t + 1)
                            for j in range(3):
                                for k in range(KC):
                                    m = pe.matmul(proj[g % 2][j][:], feat[u][:, k, g * R:(g + 1) * R], wt[:, j, k, :], start=(k == 0), stop=(k == KC - 1))
                            m.then_inc(pfull, 1)

            @block.scalar
            def _(act):
                with act.Fori(0, NB) as i:
                    for u in range(2):
                        for g in range(G):
                            t = (i * 2 + u) * G + g
                            act.wait_ge(row_free, t + 1)
                            act.wait_ge(pfull, t + 1)
                            for j in range(3):
                                m = act.activation(row[g][:, j * D:(j + 1) * D], proj[g % 2][j][:], ACT.Silu)
                            m.then_inc(silu, 1)
                        act.drain().then_inc(f_used, 1)

            @block.gpsimd
            def _(pool):
                def send(i, v, g):
                    for s in range(2):
                        hold(pool, K, row_ready, i + 1)
                        pool.indirect_dma_start(rows, bass.IndirectOffsetOnAxis(ap=ix[v][s][:, 0:1], axis=0), row[v][:], None,
                                                bounds_check=NP + 127, oob_is_err=True).then_inc(sent[v][s], 16)

                def land(j, v):
                    for s in range(2):
                        hold(pool, K, sent[v][s], (j + 1) * 16)
                    pool.nop().then_inc(row_free, 1)

                for g in range(2):
                    send(g, g, g)
                with pool.Fori(0, T // G - 1) as i:
                    for g in range(G):
                        send(i * G + g + 2, (g + 2) % NR, g)
                        land(i, g)
                for g in range(2):
                    send(T - 2 + g, (g + 2) % NR, g)
                for g in range(G):
                    land(T // G - 1, g)

            @block.vector
            def _(dve):
                dve.drain().then_inc(row_free, NR)
                dve.drain().then_inc(silu, 2)
                with dve.Fori(0, T // G) as i:
                    for g in range(G):
                        t = i * G + g
                        dve.wait_ge(silu, t + 3)
                        rw = row[g]
                        dve.tensor_tensor(sq[:], rw[:, 0:QK], rw[:, 0:QK], ALU.mult)
                        dve.tensor_copy(rw[:, 3 * D:3 * D + H], beta[:, bass.ds(t, 1), :].rearrange("p a h -> p (a h)"))
                        dve.tensor_copy(rw[:, 3 * D + H:ROW], decay[:, bass.ds(t, 1), :].rearrange("p a h -> p (a h)"))
                        for s in range(2):
                            dve.tensor_copy(ix[g][s][:], pos[:, s, bass.ds(t, 1)])
                        dve.drain()
                        dve.tensor_reduce(ss[:], sq[:].rearrange("p (h d) -> p h d", d=DK), AX.X, ALU.add)
                        dve.drain()
                        dve.tensor_scalar(ss[:], ss[:], 1e-6, None, ALU.add)
                        dve.drain()
                        rsqrt(dve, inv[:], ss[:], tmp[:])
                        dve.tensor_scalar(inv[:, H:2 * H], inv[:, H:2 * H], float(DK) ** -0.5, None, ALU.mult)
                        dve.drain()
                        v = rw[:, 0:QK].rearrange("p (h d) -> p h d", d=DK)
                        dve.tensor_tensor(v, v, inv[:].unsqueeze(2).to_broadcast([R, 2 * H, DK]), ALU.mult)
                        dve.drain().then_inc(row_ready, 1)


def chunk_products(nc, K, rows, aq, diag):
    with ExitStack() as ctx:
        P = Pools(nc, ctx, "f")
        comp = [P.sb(f"comp{u}", [128, ROW]) for u in range(2)]
        kb = [P.sb(f"kb{u}", [128, D]) for u in range(2)]
        kT = P.sb("kT", [128, 4, 128])
        bq = P.sb("bq", [128, 4, 2, 128])
        gu = [P.sb(f"gu{u}", [128, H, 128]) for u in range(2)]
        dec = P.sb("dec", [128, H, 128])
        prod = [P.sb(f"prod{u}", [128, H, 2, 128]) for u in range(2)]
        blk = [P.sb(f"blk{u}", [128, H, 32]) for u in range(2)]
        turned = [P.ps(f"turned{u}", [128, 512]) for u in range(2)]
        dsum = [P.ps(f"dsum{u}", [128, 512]) for u in range(2)]
        kq = [P.ps(f"kq{u}", [128, 2, 2, 128]) for u in range(4)]
        c_in = P.sems("c_in")
        kb_ready, gu_ready = P.sem("kb_ready"), P.sem("gu_ready")
        tfull, tfree, dfull, dec_ready, dec_cut = (P.sem(n) for n in ("tfull", "tfree", "dfull", "dec_ready", "dec_cut"))
        kfull, kfree, p_ready, blk_ready = (P.sem(n) for n in ("kfull", "kfree", "p_ready", "blk_ready"))
        out_free, cut = P.sem("out_free"), P.sem("cut")
        p_out, b_out = P.sems("p_out"), P.sems("b_out")
        NB = NCH // 2
        with nc.Block() as block:
            @block.sync
            def _(sp):
                def load(c, u):
                    sp.dma_start(comp[u][:], rows[bass.ds(c * CH, CH), :]).then_inc(c_in[u], 16)

                def leave(i, u, more):
                    c = i * 2 + u
                    sp.wait_ge(cut, c + 1)
                    sp.dma_start(diag[bass.ds(c, 1), :, :].rearrange("a p n -> p (a n)"), blk[u][:].rearrange("p h i -> p (h i)")).then_inc(b_out[u], 16)
                    sp.dma_start(aq[bass.ds(c, 1), :, :].rearrange("a p n -> p (a n)"), prod[u][:].rearrange("p h s i -> p (h s i)")).then_inc(p_out[u], 16)
                    if more:
                        load(c + 2, u)
                    sp.wait_ge(b_out[u], (i + 1) * 16)
                    sp.wait_ge(p_out[u], (i + 1) * 16)
                    sp.nop().then_inc(out_free, 1)

                load(0, 0)
                load(1, 1)
                with sp.Fori(0, NB - 1) as i:
                    for u in range(2):
                        leave(i, u, True)
                for u in range(2):
                    leave(NB - 1, u, False)

            @block.gpsimd
            def _(pool):
                with pool.Fori(0, NB) as i:
                    for u in range(2):
                        c = i * 2 + u
                        hold(pool, K, c_in[u], (i + 1) * 16)
                        hold(pool, K, kfull, c * 4 + 4)
                        pool.tensor_tensor(kb[u][:].rearrange("p (h d) -> p h d", h=H), comp[u][:, 0:D].rearrange("p (h d) -> p h d", h=H),
                                           comp[u][:, 3 * D:3 * D + H].unsqueeze(2).to_broadcast([128, H, DK]), ALU.mult).then_inc(kb_ready, 1)
                        hold(pool, K, dec_ready, c + 2)
                        pool.affine_select(out=dec[:], in_=dec[:], compare_op=ALU.is_ge, fill=0.0, base=0,
                                           pattern=[[0, H], [1, 128]], channel_multiplier=-1).then_inc(dec_cut, 1)
                        pool.drain()
                        hold(pool, K, p_ready, c + 1)
                        for b in range(4):
                            s = slice(32 * b, 32 * b + 32)
                            pool.tensor_copy(blk[u][s], prod[u][s, :, 0, s])
                        pool.drain()
                        for b in range(4):
                            s = slice(32 * b, 32 * b + 32)
                            pool.memset(prod[u][s, :, 0, s], 0.0)
                        pool.drain().then_inc(cut, 1)

            @block.tensor
            def _(pe):
                with pe.Fori(0, NB) as i:
                    for u in range(2):
                        c = i * 2 + u
                        pe.wait_ge(c_in[u], (i + 1) * 16)

                        def turn(j, src):
                            n = u * 3 + j
                            pe.wait_ge(tfree, i * 6 + n + 1)
                            for p in range(4):
                                m = pe.transpose(turned[n % 2][:, p * 128:(p + 1) * 128], src[:, p * 128:(p + 1) * 128], K.ident[:])
                            m.then_inc(tfull, 1)
                        turn(0, comp[u][:, 0:D])
                        pe.wait_ge(kb_ready, c + 1)
                        turn(1, kb[u][:])
                        pe.wait_ge(gu_ready, c + 1)
                        pe.wait_ge(dec_ready, c + 1)
                        for j in range(2):
                            m = pe.matmul(dsum[j][:], K.later[:], gu[u][:, 4 * j:4 * j + 4, :].rearrange("p h i -> p (h i)"), start=True, stop=True)
                        m.then_inc(dfull, 1)
                        turn(2, comp[u][:, D:2 * D])
                        pe.wait_ge(tfree, i * 6 + u * 3 + 5)
                        for p in range(4):
                            pe.wait_ge(kfree, c * 4 + 2 * (p // 2) + 2)
                            for hh in range(2):
                                s = slice(64 * hh, 64 * hh + 64)
                                m = pe.matmul(kq[p // 2 * 2 + hh][:, p % 2].rearrange("p s i -> p (s i)"), kT[s, p, :], bq[s, p].rearrange("p s i -> p (s i)"), start=True, stop=True)
                            if p % 2:
                                m.then_inc(kfull, 2)

            @block.scalar
            def _(act):
                with act.Fori(0, NB) as i:
                    for u in range(2):
                        c = i * 2 + u
                        act.wait_ge(kfull, c * 4 + 8)
                        for j, dst in ((0, kT[:]), (1, bq[:, :, 0, :])):
                            n = u * 3 + j
                            act.wait_ge(tfull, i * 6 + n + 1)
                            act.activation(dst, turned[n % 2][:].rearrange("p (a b) -> p a b", a=4), ACT.Copy).then_inc(tfree, 1)
                        act.wait_ge(kfree, c * 4 + 4)
                        act.wait_ge(dfull, c + 3)
                        for j in range(2):
                            m = act.activation(dec[:, 4 * j:4 * j + 4, :], dsum[j][:].rearrange("p (h i) -> p h i", h=4), ACT.Exp)
                        m.then_inc(dec_ready, 1)
                        n = u * 3 + 2
                        act.wait_ge(tfull, i * 6 + n + 1)
                        act.activation(bq[:, :, 1, :], turned[n % 2][:].rearrange("p (a b) -> p a b", a=4), ACT.Copy).then_inc(tfree, 1)

            @block.vector
            def _(dve):
                for s, n in ((tfree, 2), (kfree, 4), (kfull, 8), (dfull, 2), (out_free, 2), (dec_ready, 1)):
                    dve.drain().then_inc(s, n)
                with dve.Fori(0, NB) as i:
                    for u in range(2):
                        c = i * 2 + u
                        dve.wait_ge(c_in[u], (i + 1) * 16)
                        dve.wait_ge(dfull, c + 1)
                        dve.tensor_tensor(gu[u][:], K.upto[:].unsqueeze(1).to_broadcast([128, H, 128]),
                                          comp[u][:, 3 * D + H:ROW].unsqueeze(2).to_broadcast([128, H, 128]), ALU.mult).then_inc(gu_ready, 1)
                        dve.wait_ge(dec_cut, c + 1)
                        dve.wait_ge(out_free, c + 1)
                        for p in range(4):
                            dve.wait_ge(kfull, c * 4 + 2 * (p // 2) + 10)
                            two = slice(4 * (p // 2) + p % 2, 4 * (p // 2) + p % 2 + 3, 2)
                            m = dve.tensor_tensor(prod[u][:, two], kq[p][:],
                                                  dec[:, two, :].unsqueeze(2).to_broadcast([128, 2, 2, 128]), ALU.mult)
                            m.then_inc(kfree, 1)
                        dve.drain().then_inc(p_ready, 1)


def solve_blocks(nc, K, diag, inv):
    CG = 32
    with ExitStack() as ctx:
        P = Pools(nc, ctx, "s")
        b_sb = [P.sb(f"b{u}", [128, 32, H, 32]) for u in range(2)]
        r_sb = P.sb("r", [128, 32, H, 32])
        tmp = P.sb("tmp", [128, 16 * 16 * H])
        eye, eyei = P.sb("eye", [128, 32, 32]), P.sem("eyei")
        b_in, done, free = P.sems("b_in"), P.sem("done"), P.sem("free")
        r_out = P.sem("r_out")
        dv = diag.rearrange("(g c) (b j) n -> g (c b) (j n)", c=CG, b=4)
        rv = inv.rearrange("(g c) (b j) n -> g (c b) (j n)", c=CG, b=4)
        NGR = NCH // CG
        with nc.Block() as block:
            @block.sync
            def _(sp):
                for g in range(NGR):
                    if g >= 2:
                        sp.wait_ge(done, g - 1)
                    sp.dma_start(b_sb[g % 2][:].rearrange("p j h i -> p (j h i)"), dv[g]).then_inc(b_in[g % 2], 16)
                    if g >= 1:
                        sp.wait_ge(done, g)
                        sp.dma_start(rv[g - 1], r_sb[:].rearrange("p j h i -> p (j h i)")).then_inc(r_out, 16)
                        sp.wait_ge(r_out, 16 * g)
                        sp.nop().then_inc(free, 1)
                sp.wait_ge(done, NGR)
                sp.dma_start(rv[NGR - 1], r_sb[:].rearrange("p j h i -> p (j h i)")).then_inc(r_out, 16)
                sp.wait_ge(r_out, 16 * NGR)

            @block.gpsimd
            def _(pool):
                pool.memset(eye[:], 1.0)
                pool.drain()
                pool.affine_select(out=eye[:], in_=eye[:], compare_op=ALU.is_equal, fill=0.0, base=0,
                                   pattern=[[1, 32], [-1, 32]], channel_multiplier=0).then_inc(eyei, 1)

            @block.vector
            def _(dve):
                dve.wait_ge(eyei, 1)
                for g in range(NGR):
                    dve.wait_ge(b_in[g % 2], 16 * (g // 2 + 1))
                    if g >= 1:
                        dve.wait_ge(free, g)
                    B = b_sb[g % 2]
                    dve.tensor_copy(r_sb[:], eye[:].unsqueeze(2).to_broadcast([128, 32, H, 32]))
                    dve.drain()
                    for m in range(31, 0, -1):
                        S = [128, m, H, 32 - m]
                        t = tmp[:, 0:m * H * (32 - m)].rearrange("p (j h i) -> p j h i", j=m, h=H)
                        dve.tensor_tensor(t, B[:, 0:m, :, m:m + 1].to_broadcast(S), r_sb[:, m:m + 1, :, m:32].to_broadcast(S), ALU.mult)
                        dve.drain()
                        dve.tensor_tensor(r_sb[:, 0:m, :, m:32], r_sb[:, 0:m, :, m:32], t, ALU.subtract)
                        dve.drain()
                    dve.nop().then_inc(done, 1)


RUNS = 2 * D


def recur(nc, K, rows, aq, inv, keep, orows):
    with ExitStack() as ctx:
        P = Pools(nc, ctx, "c")
        comp = [P.sb(f"comp{u}", [128, ROW]) for u in range(2)]
        prod = [P.sb(f"prod{u}", [128, H, 2, 128]) for u in range(2)]
        tt = [P.sb(f"tt{u}", [128, H, 32]) for u in range(2)]
        td = [P.sb(f"td{u}", [128, H, 128]) for u in range(2)]
        tu = [P.sb(f"tu{u}", [128, H, 128]) for u in range(2)]
        gam = [P.sb(f"gam{u}", [128, 3, H]) for u in range(2)]
        bg = P.sb("bg", [128, H])
        X = [P.sb(f"X{u}", [128, H, 128]) for u in range(2)]
        kd = [P.sb(f"kd{u}", [128, H, DK]) for u in range(2)]
        qg = [P.sb(f"qg{u}", [128, H, DK]) for u in range(2)]
        pt, ya, yb = P.sb("pt", [128, H, 128]), P.sb("ya", [128, H, 128]), P.sb("yb", [128, H, 128])
        wtn, qgT = P.sb("wtn", [128, 4, 128]), P.sb("qgT", [128, 4, 128])
        U = P.sb("U", [128, H, DK])
        O = [P.sb(f"O{u}", [128, 4, 2, DK]) for u in range(2)]
        S = [P.sb(f"S{u}", [128, 4, DK]) for u in range(2)]
        gk, sd = P.sb("gk", [128, 4]), P.sb("sd", [128, 4, DK])
        set0 = [P.ps(f"seta{j}", [128, 4, 128]) for j in range(2)]
        set1 = [P.ps(f"setb{j}", [128, 4, 128]) for j in range(2)]
        qw = P.ps("qw", [128, 4, 128])
        ob = [P.ps(f"ob{j}", [128, 4, DK]) for j in range(2)]
        ub = [set0[j][:].rearrange("p a b -> p (a b)")[:, 0:4 * DK].rearrange("p (a d) -> p a d", d=DK) for j in range(2)]
        sg = P.ps("sg", [128, 512])
        c_in, a_in, t_in = P.sems("c_in"), P.sems("a_in"), P.sems("t_in")
        names = ("gfull", "gready", "pool_ready", "xv_ready", "tu_ready", "td_ready", "ptfull", "ptready", "yfull", "yready",
                 "qfull", "qready", "wfull", "wready", "ufull", "uready", "ofull", "oready", "sfull", "sready", "o_free", "zeroed")
        (gfull, gready, pool_ready, xv_ready, tu_ready, td_ready, ptfull, ptready, yfull, yready, qfull, qready, wfull, wready,
         ufull, uready, ofull, oready, sfull, sready, o_free, zeroed) = (P.sem(n) for n in names)
        o_out, dumped = P.sems("o_out"), P.sem("dumped")
        NB = NCH // 2
        half = [slice(0, 64), slice(64, 128)]
        flat = lambda a: a.rearrange("p h i -> p (h i)")
        with nc.Block() as block:
            @block.sync
            def _(sp):
                def load(c, u):
                    sp.dma_start(comp[u][:], rows[bass.ds(c * CH, CH), :]).then_inc(c_in[u], 16)
                    sp.dma_start(prod[u][:].rearrange("p h s i -> p (h s i)"), aq[bass.ds(c, 1), :, :].rearrange("a p n -> p (a n)")).then_inc(a_in[u], 16)
                    sp.dma_start(flat(tt[u][:]), inv[bass.ds(c, 1), :, :].rearrange("a p n -> p (a n)")).then_inc(t_in[u], 16)

                def leave(i, u, more):
                    c = i * 2 + u
                    sp.wait_ge(oready, c * 2 + 4)
                    sp.dma_start(orows[bass.ds(c * CH, CH), :], O[u][:].rearrange("p a b d -> p (a b d)")).then_inc(o_out[u], 16)
                    if more:
                        load(c + 2, u)
                    sp.wait_ge(o_out[u], (i + 1) * 16)
                    sp.nop().then_inc(o_free, 1)

                sp.dma_start(orows[NP:NP + 128, :], K.zero[:, 0:D]).then_inc(dumped, 16)
                load(0, 0)
                load(1, 1)
                with sp.Fori(0, NB - 1) as i:
                    for u in range(2):
                        leave(i, u, True)
                for u in range(2):
                    leave(NB - 1, u, False)
                sp.wait_ge(dumped, 16)

            @block.gpsimd
            def _(pool):
                for u in range(2):
                    pool.memset(td[u][:], 0.0)
                    pool.memset(tu[u][:], 0.0)
                    pool.memset(S[u][:], 0.0)
                pool.drain().then_inc(zeroed, 1)
                with pool.Fori(0, NB) as i:
                    for u in range(2):
                        c = i * 2 + u
                        hold(pool, K, gready, c + 1)
                        hold(pool, K, sfull, c + 1)
                        three = [comp[u][:, j * D:(j + 1) * D].rearrange("p (h d) -> p h d", h=H) for j in range(3)]
                        wide = lambda a: a.unsqueeze(2).to_broadcast([128, H, DK])
                        pool.tensor_tensor(bg[:], comp[u][:, 3 * D:3 * D + H], gam[u][:, 0, :], ALU.mult)
                        pool.drain()
                        pool.tensor_tensor(qg[u][:], three[1], wide(gam[u][:, 0, :]), ALU.mult)
                        pool.tensor_tensor(X[u][:, :, DK:2 * DK], three[0], wide(bg[:]), ALU.mult)
                        pool.tensor_tensor(kd[u][:], three[0], wide(gam[u][:, 1, :]), ALU.mult)
                        pool.drain().then_inc(pool_ready, 1)

            @block.tensor
            def _(pe):
                pe.wait_ge(zeroed, 1)
                with pe.Fori(0, NB) as i:
                    for u in range(2):
                        c = i * 2 + u
                        pe.wait_ge(c_in[u], (i + 1) * 16)
                        pe.wait_ge(sready, c + 1)
                        for j, m in enumerate((K.upto, K.later, K.ones)):
                            mm = pe.matmul(sg[:, 256 + j * H:256 + (j + 1) * H], m[:], comp[u][:, 3 * D + H:ROW], start=True, stop=True)
                        mm.then_inc(gfull, 1)
                        pe.wait_ge(a_in[u], (i + 1) * 16)
                        pe.wait_ge(tu_ready, c + 1)
                        for j in range(2):
                            for h in range(4 * j, 4 * j + 4):
                                mm = pe.matmul(set0[j][:, h % 4, :], tu[u][:, h, :], prod[u][:, h, 0, :], start=True, stop=True)
                            mm.then_inc(ptfull, 1)
                        pe.wait_ge(pool_ready, c + 1)
                        pe.wait_ge(wready, c + 1)
                        for p in range(4):
                            mm = pe.transpose(qw[:, p, :], qg[u][:, 2 * p:2 * p + 2, :].rearrange("p h d -> p (h d)"), K.ident[:])
                        mm.then_inc(qfull, 1)
                        pe.wait_ge(xv_ready, c + 1)
                        for s, (bank, y) in enumerate(((set1, X[u]), (set0, ya), (set1, yb))):
                            for j in range(2):
                                pe.wait_ge(*((ptready, c * 2 + j + 1) if s == 0 else (yready, c * 6 + s * 2 - 2 + j + 1)))
                                for h in range(4 * j, 4 * j + 4):
                                    mm = pe.matmul(bank[j][:, h % 4, :], pt[:, h, :], y[:, h, :], start=True, stop=True)
                                mm.then_inc(yfull, 1)
                        pe.wait_ge(qready, c + 1)
                        pe.wait_ge(td_ready, c + 1)
                        pe.wait_ge(yready, c * 6 + 6)
                        for h in range(H):
                            mm = pe.matmul(qw[half[h % 2], h // 2, :], ya[:, h, DK:2 * DK], td[u][:, h, :], start=True, stop=True)
                        mm.then_inc(wfull, 1)
                        for h in range(H):
                            pe.matmul(ub[h % 2][:, h // 2, :], td[u][:, h, :], ya[:, h, 0:DK], start=(h < 2), stop=False, skip_group_check=True)
                        pe.wait_ge(wready, c + 2)
                        for h in range(H):
                            mm = pe.matmul(ub[h % 2][:, h // 2, :], wtn[half[h % 2], h // 2, :], S[u][half[h % 2], h // 2, :],
                                           start=False, stop=True, skip_group_check=True)
                        mm.then_inc(ufull, 1)
                        pe.wait_ge(oready, c * 2 + 2)
                        for h in range(H):
                            pe.matmul(ob[h % 2][:, h // 2, :], qgT[half[h % 2], h // 2, :], S[u][half[h % 2], h // 2, :],
                                      start=(h < 2), stop=False, skip_group_check=True)
                        pe.wait_ge(uready, c + 1)
                        for h in range(H):
                            mm = pe.matmul(sg[half[h % 2], (h // 2) * DK:(h // 2 + 1) * DK], kd[u][:, h, :], U[:, h, :], start=True, stop=True)
                        mm.then_inc(sfull, 1)
                        for h in range(H):
                            mm = pe.matmul(ob[h % 2][:, h // 2, :], prod[u][:, h, 1, :], U[:, h, :], start=False, stop=True, skip_group_check=True)
                        mm.then_inc(ofull, 1)

            @block.scalar
            def _(act):
                act.wait_ge(zeroed, 1)
                with act.Fori(0, NB) as i:
                    for u in range(2):
                        c = i * 2 + u
                        act.wait_ge(gfull, c + 1)
                        act.activation(gam[u][:].rearrange("p j h -> p (j h)"), sg[:, 256:256 + 3 * H], ACT.Exp).then_inc(gready, 1)
                        act.wait_ge(t_in[u], (i + 1) * 16)
                        for b in range(4):
                            s = slice(32 * b, 32 * b + 32)
                            m = act.activation(td[u][s, :, s], tt[u][s], ACT.Copy)
                        m.then_inc(td_ready, 1)
                        for j in range(2):
                            act.wait_ge(ptfull, c * 2 + j + 1)
                            act.activation(pt[:, 4 * j:4 * j + 4, :], set0[j][:], ACT.Copy).then_inc(ptready, 1)
                        act.wait_ge(qfull, c + 1)
                        act.activation(qgT[:], qw[:], ACT.Copy).then_inc(qready, 1)
                        act.wait_ge(wfull, c + 1)
                        act.activation(wtn[:], qw[:], ACT.Copy, scale=-1.0).then_inc(wready, 1)
                        act.wait_ge(ofull, c + 1)
                        act.wait_ge(o_free, c + 1)
                        for j in range(2):
                            act.activation(O[u][:, :, j, :], ob[j][:], ACT.Copy).then_inc(oready, 1)

            @block.vector
            def _(dve):
                dve.wait_ge(zeroed, 1)
                for s, n in ((sready, 1), (wready, 1), (oready, 2), (o_free, 2), (sfull, 2)):
                    dve.drain().then_inc(s, n)
                with dve.Fori(0, NB) as i:
                    for u in range(2):
                        c = i * 2 + u
                        dve.wait_ge(t_in[u], (i + 1) * 16)
                        for b in range(4):
                            s = slice(32 * b, 32 * b + 32)
                            dve.transpose(tu[u][s, :, s], tt[u][s])
                        dve.drain().then_inc(tu_ready, 1)
                        dve.wait_ge(c_in[u], (i + 1) * 16)
                        dve.tensor_tensor(X[u][:, :, 0:DK], comp[u][:, 2 * D:3 * D].rearrange("p (h d) -> p h d", h=H),
                                          comp[u][:, 3 * D:3 * D + H].unsqueeze(2).to_broadcast([128, H, DK]), ALU.mult)
                        dve.wait_ge(gready, c + 1)
                        for hh in range(2):
                            s = half[hh]
                            dve.tensor_scalar(gk[s], gam[u][s, 2, hh:H:2], keep[s, bass.ds(c + 1, 1)], None, ALU.mult)
                        dve.drain().then_inc(xv_ready, 1)
                        dve.wait_ge(pool_ready, c + 1)
                        for st, (bank, y) in enumerate(((set1, ya), (set0, yb), (set1, ya))):
                            for j in range(2):
                                dve.wait_ge(yfull, c * 6 + st * 2 + j + 1)
                                dve.tensor_tensor(y[:, 4 * j:4 * j + 4, :], X[u][:, 4 * j:4 * j + 4, :], bank[j][:], ALU.subtract).then_inc(yready, 1)
                        dve.tensor_tensor(sd[:], S[u][:], gk[:].unsqueeze(2).to_broadcast([128, 4, DK]), ALU.mult)
                        dve.wait_ge(ufull, c + 1)
                        for j in range(2):
                            m = dve.tensor_copy(U[:, j:H:2, :], ub[j])
                        m.then_inc(uready, 1)
                        dve.wait_ge(sfull, c + 3)
                        dve.scalar_tensor_tensor(S[1 - u][:].rearrange("p a d -> p (a d)"), sg[:, 0:256], keep[:, bass.ds(c + 1, 1)], sd[:].rearrange("p a d -> p (a d)"),
                                                 ALU.mult, ALU.add)
                        dve.drain().then_inc(sready, 1)


def finish(nc, K, h3T, x3, orows, w, weights, pos, out):
    with ExitStack() as ctx:
        P = Pools(nc, ctx, "g")
        wg, wo = P.sb("wg", [128, KC, D]), P.sb("wo", [128, KC, D])
        nw = P.sb("nw", [R, H, DK])
        feat = [P.sb(f"feat{u}", [128, KC, GR]) for u in range(2)]
        xin = [P.sb(f"xin{u}", [R, G, D]) for u in range(2)]
        ix = [[P.sb(f"ix{v}{s}", [R, 1], I32) for s in range(2)] for v in range(2)]
        o = [[P.sb(f"o{v}{s}", [R, D]) for s in range(2)] for v in range(2)]
        gate = [P.sb(f"gate{v}", [R, D]) for v in range(2)]
        core = [P.sb(f"core{v}", [R, D]) for v in range(2)]
        sq = P.sb("sq", [R, D])
        cT = [P.sb(f"cT{v}", [128, KC, R]) for v in range(2)]
        ss, inv, tmp = P.sb("ss", [R, H]), P.sb("inv", [R, H]), P.sb("tmp", [R, H])
        pg = [P.ps(f"pg{v}", [R, 512]) for v in range(2)]
        pt = [P.ps(f"pt{v}", [128, KC, R]) for v in range(2)]
        po = [P.ps(f"po{v}", [R, 512]) for v in range(2)]
        wld = P.sem("wld")
        f_in, x_in, x_out = P.sems("f_in"), P.sems("x_in"), P.sems("x_out")
        got = [[P.sem(f"got{v}{s}") for s in range(2)] for v in range(2)]
        gfull, gready, cready, tfull, tready, pfull, pfree, group, o_free = (P.sem(n) for n in (
            "gfull", "gready", "cready", "tfull", "tready", "pfull", "pfree", "group", "o_free"))
        xrows, outrows = (a.rearrange("(n r) d -> r n d", r=R) for a in (x3, out))
        NB = NG // 2
        with nc.Block() as block:
            @block.sync
            def _(sp):
                sp.dma_start(wg[:], w["wg"].rearrange("(k p) n -> p k n", p=128)).then_inc(wld, 16)
                sp.dma_start(wo[:], w["wo"].rearrange("(k p) n -> p k n", p=128)).then_inc(wld, 16)
                for h in range(H):
                    sp.dma_start(nw[:, h, :], w["nw"].to_broadcast([R, DK])).then_inc(wld, 16)

                def load(ig, u):
                    sp.dma_start(feat[u][:].rearrange("p k n -> p (k n)"), h3T[bass.ds(ig, 1), :, :].rearrange("a p n -> p (a n)")).then_inc(f_in[u], 16)
                    sp.dma_start(xin[u][:], xrows[:, bass.ds(ig * G, G), :]).then_inc(x_in[u], 16)

                def leave(i, u, more):
                    ig = i * 2 + u
                    sp.wait_ge(pfree, ig * G + G + 2)
                    sp.dma_start(outrows[:, bass.ds(ig * G, G), :], xin[u][:]).then_inc(x_out[u], 16)
                    sp.wait_ge(x_out[u], (i + 1) * 16)
                    if more:
                        load(ig + 2, u)
                load(0, 0)
                load(1, 1)
                with sp.Fori(0, NB - 1) as i:
                    for u in range(2):
                        leave(i, u, True)
                for u in range(2):
                    leave(NB - 1, u, False)

            @block.gpsimd
            def _(pool):
                with pool.Fori(0, T // 2) as i:
                    for v in range(2):
                        t = i * 2 + v
                        hold(pool, K, cready, t + 1)
                        for s in range(2):
                            pool.tensor_copy(ix[v][s][:], pos[:, s, bass.ds(t, 1)])
                        pool.drain()
                        for s in range(2):
                            pool.indirect_dma_start(o[v][s][:], None, orows, bass.IndirectOffsetOnAxis(ap=ix[v][s][:, 0:1], axis=0),
                                                    bounds_check=NP + 127, oob_is_err=True).then_inc(got[v][s], 16)

            @block.tensor
            def _(pe):
                pe.wait_ge(wld, 16 * (2 + H))
                with pe.Fori(0, NB) as i:
                    for u in range(2):
                        pe.wait_ge(f_in[u], (i + 1) * 16)
                        for g in range(G):
                            v = g % 2
                            t = (i * 2 + u) * G + g
                            pe.wait_ge(gready, t + 1)
                            for k in range(KC):
                                m = pe.matmul(pg[v][:], feat[u][:, k, g * R:(g + 1) * R], wg[:, k, :], start=(k == 0), stop=(k == KC - 1))
                            m.then_inc(gfull, 1)
                            pe.wait_ge(cready, t + 3)
                            for k in range(KC):
                                m = pe.transpose(pt[v][:, k, :], core[v][:, k * 128:(k + 1) * 128], K.ident[0:R, 0:R])
                            m.then_inc(tfull, 1)
                            pe.wait_ge(tready, t + 1)
                            pe.wait_ge(pfree, t + 1)
                            for k in range(KC):
                                m = pe.matmul(po[v][:], cT[v][:, k, :], wo[:, k, :], start=(k == 0), stop=(k == KC - 1))
                            m.then_inc(pfull, 1)

            @block.scalar
            def _(act):
                with act.Fori(0, T // 2) as i:
                    for v in range(2):
                        t = i * 2 + v
                        act.wait_ge(gfull, t + 1)
                        act.wait_ge(cready, t + 1)
                        act.activation(gate[v][:], pg[v][:], ACT.Silu).then_inc(gready, 1)
                        act.wait_ge(tfull, t + 1)
                        act.activation(cT[v][:], pt[v][:], ACT.Copy).then_inc(tready, 1)

            @block.vector
            def _(dve):
                for s, n in ((gready, 2), (cready, 2), (pfree, 2)):
                    dve.drain().then_inc(s, n)
                dve.wait_ge(wld, 16 * (2 + H))
                heads = lambda a: a.rearrange("p (h d) -> p h d", h=H)
                with dve.Fori(0, NB) as i:
                    for u in range(2):
                        dve.wait_ge(x_in[u], (i + 1) * 16)
                        for g in range(G):
                            v = g % 2
                            t = (i * 2 + u) * G + g
                            dve.wait_ge(got[v][0], (i * 4 + u * 2 + g // 2 + 1) * 16)
                            dve.wait_ge(got[v][1], (i * 4 + u * 2 + g // 2 + 1) * 16)
                            dve.tensor_scalar(o[v][0][:], o[v][0][:], weights[:, 0, bass.ds(t, 1)], None, ALU.mult)
                            dve.drain()
                            dve.wait_ge(pfree, t + 1)
                            dve.scalar_tensor_tensor(core[v][:], o[v][1][:], weights[:, 1, bass.ds(t, 1)], o[v][0][:], ALU.mult, ALU.add)
                            dve.drain()
                            dve.tensor_tensor(sq[:], core[v][:], core[v][:], ALU.mult)
                            dve.drain()
                            dve.tensor_reduce(ss[:], heads(sq[:]), AX.X, ALU.add)
                            dve.wait_ge(gready, t + 3)
                            dve.tensor_tensor(heads(gate[v][:]), heads(gate[v][:]), nw[:], ALU.mult)
                            dve.drain()
                            dve.tensor_scalar(ss[:], ss[:], 1.0 / DK, 1e-5, ALU.mult, ALU.add)
                            dve.tensor_tensor(core[v][:], core[v][:], gate[v][:], ALU.mult)
                            dve.drain()
                            rsqrt(dve, inv[:], ss[:], tmp[:])
                            dve.tensor_tensor(heads(core[v][:]), heads(core[v][:]), inv[:].unsqueeze(2).to_broadcast([R, H, DK]), ALU.mult)
                            dve.drain().then_inc(cready, 1)
                            dve.wait_ge(pfull, t + 1)
                            dve.tensor_tensor(xin[u][:, g, :], po[v][:], xin[u][:, g, :], ALU.add)
                            dve.drain().then_inc(pfree, 1)


INS = ("x", "src", "dst", "g1", "g2", "gb1", "gb2", "up", "gate", "gateb", "bup", "down", "bdown", "n1", "n2", "nb1", "nb2",
       "wl", "dtb", "alog", "wk", "wq", "wv", "wg", "wo", "nw")


def program(nc, a, out):
    def scratch(name, shape):
        return nc.dram_tensor(name, list(shape), F32, kind="Internal").ap()

    table0, table1 = scratch("table0", (N + R, D + 1)), scratch("table1", (N + R, D))
    x2, h2, x3, h3T = scratch("x2", (N, D)), scratch("h2", (N, D)), scratch("x3", (N, D)), scratch("h3T", (NG, 128, KC * GR))
    rows, orows = scratch("rows", (NP + 128, ROW)), scratch("orows", (NP + 128, D))
    aq, diag, inv = scratch("aq", (NCH, 128, 2 * H * CH)), scratch("diag", (NCH, 128, H * 32)), scratch("inv", (NCH, 128, H * 32))
    with ExitStack() as ctx:
        K = Consts()
        K.pool = Pools(nc, ctx, "k")
        constants(nc, K)
        aggregate(nc, K, "a", a["src"], a["dst"], a["x"], table0, True)
        first_layer(nc, K, a["x"], table0, a, x2, h2, rows)
        aggregate(nc, K, "n", a["src"], a["dst"], h2, table1, False)
        weights, pos = K.pool.sb("weights", [R, 2, T]), K.pool.sb("pos", [R, 2, T], I32)
        beta, decay, keep = K.pool.sb("beta", [R, T, H]), K.pool.sb("decay", [R, T, H]), K.pool.sb("keep", [128, NCH + 1])
        logits = K.pool.sb("logits", [R, T, NL])
        second_gnn(nc, K, h2, table1, x2, a, x3, h3T, logits)
        route(nc, K, logits, a, weights, pos, beta, decay, keep)
        project(nc, K, h3T, a, pos, beta, decay, rows)
        chunk_products(nc, K, rows, aq, diag)
        solve_blocks(nc, K, diag, inv)
        recur(nc, K, rows, aq, inv, keep, orows)
        finish(nc, K, h3T, x3, orows, a, weights, pos, out)


def kernel(**inputs):
    import numpy as np
    import concourse.bacc as bacc
    from concourse.bass_utils import run_bass_kernel_spmd

    v = {k: np.asarray(a) for k, a in inputs.items()}
    f = lambda name: v["L0_ffn_" + name]
    g = lambda name: v["L1_ffn_" + name]
    laid = {
        "x": v["x"], "src": v["src"].reshape(T, R), "dst": v["dst"].reshape(T, R),
        "g1": v["L0_gnn_W1"].T, "g2": v["L0_gnn_W2"].T, "gb1": v["L0_gnn_b1"][None], "gb2": v["L0_gnn_b2"][None],
        "up": np.concatenate([f("sw1").reshape(-1, D), f("rw1").reshape(-1, D)]).T, "gate": f("gate_w").T,
        "gateb": f("gate_b")[None], "bup": np.concatenate([f("sb1").ravel(), f("rb1").ravel()]).reshape(HC, 128).T,
        "down": np.concatenate([f("sw2").transpose(0, 2, 1).reshape(-1, D), f("rw2").transpose(0, 2, 1).reshape(-1, D)]),
        "bdown": np.concatenate([f("rb2"), f("sb2")]),
        "n1": v["L1_gnn_W1"], "n2": v["L1_gnn_W2"], "nb1": v["L1_gnn_b1"].reshape(KC, 128).T, "nb2": v["L1_gnn_b2"][None],
        "wl": np.concatenate([g("Wgate"), g("Wb"), g("Wa")], axis=1), "dtb": g("dt_bias")[None], "alog": g("A_log")[None],
        "wk": g("Wk"), "wq": g("Wq"), "wv": g("Wv"), "wg": g("Wg"), "wo": g("Wo"), "nw": g("o_norm_weight")[None],
    }
    nc = bacc.Bacc("TRN2", target_bir_lowering=False, num_devices=1)
    arrays, aps = {}, {}
    for name in INS:
        a = np.ascontiguousarray(laid[name])
        arrays[f"in_{name}"] = a
        aps[name] = nc.dram_tensor(f"in_{name}", a.shape, mybir.dt.from_np(a.dtype), kind="ExternalInput").ap()
    out = nc.dram_tensor("out", (N, D), F32, kind="ExternalOutput").ap()
    program(nc, aps, out)
    return run_bass_kernel_spmd(nc, [arrays], core_ids=[0]).results[0]["out"]
```

```python
from contextlib import ExitStack
import concourse.bass as bass
from concourse import mybir

F32 = mybir.dt.float32
I32 = mybir.dt.int32
ALU = mybir.AluOpType
ACT = mybir.ActivationFunctionType
AX = mybir.AxisListType

N = 10000
D = 512
KC = D // 128
R = 125
T = N // R
G = 4
GR = G * R
NG = N // GR
V4 = 4
ER = 8
HF = 640
HC = HF // 128
E4 = 4
H = 8
DK = 64
CH = 128
NCH = 2 * N // CH + E4
NP = NCH * CH
BETA, DECAY = 2 * D, 2 * D + H
V = CKQ = 2 * D + 2 * H
ROW = V + D
RSQRT_SEED = 0x5F3759DF


class Consts:
    pass


class Pools:

    def __init__(self, nc, ctx, tag):
        self.nc, self.ctx, self.tag = nc, ctx, tag
        self.held = []
        ctx.callback(self.release)

    def release(self):
        self.nc.clear_and_free_semaphores(self.held)
        self.nc.all_engine_barrier()

    def sb(self, name, shape, dt=F32):
        return self.ctx.enter_context(self.nc.sbuf_tensor(f"{self.tag}_{name}", shape, dt))

    def ps(self, name, shape, dt=F32):
        return self.ctx.enter_context(self.nc.psum_tensor(f"{self.tag}_{name}", shape, dt))

    def sem(self, name):
        self.held.append(self.nc.alloc_semaphore(name=f"{self.tag}_{name}"))
        return self.held[-1]

    def sems(self, name, n=2):
        return [self.sem(f"{name}{i}") for i in range(n)]


def hold(eng, K, sem, value):
    eng.wait_ge(sem, value)
    eng.nop().then_inc(K.passed, 1)


def rsqrt(dve, y, v, tmp):
    dve.tensor_scalar(y.bitcast(I32), v.bitcast(I32), 1, None, ALU.arith_shift_right)
    dve.drain()
    dve.tensor_scalar(y.bitcast(I32), y.bitcast(I32), -1.0, float(RSQRT_SEED), ALU.mult, ALU.add)
    dve.drain()
    for _ in range(3):
        dve.tensor_tensor(tmp, y, y, ALU.mult)
        dve.drain()
        dve.scalar_tensor_tensor(tmp, tmp, -0.5, v, ALU.mult, ALU.mult)
        dve.drain()
        dve.scalar_tensor_tensor(y, tmp, 1.5, y, ALU.add, ALU.mult)
        dve.drain()


def moments(dve, rows, n, stats, mv):
    for g in range(n):
        dve.bn_stats(stats[0:R, g, :], rows[0:R, g, 0:D])
    dve.drain()
    for g in range(n):
        dve.bn_aggr(mv[0:R, g, :], stats[0:R, g, :])
    dve.drain()


def layernorm(dve, out, rows, n, stats, mv, rstd, var, tmp):
    moments(dve, rows, n, stats, mv)
    dve.tensor_scalar(var[0:R, 0:n], mv[0:R, 0:n, 1], 1e-5, None, ALU.add)
    dve.drain()
    rsqrt(dve, rstd[0:R, 0:n], var[0:R, 0:n], tmp[0:R, 0:n])
    for g in range(n):
        dve.tensor_scalar(out[0:R, g, 0:D], rows[0:R, g, 0:D], mv[0:R, g, 0:1], rstd[0:R, g:g + 1],
                          ALU.subtract, ALU.mult)


def constants(nc, K):
    K.ident = K.pool.sb("ident", [128, 128])
    K.later = K.pool.sb("later", [128, 128])
    K.upto = K.pool.sb("upto", [128, 128])
    K.before = K.pool.sb("before", [128, 128])
    K.ones = K.pool.sb("ones", [128, 128])
    K.zero = K.pool.sb("zero", [128, ROW])
    K.dump = K.pool.sb("dump", [128, 1])
    K.dumpi = K.pool.sb("dumpi", [128, 1], I32)
    filled, K.passed = K.pool.sem("filled"), K.pool.sem("passed")
    with nc.Block() as block:
        @block.gpsimd
        def _(pool):
            pool.memset(K.ident[:], 0.0)
            pool.memset(K.ones[:], 1.0)
            pool.memset(K.zero[:], 0.0)
            pool.iota(K.dumpi[:], pattern=[[0, 1]], base=N, channel_multiplier=1).then_inc(filled, 1)
            pool.wait_ge(filled, 1)
            pool.affine_select(out=K.ident[:], in_=K.ident[:], compare_op=ALU.not_equal, fill=1.0, base=0,
                               pattern=[[-1, 128]], channel_multiplier=1)
            pool.affine_select(out=K.later[:], in_=K.ones[:], compare_op=ALU.is_gt, fill=0.0, base=0,
                               pattern=[[-1, 128]], channel_multiplier=1)
            pool.affine_select(out=K.upto[:], in_=K.ones[:], compare_op=ALU.is_ge, fill=0.0, base=0,
                               pattern=[[1, 128]], channel_multiplier=-1)
            pool.affine_select(out=K.before[:], in_=K.ones[:], compare_op=ALU.is_gt, fill=0.0, base=0,
                               pattern=[[1, 128]], channel_multiplier=-1)
            pool.tensor_copy(K.dump[:], K.dumpi[:]).then_inc(filled, 1)
            pool.wait_ge(filled, 2)


def aggregate(nc, K, tag, src, dst, dstrows, rows, tables, first):
    W = D + 1 if first else D
    BT = 2 * V4
    with ExitStack() as ctx:
        P = Pools(nc, ctx, tag)
        srcix = [P.sb(f"srcix{p}", [R, V4], I32) for p in range(2)]
        dstcol = [P.sb(f"dstcol{p}", [R, V4], I32) for p in range(2)]
        dstrow = [P.sb(f"dstrow{p}", [R, V4, R], I32) for p in range(2)]
        rowf, colf, scr = P.sb("rowf", [R, V4, R]), P.sb("colf", [R, V4]), P.sb("scr", [R, V4, R])
        eq = [P.sb(f"eq{p}", [R, V4, R]) for p in range(2)]
        earlier, move = P.sb("earlier", [R, V4]), P.sb("move", [R, V4])
        degree = P.sb("degree", [R, V4])
        sidx = [P.sb(f"sidx{p}", [R, V4], I32) for p in range(2)]
        gath = [P.sb(f"gath{p}", [R, V4, D]) for p in range(2)]
        comb = [P.sb(f"comb{j}", [R, W]) for j in range(BT)]
        stats, mv = P.sb("stats", [R, V4, 6]), P.sb("mv", [R, V4, 2])
        rstd, var, tmp = P.sb("rstd", [R, V4]), P.sb("var", [R, V4]), P.sb("tmp", [R, V4])
        total = [P.ps(f"total{j}", [R, 512]) for j in range(BT)]
        zeroed = P.sems("zeroed")
        src_in, col_in, row_in = P.sems("src_in"), P.sems("col_in"), P.sems("row_in")
        set_done = P.sem("set_done")
        gathered, added = P.sems("gathered", BT), P.sems("added", BT)
        landed = P.sem("landed")
        gath_ready, summed, comb_ready = P.sem("gath_ready"), P.sem("summed"), P.sem("comb_ready")
        NB = T // BT

        with nc.Block() as block:
            @block.sync
            def _(sp):
                with sp.Fori(0, NB) as i:
                    for p in range(2):
                        q = i * 2 + p
                        sp.wait_ge(set_done, q + 1)
                        sp.dma_start(srcix[p][:], src[bass.ds(q, 1), :, :].rearrange("a r v -> (a r) v")).then_inc(src_in[p], 16)
                        sp.dma_start(dstcol[p][:], dst[bass.ds(q, 1), :, :].rearrange("a r v -> (a r) v")).then_inc(col_in[p], 16)
                        sp.dma_start(dstrow[p][:], dstrows[bass.ds(q * V4, V4), :].unsqueeze(0).to_broadcast([R, V4, R])).then_inc(row_in[p], 16)

            @block.gpsimd
            def _(pool):
                def gather(i, p):
                    hold(pool, K, src_in[p], (i + 1) * 16)
                    hold(pool, K, summed, (i * 2 + p + 1) * V4)
                    for v in range(V4):
                        pool.indirect_dma_start(gath[p][:, v, :], None, rows,
                                                bass.IndirectOffsetOnAxis(ap=srcix[p][:, v:v + 1], axis=0),
                                                bounds_check=N - 1, oob_is_err=True).then_inc(gathered[p * V4 + v], 16)

                def add(i, j, later):
                    hold(pool, K, comb_ready, i * BT + j + 1)
                    if later:
                        hold(pool, K, added[(j - 2) % BT], (i + (1 if j >= 2 else 0)) * 16)
                        pool.nop().then_inc(landed, 1)
                    p, v = j // V4, j % V4
                    pool.indirect_dma_start(tables[j % 2], bass.IndirectOffsetOnAxis(ap=sidx[p][:, v:v + 1], axis=0),
                                            comb[j][:], None, bounds_check=N + R - 1, oob_is_err=True,
                                            compute_op=ALU.add).then_inc(added[j], 16)

                gather(0, 0)
                gather(0, 1)
                if first:
                    for t in range(2):
                        pool.wait_ge(zeroed[t], 32)
                for j in range(BT):
                    add(0, j, j >= 2)
                    if j % V4 == V4 - 1:
                        gather(1, j // V4)
                with pool.Fori(0, NB - 2) as i:
                    for j in range(BT):
                        add(i + 1, j, True)
                        if j % V4 == V4 - 1:
                            gather(i + 2, j // V4)
                for j in range(BT):
                    add(NB - 1, j, True)
                for j in (BT - 2, BT - 1):
                    pool.wait_ge(added[j], NB * 16)

            @block.vector
            def _(dve):
                dve.drain().then_inc(set_done, 2)
                dve.drain().then_inc(landed, BT)
                dve.drain().then_inc(summed, BT)
                with dve.Fori(0, NB) as i:
                    for p in range(2):
                        q = i * 2 + p
                        S = [R, V4, R]
                        dve.wait_ge(col_in[p], (i + 1) * 16)
                        dve.wait_ge(row_in[p], (i + 1) * 16)
                        dve.wait_ge(summed, (q + 1) * V4)
                        dve.wait_ge(landed, (q + 1) * V4)
                        dve.tensor_copy(rowf[:], dstrow[p][:])
                        dve.tensor_copy(colf[:], dstcol[p][:])
                        dve.drain()
                        dve.tensor_tensor(eq[p][:], rowf[:], colf[:].unsqueeze(2).to_broadcast(S), ALU.is_equal)
                        dve.drain()
                        dve.tensor_tensor(scr[:], eq[p][:], K.later[0:R, 0:R].unsqueeze(1).to_broadcast(S), ALU.mult)
                        dve.tensor_reduce(degree[:], eq[p][:], AX.X, ALU.add)
                        dve.drain()
                        dve.tensor_reduce(earlier[:], scr[:], AX.X, ALU.add)
                        dve.tensor_tensor(move[:], K.dump[0:R, 0:1].to_broadcast([R, V4]), colf[:], ALU.subtract)
                        if first:
                            for v in range(V4):
                                dve.tensor_copy(comb[p * V4 + v][:, D:W], degree[:, v:v + 1])
                        dve.drain()
                        dve.tensor_scalar(earlier[:], earlier[:], 1.0, None, ALU.min)
                        dve.drain()
                        dve.tensor_tensor(move[:], move[:], earlier[:], ALU.mult)
                        dve.drain()
                        dve.tensor_tensor(sidx[p][:], move[:], colf[:], ALU.add)
                        dve.drain()
                        for v in range(V4):
                            dve.wait_ge(gathered[p * V4 + v], (i + 1) * 16)
                        if first:
                            layernorm(dve, gath[p], gath[p], V4, stats, mv, rstd, var, tmp)
                            dve.drain()
                        dve.nop().then_inc(gath_ready, 1)
                        dve.nop().then_inc(set_done, 1)

            @block.tensor
            def _(pe):
                with pe.Fori(0, NB) as i:
                    for p in range(2):
                        pe.wait_ge(gath_ready, i * 2 + p + 1)
                        for v in range(V4):
                            pe.matmul(total[p * V4 + v][:, :], eq[p][:, v, :], gath[p][:, v, :], start=True, stop=True)\
                                .then_inc(summed, 1)

            @block.scalar
            def _(act):
                if first:
                    for t in range(2):
                        act.dma_start(tables[t][0:N, :].rearrange("(p t) w -> p t w", p=R),
                                      K.zero[0:R, 0:W].unsqueeze(1).to_broadcast([R, T, W])).then_inc(zeroed[t], 16)
                        act.wait_ge(zeroed[t], 16)
                        act.dma_start(tables[t][N:N + R, :], K.zero[0:R, 0:W]).then_inc(zeroed[t], 16)
                with act.Fori(0, NB) as i:
                    for j in range(BT):
                        act.wait_ge(summed, i * BT + j + BT + 1)
                        act.activation(comb[j][:, 0:D], total[j][:, :], ACT.Copy).then_inc(comb_ready, 1)


def first_layer(nc, K, x, tables, w, x2, h2, rows, tables1):
    with ExitStack() as ctx:
        P = Pools(nc, ctx, "b")
        w1, w2 = P.sb("w1", [128, KC, D]), P.sb("w2", [128, KC, D])
        wup, wgate = P.sb("wup", [128, KC, HF]), P.sb("wgate", [128, KC, ER])
        wdown = P.sb("wdown", [128, HC, D])
        bup, bdown = P.sb("bup", [128, HC]), P.sb("bdown", [ER + 2, D])
        spread = P.sb("spread", [ER + 2, ER // 2, 128])
        bias1, bias2, gbias = P.sb("bias1", [R, D]), P.sb("bias2", [R, D]), P.sb("gbias", [R, G, ER])
        desc = P.sb("desc", [R, G, ER])
        desci = P.sb("desci", [R, G, ER], I32)
        xin = [P.sb(f"xin{u}", [R, G, D]) for u in range(2)]
        agg, odd = ([P.sb(f"{n}{u}", [R, G, D + 1]) for u in range(2)] for n in ("agg", "odd"))
        x1 = [P.sb(f"x1{u}", [R, G, D]) for u in range(2)]
        xn, x1n, h2n = P.sb("xn", [R, G, D]), P.sb("x1n", [R, G, D]), P.sb("h2n", [R, G, D])
        featA, featB, featC = (P.sb(n, [128, KC, GR]) for n in ("featA", "featB", "featC"))
        hid = P.sb("hid", [128, HC, GR])
        stats, mv = P.sb("stats", [R, G, 6]), P.sb("mv", [R, G, 2])
        rstd, var, tmp = P.sb("rstd", [R, G]), P.sb("var", [R, G]), P.sb("tmp", [R, G])
        recip = P.sb("recip", [R, G])
        lg, pr, ta, tb = (P.sb(n, [R, G, ER]) for n in ("lg", "pr", "ta", "tb"))
        cw = P.sb("cw", [R, G, ER + 2])
        cwT = P.sb("cwT", [ER + 2, GR])
        red = P.sb("red", [R, G])
        turned = [P.ps(f"turned{u}", [128, 512]) for u in range(2)]
        acc = [P.ps(f"acc{u}", [128, 512]) for u in range(2)]
        up = [P.ps(f"up{u}", [128, 512]) for u in range(2)]
        small = P.ps("small", [128, 512])
        wide = P.ps("wide", [128, 512])
        wld, wready, counted = P.sem("wld"), P.sem("wready"), P.sem("counted")
        x_in, a_in, o_in = P.sems("x_in"), P.sems("a_in"), P.sems("o_in")
        xn_ready, an_ready, x_used = P.sem("xn_ready"), P.sem("an_ready"), P.sem("x_used")
        tfull, tfree = P.sem("tfull"), P.sem("tfree")
        afull, afree = P.sem("afull"), P.sem("afree")
        hfull, hfree = P.sem("hfull"), P.sem("hfree")
        x1n_ready = P.sem("x1n_ready")
        gates_full, cw_ready, cwT_full, cwT_ready = P.sem("gates_full"), P.sem("cw_ready"), P.sem("cwT_full"), P.sem("cwT_ready")
        exp_in, exp_out = P.sem("exp_in"), P.sem("exp_out")
        wfull, wfree = P.sem("wfull"), P.sem("wfree")
        hid_ready = P.sem("hid_ready")
        x2_ready, h2_ready, x1_free, h2_free = P.sem("x2_ready"), P.sem("h2_ready"), P.sem("x1_free"), P.sem("h2_free")
        z_out, z_rest = [P.sems(f"z_out{n}_") for n in range(3)], P.sems("z_rest", 3)
        x2_out, h2_out = P.sems("x2_out"), P.sem("h2_out")
        xrows = x.rearrange("(n r) d -> r n d", r=R)
        trows = [t[0:N, :].rearrange("(n r) d -> r n d", r=R) for t in tables]
        x2rows = x2.rearrange("(n r) d -> r n d", r=R)
        h2rows = h2.rearrange("(n r) d -> r n d", r=R)

        spreads = (wide, small)
        NB = NG // 2
        SA, SB = 2 * KC, KC

        def steps(eng, step):
            step(0, 0, True, False, True)
            step(0, 1, True, True, True)
            with eng.Fori(0, NB - 2) as i:
                for u in range(2):
                    step(i + 1, u, True, True, True)
            step(NB - 1, 0, True, True, True)
            step(NB - 1, 1, True, True, False)
            step(NB, 0, False, True, False)

        def bases(ig, a, b):
            if a and not b:
                return 0, 0, 0, 0
            t, m = ig * (SA + SB) - SB, ig * 2 * G - G
            return t, m, t + (SA if a else 0), m + (G if a else 0)

        with nc.Block() as block:
            @block.sync
            def _(sp):
                loads = [(w1, w["g1"].rearrange("(k p) n -> p k n", p=128)), (w2, w["g2"].rearrange("(k p) n -> p k n", p=128)),
                         (wup, w["up"].rearrange("(k p) n -> p k n", p=128)), (wgate, w["gate"].rearrange("(k p) n -> p k n", p=128)),
                         (wdown, w["down"].rearrange("(k p) n -> p k n", p=128)), (bup, w["bup"]), (bdown, w["bdown"]),
                         (bias1, w["gb1"].to_broadcast([R, D])), (bias2, w["gb2"].to_broadcast([R, D]))]
                for t, a in loads:
                    sp.dma_start(t[:], a).then_inc(wld, 16)
                for g in range(G):
                    sp.dma_start(gbias[:, g, :], w["gateb"].to_broadcast([R, ER])).then_inc(wld, 16)
                sp.wait_ge(wld, 16 * (len(loads) + G))
                sp.nop().then_inc(wready, 1)

                def load(t, u):
                    sp.dma_start(xin[u][:], xrows[:, bass.ds(t, G), :]).then_inc(x_in[u], 16)
                    sp.dma_start(agg[u][:], trows[0][:, bass.ds(t, G), :]).then_inc(a_in[u], 16)
                    sp.dma_start(odd[u][:], trows[1][:, bass.ds(t, G), :]).then_inc(o_in[u], 16)

                def load_next(i, u):
                    sp.wait_ge(x_used, i * 2 + u + 1)
                    load((i * 2 + u + 2) * G, u)

                def leave(i, u):
                    ig, w = i * 2 + u, 1 - u
                    t = (ig - 1) * G
                    sp.wait_ge(x2_ready, ig)
                    sp.dma_start(x2rows[:, bass.ds(t, G), :], x1[w][:]).then_inc(x2_out[w], 16)
                    sp.wait_ge(h2_ready, ig)
                    sp.dma_start(h2rows[:, bass.ds(t, G), :], h2n[:]).then_inc(h2_out, 16)
                    sp.wait_ge(x2_out[w], (i + u) * 16)
                    sp.nop().then_inc(x1_free, 1)
                    sp.wait_ge(h2_out, ig * 16)
                    sp.nop().then_inc(h2_free, 1)

                for u in range(2):
                    load(u * G, u)
                load_next(0, 0)
                load_next(0, 1)
                leave(0, 1)
                with sp.Fori(0, NB - 2) as i:
                    for u in range(2):
                        load_next(i + 1, u)
                        leave(i + 1, u)
                leave(NB - 1, 0)
                leave(NB - 1, 1)
                leave(NB, 0)

            @block.gpsimd
            def _(pool):
                pool.memset(cw[:], 1.0)
                pool.memset(spread[:], 1.0)
                pool.iota(desci[:], pattern=[[0, G], [-1, ER]], base=ER, channel_multiplier=0).then_inc(counted, 1)
                pool.wait_ge(counted, 1)
                pool.tensor_copy(desc[:], desci[:])
                pool.affine_select(out=spread[:], in_=spread[:], compare_op=ALU.is_ge, fill=0.0, base=0,
                                   pattern=[[128, ER // 2], [1, 128]], channel_multiplier=-64)
                pool.drain()
                pool.affine_select(out=spread[:], in_=spread[:], compare_op=ALU.is_ge, fill=0.0, base=63,
                                   pattern=[[-128, ER // 2], [-1, 128]], channel_multiplier=64)
                pool.drain()
                pool.wait_ge(wready, 1)
                pool.tensor_tensor(bias1[:], bias1[:], bias2[:], ALU.add).then_inc(wready, 1)

            @block.tensor
            def _(pe):
                pe.wait_ge(wready, 2)

                def turn(ti, j, srcs):
                    for k in range(KC):
                        n = j * KC + k
                        pe.wait_ge(tfree, ti + n + 1)
                        for g in range(G):
                            m = pe.transpose(turned[n % 2][:, g * R:(g + 1) * R], srcs[:, g, k * 128:(k + 1) * 128], K.ident[0:R, 0:R])
                        m.then_inc(tfull, 1)

                def step(i, u, a, b, more):
                    ig = i * 2 + u
                    ta, ma, tb, mb = bases(ig, a, b)
                    if a:
                        pe.wait_ge(xn_ready, ig + 1)
                        turn(ta, 0, xn)
                        pe.wait_ge(an_ready, ig + 1)
                        turn(ta, 1, agg[u])
                        pe.wait_ge(tfree, ta + SA + 2)
                        for g in range(G):
                            pe.wait_ge(afree, ma + g + 1)
                            for k in range(KC):
                                pe.matmul(acc[g % 2][0:R, :], featA[:, k, g * R:(g + 1) * R], w1[:, k, :], start=(k == 0), stop=False)
                            for k in range(KC):
                                m = pe.matmul(acc[g % 2][0:R, :], featB[:, k, g * R:(g + 1) * R], w2[:, k, :], start=False, stop=(k == KC - 1))
                            m.then_inc(afull, 1)
                    if b:
                        pe.wait_ge(x1n_ready, ig)
                        turn(tb, 0, x1n)
                        pe.wait_ge(tfree, tb + SB + 2)
                        for g in range(G):
                            for k in range(KC):
                                m = pe.matmul(small[0:R, g * ER:(g + 1) * ER], featC[:, k, g * R:(g + 1) * R], wgate[:, k, :], start=(k == 0), stop=(k == KC - 1))
                        m.then_inc(gates_full, 1)
                        for c in range(HC):
                            pe.wait_ge(hfree, (ig - 1) * HC + c + 1)
                            for k in range(KC):
                                m = pe.matmul(up[c % 2][:, 0:GR], wup[:, k, c * 128:(c + 1) * 128], featC[:, k, :], start=(k == 0), stop=(k == KC - 1))
                            m.then_inc(hfull, 1)
                        pe.wait_ge(cw_ready, ig)
                        for g in range(G):
                            m = pe.transpose(wide[0:ER + 2, g * R:(g + 1) * R], cw[:, g, :], K.ident[0:R, 0:R])
                        m.then_inc(cwT_full, 1)
                        pe.wait_ge(cwT_ready, ig)
                        for c in range(ER // 2):
                            pe.wait_ge(wfree, (ig - 1) * (ER // 2) + c + 1)
                            pe.matmul(spreads[c % 2][:, 0:GR], spread[:, c, :], cwT[:], start=True, stop=True).then_inc(wfull, 1)
                        pe.wait_ge(hid_ready, ig)
                        for g in range(G):
                            pe.wait_ge(afree, mb + g + 1)
                            for c in range(HC):
                                pe.matmul(acc[g % 2][0:R, :], hid[:, c, g * R:(g + 1) * R], wdown[:, c, :], start=(c == 0), stop=False)
                            pe.matmul(acc[g % 2][0:R, :], cwT[:, g * R:(g + 1) * R], bdown[:], start=False, stop=True).then_inc(afull, 1)
                steps(pe, step)

            @block.scalar
            def _(act):
                act.wait_ge(wready, 2)

                def evict(base, j, dst):
                    for k in range(KC):
                        n = j * KC + k
                        act.wait_ge(tfull, base + n + 1)
                        act.activation(dst[:, k, :], turned[n % 2][:, 0:GR], ACT.Copy).then_inc(tfree, 1)

                PR = (NP + 128) // 128
                zrows = rows.rearrange("(p t) w -> p t w", p=128)
                part = (PR - 1) // NG
                act.dma_start(zrows[:, PR - 1, :], K.zero[:]).then_inc(z_rest[2], 16)
                ztabs = [t.rearrange("(n r) d -> r n d", r=R) for t in tables1]
                for n in range(2):
                    act.dma_start(ztabs[n][:, T, :], K.zero[0:R, 0:D]).then_inc(z_rest[n], 16)
                def step(i, u, a, b, more):
                    ig = i * 2 + u
                    ta, _, tb, _ = bases(ig, a, b)
                    if a:
                        act.dma_start(zrows[:, bass.ds(ig * part, part), :], K.zero[:].unsqueeze(1).to_broadcast([128, part, ROW])).then_inc(z_out[2][u], 16)
                        for n in range(2):
                            act.dma_start(ztabs[n][:, bass.ds(ig * G, G), :], K.zero[0:R, 0:D].unsqueeze(1).to_broadcast([R, G, D])).then_inc(z_out[n][u], 16)
                        evict(ta, 0, featA)
                        evict(ta, 1, featB)
                    if b:
                        evict(tb, 0, featC)
                        act.wait_ge(exp_in, ig)
                        act.activation(pr[:], lg[:], ACT.Exp).then_inc(exp_out, 1)
                        for c in range(HC):
                            act.wait_ge(hfull, (ig - 1) * HC + c + 1)
                            act.activation(hid[:, c, :], up[c % 2][:, 0:GR], ACT.Gelu, bias=bup[:, c:c + 1]).then_inc(hfree, 1)
                steps(act, step)
                for n in range(3):
                    act.wait_ge(z_rest[n], 16)
                    for u in range(2):
                        act.wait_ge(z_out[n][u], 16 * NB)

            @block.vector
            def _(dve):
                dve.wait_ge(wready, 2)
                for s, n in ((tfree, 2), (afree, 2), (hfree, 2), (wfree, 2), (x1_free, 2), (h2_free, 1)):
                    dve.drain().then_inc(s, n)

                def topk_onehot(dst, p, m):
                    dve.tensor_reduce(red[:], p, AX.X, ALU.max)
                    dve.drain()
                    dve.tensor_tensor(dst, p, red[:].unsqueeze(2).to_broadcast([R, G, ER]), ALU.is_equal)
                    dve.drain()
                    dve.tensor_tensor(dst, dst, desc[:], ALU.mult)
                    dve.drain()
                    dve.tensor_reduce(red[:], dst, AX.X, ALU.max)
                    dve.drain()
                    dve.tensor_tensor(dst, desc[:], red[:].unsqueeze(2).to_broadcast([R, G, ER]), ALU.is_equal)
                    dve.drain()

                def mean(u):
                    dve.tensor_tensor(recip[:], agg[u][:, :, D], odd[u][:, :, D], ALU.add)
                    dve.drain()
                    dve.tensor_scalar(recip[:], recip[:], 1.0, None, ALU.max)
                    dve.drain()
                    dve.reciprocal(recip[:], recip[:])
                    dve.drain()
                    for g in range(G):
                        dve.tensor_tensor(agg[u][:, g, 0:D], agg[u][:, g, 0:D], odd[u][:, g, 0:D], ALU.add)
                    dve.drain()
                    for g in range(G):
                        dve.tensor_scalar(agg[u][:, g, 0:D], agg[u][:, g, 0:D], recip[:, g:g + 1], None, ALU.mult)
                    dve.drain().then_inc(an_ready, 1)

                def norm(u):
                    layernorm(dve, xn, xin[u], G, stats, mv, rstd, var, tmp)
                    dve.drain().then_inc(xn_ready, 1)
                    for g in range(G):
                        dve.tensor_tensor(xin[u][:, g, :], xin[u][:, g, :], bias1[:], ALU.add)
                    dve.drain()

                def step(i, u, a, b, more):
                    ig, w = i * 2 + u, 1 - u
                    _, ma, _, mb = bases(ig, a, b)
                    if b:
                        layernorm(dve, x1n, x1[w], G, stats, mv, rstd, var, tmp)
                        dve.drain().then_inc(x1n_ready, 1)
                    if a:
                        dve.wait_ge(x1_free, ig + 1)
                        for g in range(G):
                            dve.wait_ge(afull, ma + g + 1)
                            m = dve.tensor_tensor(x1[u][:, g, :], acc[g % 2][0:R, :], xin[u][:, g, :], ALU.add)
                            m.then_inc(afree, 1)
                        dve.drain().then_inc(x_used, 1)
                    if more:
                        dve.wait_ge(a_in[w], (i + 1 + u) * 16)
                        dve.wait_ge(o_in[w], (i + 1 + u) * 16)
                        mean(w)
                    if b:
                        dve.wait_ge(gates_full, ig)
                        dve.tensor_tensor(lg[:], small[0:R, 0:G * ER].rearrange("p (g e) -> p g e", g=G), gbias[:], ALU.add)
                        dve.drain()
                        dve.tensor_reduce(red[:], lg[:], AX.X, ALU.max)
                        dve.drain()
                        dve.tensor_tensor(lg[:], lg[:], red[:].unsqueeze(2).to_broadcast([R, G, ER]), ALU.subtract)
                        dve.drain().then_inc(exp_in, 1)
                        dve.wait_ge(exp_out, ig)
                        dve.tensor_reduce(red[:], pr[:], AX.X, ALU.add)
                        dve.drain()
                        dve.reciprocal(red[:], red[:])
                        dve.drain()
                        dve.tensor_tensor(pr[:], pr[:], red[:].unsqueeze(2).to_broadcast([R, G, ER]), ALU.mult)
                        dve.drain()
                        topk_onehot(ta[:], pr[:], red)
                        dve.scalar_tensor_tensor(lg[:], ta[:], -2.0, pr[:], ALU.mult, ALU.add)
                        dve.drain()
                        topk_onehot(tb[:], lg[:], red)
                        dve.tensor_tensor(ta[:], ta[:], tb[:], ALU.add)
                        dve.drain()
                        dve.tensor_tensor(cw[:, :, 0:ER], ta[:], pr[:], ALU.mult)
                        dve.drain().then_inc(cw_ready, 1)
                        dve.wait_ge(cwT_full, ig)
                        dve.tensor_copy(cwT[:], wide[0:ER + 2, 0:GR])
                        dve.drain().then_inc(cwT_ready, 1)
                        dve.wait_ge(hfree, (ig - 1) * HC + HC + 2)
                        for c in range(ER // 2):
                            dve.wait_ge(wfull, (ig - 1) * (ER // 2) + c + 1)
                            hc = HC - ER // 2 + c
                            dve.tensor_tensor(hid[:, hc, :], spreads[c % 2][:, 0:GR], hid[:, hc, :], ALU.mult).then_inc(wfree, 1)
                        dve.drain().then_inc(hid_ready, 1)
                    if more:
                        dve.wait_ge(x_in[w], (i + 1 + u) * 16)
                        norm(w)
                    if b:
                        for g in range(G):
                            dve.wait_ge(afull, mb + g + 1)
                            dve.tensor_tensor(x1[w][:, g, :], acc[g % 2][0:R, :], x1[w][:, g, :], ALU.add).then_inc(afree, 1)
                        dve.drain().then_inc(x2_ready, 1)
                        dve.wait_ge(h2_free, ig)
                        layernorm(dve, h2n, x1[w], G, stats, mv, rstd, var, tmp)
                        dve.drain().then_inc(h2_ready, 1)

                dve.wait_ge(a_in[0], 16)
                dve.wait_ge(o_in[0], 16)
                mean(0)
                dve.wait_ge(x_in[0], 16)
                norm(0)
                steps(dve, step)


NL = E4 + 2 * H


def second_gnn(nc, K, h2, tables, x2, w, x3, h3T, logits):
    with ExitStack() as ctx:
        P = Pools(nc, ctx, "d")
        w1, w2 = P.sb("w1", [128, KC, D]), P.sb("w2", [128, KC, D])
        wl = P.sb("wl", [128, KC, NL])
        b1, b2 = P.sb("b1", [128, KC]), P.sb("b2", [R, D])
        hin = [P.sb(f"hin{u}", [R, G, D]) for u in range(2)]
        xin = [P.sb(f"xin{u}", [R, G, D]) for u in range(2)]
        agg, odd, h3n = P.sb("agg", [R, G, D]), P.sb("odd", [R, G, D]), P.sb("h3n", [R, G, D])
        featA, hid = P.sb("featA", [128, KC, GR]), P.sb("hid", [128, KC, GR])
        featB = [P.sb(f"featB{u}", [128, KC, GR]) for u in range(2)]
        stats, mv = P.sb("stats", [R, G, 6]), P.sb("mv", [R, G, 2])
        rstd, var, tmp = P.sb("rstd", [R, G]), P.sb("var", [R, G]), P.sb("tmp", [R, G])
        turned = [P.ps(f"turned{u}", [128, 512]) for u in range(2)]
        acc = [P.ps(f"acc{u}", [128, 512]) for u in range(2)]
        up = [P.ps(f"up{u}", [128, 512]) for u in range(2)]
        small = P.ps("small", [128, 512])
        wld, wready = P.sem("wld"), P.sem("wready")
        h_in, x_in, a_in, o_in = P.sems("h_in"), P.sems("x_in"), P.sem("a_in"), P.sem("o_in")
        fb_free = P.sem("fb_free")
        s_ready, h3_ready = P.sem("s_ready"), P.sem("h3_ready")
        tfull, tfree, afull, afree = P.sem("tfull"), P.sem("tfree"), P.sem("afull"), P.sem("afree")
        hfull, hfree = P.sem("hfull"), P.sem("hfree")
        lfull, lfree = P.sem("lfull"), P.sem("lfree")
        x3_ready = P.sem("x3_ready")
        x3_out, fb_out = P.sems("x3_out"), P.sems("fb_out")
        hrows, xrows, x3rows = (a.rearrange("(n r) d -> r n d", r=R) for a in (h2, x2, x3))
        trows = [t[0:N, :].rearrange("(n r) d -> r n d", r=R) for t in tables]
        NB = NG // 2

        def steps(eng, step):
            step(0, 0, True, False, True)
            step(0, 1, True, True, True)
            with eng.Fori(0, NB - 2) as i:
                for u in range(2):
                    step(i + 1, u, True, True, True)
            step(NB - 1, 0, True, True, True)
            step(NB - 1, 1, True, True, False)
            step(NB, 0, False, True, False)

        def bases(ig, a, b):
            if a and not b:
                return 0, 0
            return ig * 2 * KC - KC, ig * 2 * KC - KC + (KC if a else 0)

        with nc.Block() as block:
            @block.sync
            def _(sp):
                loads = [(w1, w["n1"].rearrange("(k p) n -> p k n", p=128)), (w2, w["n2"].rearrange("(k p) n -> p k n", p=128)),
                         (wl, w["wl"].rearrange("(k p) n -> p k n", p=128)), (b1, w["nb1"]), (b2, w["nb2"].to_broadcast([R, D]))]
                for t, a in loads:
                    sp.dma_start(t[:], a).then_inc(wld, 16)
                sp.wait_ge(wld, 16 * len(loads))
                sp.nop().then_inc(wready, 1)

                def load_h(ig, u):
                    sp.dma_start(hin[u][:], hrows[:, bass.ds(ig * G, G), :]).then_inc(h_in[u], 16)

                def load_x(ig, u):
                    sp.dma_start(xin[u][:], xrows[:, bass.ds(ig * G, G), :]).then_inc(x_in[u], 16)

                def load_agg(ig):
                    sp.dma_start(agg[:], trows[0][:, bass.ds(ig * G, G), :]).then_inc(a_in, 16)
                    sp.dma_start(odd[:], trows[1][:, bass.ds(ig * G, G), :]).then_inc(o_in, 16)

                def step(i, u, a, b, next_x, ahead):
                    ig, w = i * 2 + u, 1 - u
                    ta, tb = bases(ig, a, b)
                    if next_x:
                        hold(sp, K, x3_out[w], (i + u) * 16)
                        hold(sp, K, h3_ready, ig)
                        load_x(ig + 1, w)
                    if ahead:
                        hold(sp, K, tfull, ta + KC)
                        load_h(ig + 2, u)
                        hold(sp, K, s_ready, ig + 2)
                        load_agg(ig + 2)
                    if b:
                        sp.wait_ge(tfree, tb + KC + 2)
                        sp.dma_start(h3T[bass.ds(ig - 1, 1), :, :].rearrange("a p n -> p (a n)"), featB[w][:].rearrange("p k n -> p (k n)")).then_inc(fb_out[w], 16)
                    if a:
                        sp.wait_ge(x3_ready, ig + 1)
                        sp.dma_start(x3rows[:, bass.ds(ig * G, G), :], xin[u][:]).then_inc(x3_out[u], 16)
                    if b:
                        sp.wait_ge(fb_out[w], (i + u) * 16)
                        sp.nop().then_inc(fb_free, 1)

                load_agg(0)
                for u in range(2):
                    load_h(u, u)
                    load_x(u, u)
                sp.wait_ge(s_ready, 1)
                load_agg(1)
                step(0, 0, True, False, False, True)
                step(0, 1, True, True, True, True)
                with sp.Fori(0, NB - 2) as i:
                    for u in range(2):
                        step(i + 1, u, True, True, True, True)
                step(NB - 1, 0, True, True, True, False)
                step(NB - 1, 1, True, True, False, False)
                step(NB, 0, False, True, False, False)
                for u in range(2):
                    sp.wait_ge(x3_out[u], NB * 16)

            @block.tensor
            def _(pe):
                pe.wait_ge(wready, 1)

                def turn(ti, j, srcs):
                    for k in range(KC):
                        n = j * KC + k
                        pe.wait_ge(tfree, ti + n + 1)
                        for g in range(G):
                            m = pe.transpose(turned[n % 2][:, g * R:(g + 1) * R], srcs[:, g, k * 128:(k + 1) * 128], K.ident[0:R, 0:R])
                        m.then_inc(tfull, 1)

                def step(i, u, a, b, more):
                    ig = i * 2 + u
                    ta, tb = bases(ig, a, b)
                    if a:
                        pe.wait_ge(s_ready, ig + 1)
                        turn(ta, 0, hin[u])
                        pe.wait_ge(tfree, ta + KC + 2)
                        for c in range(KC):
                            pe.wait_ge(hfree, ig * KC + c + 1)
                            for k in range(KC):
                                m = pe.matmul(up[c % 2][:, 0:GR], w1[:, k, c * 128:(c + 1) * 128], featA[:, k, :], start=(k == 0), stop=(k == KC - 1))
                            m.then_inc(hfull, 1)
                    if b:
                        pe.wait_ge(h3_ready, ig)
                        turn(tb, 0, h3n)
                        pe.wait_ge(tfree, tb + KC + 2)
                        pe.wait_ge(lfree, ig)
                        for g in range(G):
                            for k in range(KC):
                                m = pe.matmul(small[0:R, g * NL:(g + 1) * NL], featB[1 - u][:, k, g * R:(g + 1) * R], wl[:, k, :], start=(k == 0), stop=(k == KC - 1))
                        m.then_inc(lfull, 1)
                    if a:
                        pe.wait_ge(hfree, ig * KC + KC + 2)
                        for g in range(G):
                            pe.wait_ge(afree, ig * G + g + 1)
                            for k in range(KC):
                                m = pe.matmul(acc[g % 2][0:R, :], hid[:, k, g * R:(g + 1) * R], w2[:, k, :], start=(k == 0), stop=(k == KC - 1))
                            m.then_inc(afull, 1)
                steps(pe, step)

            @block.scalar
            def _(act):
                act.wait_ge(wready, 1)

                def evict(base, j, dst):
                    for k in range(KC):
                        n = j * KC + k
                        act.wait_ge(tfull, base + n + 1)
                        act.activation(dst[:, k, :], turned[n % 2][:, 0:GR], ACT.Copy).then_inc(tfree, 1)

                def step(i, u, a, b, more):
                    ig = i * 2 + u
                    ta, tb = bases(ig, a, b)
                    if a:
                        evict(ta, 0, featA)
                        for c in range(KC):
                            act.wait_ge(hfull, ig * KC + c + 1)
                            act.activation(hid[:, c, :], up[c % 2][:, 0:GR], ACT.Relu, bias=b1[:, c:c + 1]).then_inc(hfree, 1)
                    if b:
                        act.wait_ge(fb_free, ig)
                        evict(tb, 0, featB[1 - u])
                steps(act, step)

            @block.vector
            def _(dve):
                dve.wait_ge(wready, 1)
                for s, n in ((tfree, 2), (afree, 2), (hfree, 2), (lfree, 1), (fb_free, 2)):
                    dve.drain().then_inc(s, n)
                def take(ig, i, u):
                    dve.wait_ge(h_in[u], (i + 1) * 16)
                    dve.wait_ge(a_in, (ig + 1) * 16)
                    dve.wait_ge(o_in, (ig + 1) * 16)
                    for g in range(G):
                        dve.tensor_tensor(agg[:, g, :], agg[:, g, :], odd[:, g, :], ALU.add)
                    dve.drain()
                    for g in range(G):
                        dve.tensor_tensor(hin[u][:, g, :], hin[u][:, g, :], agg[:, g, :], ALU.add)
                    dve.drain().then_inc(s_ready, 1)

                def step(i, u, a, b, more):
                    ig, w = i * 2 + u, 1 - u
                    if b:
                        layernorm(dve, h3n, xin[w], G, stats, mv, rstd, var, tmp)
                        dve.drain().then_inc(h3_ready, 1)
                    if more:
                        take(ig + 1, i + u, w)
                    if a:
                        dve.wait_ge(x_in[u], (i + 1) * 16)
                        for g in range(G):
                            dve.tensor_tensor(xin[u][:, g, :], xin[u][:, g, :], b2[:], ALU.add)
                        dve.drain()
                    if b:
                        dve.wait_ge(lfull, ig)
                        dve.tensor_copy(logits[:, bass.ds(ig * G - G, G), :], small[0:R, 0:G * NL].rearrange("p (g e) -> p g e", g=G)).then_inc(lfree, 1)
                    if a:
                        for g in range(G):
                            dve.wait_ge(afull, ig * G + g + 1)
                            dve.tensor_tensor(xin[u][:, g, :], acc[g % 2][0:R, :], xin[u][:, g, :], ALU.add).then_inc(afree, 1)
                        dve.drain().then_inc(x3_ready, 1)
                take(0, 0, 0)
                steps(dve, step)


def route(nc, K, logits, w, weights, pos, beta, decay, keep):
    S = [R, T, E4]
    with ExitStack() as ctx:
        P = Pools(nc, ctx, "r")
        p, e1, e2, m, desc, allpos = (P.sb(n, S) for n in ("p", "e1", "e2", "m", "desc", "allpos"))
        desci = P.sb("desci", S, I32)
        red, w1, w2, any2, at1, at2 = (P.sb(n, [R, T]) for n in ("red", "w1", "w2", "any2", "at1", "at2"))
        tot, run = P.sb("tot", [128, E4, T]), P.sb("run", [128, E4, T])
        onesT = P.sb("onesT", [128, T])
        cnt, cnti, start = P.sb("cnt", [128, E4]), P.sb("cnti", [128, E4], I32), P.sb("start", [128, E4])
        SB = [R, T, H]
        y, z, z2, s, den = (P.sb(n, SB) for n in ("y", "z", "z2", "s", "den"))
        dtb, alog = P.sb("dtb", [R, H]), P.sb("alog", [R, H])
        chunki, chunk, hit = P.sb("chunki", [128, NCH + 1], I32), P.sb("chunk", [128, NCH + 1]), P.sb("hit", [128, NCH + 1])
        dumpno = P.sb("dumpno", [128, 1])
        dumpi = P.sb("dumpi", [128, 1], I32)
        before, total = P.ps("before", [R, T * E4]), P.ps("total", [128, T * E4])
        made, ld, a_go, a_done, g_go, g_done, pre = (P.sem(n) for n in ("made", "ld", "a_go", "a_done", "g_go", "g_done", "pre"))
        bc = lambda a: a.unsqueeze(2).to_broadcast(S)
        bh = lambda a: a.unsqueeze(1).to_broadcast(SB)
        with nc.Block() as block:
            @block.sync
            def _(sp):
                sp.dma_start(dtb[:], w["dtb"].to_broadcast([R, H])).then_inc(ld, 16)
                sp.dma_start(alog[:], w["alog"].to_broadcast([R, H])).then_inc(ld, 16)

            @block.gpsimd
            def _(pool):
                pool.iota(desci[:], pattern=[[0, T], [-1, E4]], base=E4, channel_multiplier=0)
                pool.iota(chunki[:], pattern=[[CH, NCH + 1]], base=0, channel_multiplier=0)
                pool.iota(dumpi[:], pattern=[[0, 1]], base=NP, channel_multiplier=1)
                pool.drain()
                pool.tensor_copy(desc[:], desci[:])
                pool.tensor_copy(chunk[:], chunki[:])
                pool.tensor_copy(dumpno[:], dumpi[:]).then_inc(made, 1)

            @block.scalar
            def _(act):
                act.wait_ge(a_go, 1)
                act.activation(p[:], p[:], ACT.Exp).then_inc(a_done, 1)
                act.wait_ge(a_go, 2)
                act.activation(z[:], z[:], ACT.Exp)
                act.activation(alog[:], alog[:], ACT.Exp).then_inc(a_done, 1)
                act.wait_ge(a_go, 3)
                act.activation(beta[:], beta[:], ACT.Sigmoid).then_inc(a_done, 1)

            @block.tensor
            def _(pe):
                pe.wait_ge(g_go, 1)
                mm = m[:].rearrange("p t e -> p (t e)")
                pe.matmul(before[:], K.before[0:R, 0:R], mm, start=True, stop=True)
                pe.matmul(total[:], K.ones[0:R, 0:128], mm, start=True, stop=True).then_inc(g_done, 1)

            @block.vector
            def _(dve):
                d = dve.drain

                def first_largest(dst, src):
                    dve.tensor_reduce(red[:], src, AX.X, ALU.max); d()
                    dve.tensor_tensor(dst, src, bc(red[:]), ALU.is_equal); d()
                    dve.tensor_tensor(dst, dst, desc[:], ALU.mult); d()
                    dve.tensor_reduce(red[:], dst, AX.X, ALU.max); d()
                    dve.tensor_tensor(dst, desc[:], bc(red[:]), ALU.is_equal); d()

                def weigh(dst, onehot, vals):
                    dve.tensor_tensor(m[:], onehot, vals, ALU.mult); d()
                    dve.tensor_reduce(dst, m[:], AX.X, ALU.add); d()

                dve.wait_ge(made, 1)
                dve.wait_ge(ld, 32)
                dve.tensor_reduce(red[:], logits[:, :, 0:E4], AX.X, ALU.max); d()
                dve.tensor_tensor(p[:], logits[:, :, 0:E4], bc(red[:]), ALU.subtract)
                d().then_inc(a_go, 1)
                dve.tensor_tensor(y[:], logits[:, :, E4 + H:NL], bh(dtb[:]), ALU.add); d()
                dve.tensor_scalar(z[:], y[:], -1.0, None, ALU.mult); d()
                dve.tensor_tensor(z[:], z[:], y[:], ALU.min)
                d().then_inc(a_go, 1)
                dve.tensor_copy(beta[:], logits[:, :, E4:E4 + H])
                d().then_inc(a_go, 1)
                dve.wait_ge(a_done, 1)
                dve.tensor_reduce(red[:], p[:], AX.X, ALU.add); d()
                dve.reciprocal(red[:], red[:]); d()
                dve.tensor_tensor(p[:], p[:], bc(red[:]), ALU.mult); d()
                first_largest(e1[:], p[:])
                weigh(w1[:], e1[:], p[:])
                dve.scalar_tensor_tensor(allpos[:], e1[:], -2.0, p[:], ALU.mult, ALU.add); d()
                first_largest(e2[:], allpos[:])
                weigh(w2[:], e2[:], p[:])
                dve.tensor_tensor(red[:], w1[:], w2[:], ALU.add); d()
                dve.reciprocal(red[:], red[:]); d()
                dve.tensor_tensor(weights[:, 0, :], w1[:], red[:], ALU.mult)
                dve.tensor_tensor(weights[:, 1, :], w2[:], red[:], ALU.mult); d()
                dve.tensor_scalar(any2[:], weights[:, 1, :], 0.0, None, ALU.is_gt); d()
                dve.tensor_tensor(e2[:], e2[:], bc(any2[:]), ALU.mult); d()
                dve.tensor_tensor(m[:], e1[:], e2[:], ALU.add)
                d().then_inc(g_go, 1)
                dve.wait_ge(g_done, 1)
                dve.tensor_copy(tot[:], total[:].rearrange("p (t e) -> p e t", e=E4))
                dve.memset(onesT[:], 1.0); d()
                for e in range(E4):
                    dve.tensor_tensor_scan(run[:, e, :], onesT[:], tot[:, e, :], 0.0, ALU.mult, ALU.add)
                d()
                dve.tensor_copy(cnt[:], run[:, :, T - 1]); d()
                dve.tensor_tensor(run[:], run[:], tot[:], ALU.subtract)
                dve.tensor_scalar(cnti[:], cnt[:], float(CH - 1), None, ALU.add); d()
                dve.tensor_scalar(cnti[:], cnti[:], 7, 7, ALU.arith_shift_right, ALU.arith_shift_left); d()
                dve.tensor_copy(cnt[:], cnti[:])
                dve.memset(start[:], 0.0); d()
                for e in range(1, E4):
                    dve.tensor_tensor(start[:, e:e + 1], start[:, e - 1:e], cnt[:, e - 1:e], ALU.add); d()
                dve.tensor_tensor(allpos[:], before[:].rearrange("p (t e) -> p t e", e=E4), run[0:R].rearrange("p e t -> p t e"), ALU.add); d()
                dve.tensor_tensor(allpos[:], allpos[:], start[0:R, :].unsqueeze(1).to_broadcast(S), ALU.add); d()
                weigh(at1[:], e1[:], allpos[:])
                weigh(at2[:], e2[:], allpos[:])
                dve.tensor_copy(pos[:, 0, :], at1[:])
                dve.tensor_scalar(any2[:], any2[:], -1.0, 1.0, ALU.mult, ALU.add); d()
                dve.tensor_tensor(any2[:], any2[:], dumpno[0:R, 0:1].to_broadcast([R, T]), ALU.mult); d()
                dve.tensor_tensor(pos[:, 1, :], at2[:], any2[:], ALU.add)
                dve.wait_ge(a_done, 2)
                dve.tensor_scalar(den[:], z[:], 2.0, None, ALU.add); d()
                dve.reciprocal(den[:], den[:]); d()
                dve.tensor_tensor(s[:], z[:], den[:], ALU.mult); d()
                dve.tensor_tensor(z2[:], s[:], s[:], ALU.mult); d()
                dve.tensor_scalar(den[:], z2[:], 1.0 / 17, 1.0 / 15, ALU.mult, ALU.add); d()
                for n in (13, 11, 9, 7, 5, 3, 1):
                    dve.tensor_tensor(den[:], den[:], z2[:], ALU.mult); d()
                    dve.tensor_scalar(den[:], den[:], 1.0 / n, None, ALU.add); d()
                dve.tensor_tensor(den[:], den[:], s[:], ALU.mult); d()
                dve.tensor_scalar(y[:], y[:], 0.0, None, ALU.max); d()
                dve.scalar_tensor_tensor(den[:], den[:], 2.0, y[:], ALU.mult, ALU.add); d()
                dve.tensor_tensor(den[:], den[:], bh(alog[:]), ALU.mult); d()
                dve.tensor_scalar(decay[:], den[:], -1.0, -3.0e38, ALU.mult, ALU.max)
                dve.wait_ge(a_done, 3)
                dve.memset(keep[:], 1.0); d()
                for e in range(E4):
                    dve.tensor_scalar(hit[:], chunk[:], start[:, e:e + 1], None, ALU.not_equal); d()
                    dve.tensor_tensor(keep[:], keep[:], hit[:], ALU.mult); d()


CG = 32


def project(nc, K, h3T, w, pos, beta, decay, rows):
    QK = 2 * D
    NR = 4
    with ExitStack() as ctx:
        P = Pools(nc, ctx, "e")
        wt = P.sb("w", [128, 3, KC, D])
        feat = [P.sb(f"feat{u}", [128, KC, GR]) for u in range(2)]
        row = [P.sb(f"row{v}", [R, ROW]) for v in range(NR)]
        ix = [[P.sb(f"ix{v}{s}", [R, 1], I32) for s in range(2)] for v in range(NR)]
        sq = P.sb("sq", [R, QK])
        ss, inv, tmp = P.sb("ss", [R, 2 * H]), P.sb("inv", [R, 2 * H]), P.sb("tmp", [R, 2 * H])
        proj = [[P.ps(f"proj{v}{j}", [R, 512]) for j in range(3)] for v in range(2)]
        wld = P.sem("wld")
        f_in, f_used = P.sems("f_in"), P.sem("f_used")
        pfull, silu, row_ready, row_free = P.sem("pfull"), P.sem("silu"), P.sem("row_ready"), P.sem("row_free")
        sent = [[P.sem(f"sent{v}{s}") for s in range(2)] for v in range(NR)]
        NB = NG // 2
        with nc.Block() as block:
            @block.sync
            def _(sp):
                for j, n in enumerate(("wk", "wq", "wv")):
                    sp.dma_start(wt[:, j], w[n].rearrange("(k p) n -> p k n", p=128)).then_inc(wld, 16)

                def load(ig, u):
                    sp.dma_start(feat[u][:].rearrange("p k n -> p (k n)"), h3T[bass.ds(ig, 1), :, :].rearrange("a p n -> p (a n)")).then_inc(f_in[u], 16)
                load(0, 0)
                load(1, 1)
                with sp.Fori(0, NB - 1) as i:
                    for u in range(2):
                        sp.wait_ge(f_used, i * 2 + u + 1)
                        load(i * 2 + u + 2, u)

            @block.tensor
            def _(pe):
                pe.wait_ge(wld, 48)
                with pe.Fori(0, NB) as i:
                    for u in range(2):
                        pe.wait_ge(f_in[u], (i + 1) * 16)
                        for g in range(G):
                            t = (i * 2 + u) * G + g
                            pe.wait_ge(silu, t + 1)
                            for j in range(3):
                                for k in range(KC):
                                    m = pe.matmul(proj[g % 2][j][:], feat[u][:, k, g * R:(g + 1) * R], wt[:, j, k, :], start=(k == 0), stop=(k == KC - 1))
                            m.then_inc(pfull, 1)

            @block.scalar
            def _(act):
                with act.Fori(0, NB) as i:
                    for u in range(2):
                        for g in range(G):
                            t = (i * 2 + u) * G + g
                            act.wait_ge(row_free, t + 1)
                            act.wait_ge(pfull, t + 1)
                            for j, at in enumerate((0, D, V)):
                                m = act.activation(row[g][:, at:at + D], proj[g % 2][j][:], ACT.Silu)
                            m.then_inc(silu, 1)
                        act.drain().then_inc(f_used, 1)

            @block.gpsimd
            def _(pool):
                def send(i, v, g):
                    for s in range(2):
                        hold(pool, K, row_ready, i + 1)
                        pool.indirect_dma_start(rows, bass.IndirectOffsetOnAxis(ap=ix[v][s][:, 0:1], axis=0), row[v][:], None,
                                                bounds_check=NP + 127, oob_is_err=True).then_inc(sent[v][s], 16)

                def land(j, v):
                    for s in range(2):
                        hold(pool, K, sent[v][s], (j + 1) * 16)
                    pool.nop().then_inc(row_free, 1)

                for g in range(2):
                    send(g, g, g)
                with pool.Fori(0, T // G - 1) as i:
                    for g in range(G):
                        send(i * G + g + 2, (g + 2) % NR, g)
                        land(i, g)
                for g in range(2):
                    send(T - 2 + g, (g + 2) % NR, g)
                for g in range(G):
                    land(T // G - 1, g)

            @block.vector
            def _(dve):
                dve.drain().then_inc(row_free, NR)
                dve.drain().then_inc(silu, 2)
                with dve.Fori(0, T // G) as i:
                    for g in range(G):
                        t = i * G + g
                        dve.wait_ge(silu, t + 3)
                        rw = row[g]
                        dve.tensor_tensor(sq[:], rw[:, 0:QK], rw[:, 0:QK], ALU.mult)
                        dve.tensor_copy(rw[:, BETA:BETA + H], beta[:, bass.ds(t, 1), :].rearrange("p a h -> p (a h)"))
                        dve.tensor_copy(rw[:, DECAY:DECAY + H], decay[:, bass.ds(t, 1), :].rearrange("p a h -> p (a h)"))
                        for s in range(2):
                            dve.tensor_copy(ix[g][s][:], pos[:, s, bass.ds(t, 1)])
                        dve.drain()
                        dve.tensor_reduce(ss[:], sq[:].rearrange("p (h d) -> p h d", d=DK), AX.X, ALU.add)
                        dve.drain()
                        dve.tensor_scalar(ss[:], ss[:], 1e-6, None, ALU.add)
                        dve.drain()
                        rsqrt(dve, inv[:], ss[:], tmp[:])
                        dve.tensor_scalar(inv[:, H:2 * H], inv[:, H:2 * H], float(DK) ** -0.5, None, ALU.mult)
                        dve.drain()
                        v = rw[:, 0:QK].rearrange("p (h d) -> p h d", d=DK)
                        dve.tensor_tensor(v, v, inv[:].unsqueeze(2).to_broadcast([R, 2 * H, DK]), ALU.mult)
                        dve.drain().then_inc(row_ready, 1)


def chunk_products(nc, K, rows, ap, aq, diag):
    JB = 4
    with ExitStack() as ctx:
        P = Pools(nc, ctx, "f")
        comp = [P.sb(f"comp{j}", [128, CKQ]) for j in range(JB)]
        kb = [P.sb(f"kb{u}", [128, D]) for u in range(2)]
        kT = [P.sb(f"kT{u}", [128, 4, 128]) for u in range(2)]
        bq = [P.sb(f"bq{u}", [128, 4, 2, 128]) for u in range(2)]
        gu = [P.sb(f"gu{u}", [128, H, 128]) for u in range(2)]
        dec = [P.sb(f"dec{u}", [128, H, 128]) for u in range(2)]
        prod = [P.sb(f"prod{u}", [128, 2, H, 128]) for u in range(2)]
        blk = [P.sb(f"blk{u}", [128, H, 32]) for u in range(2)]
        turned = [P.ps(f"turned{u}", [128, 512]) for u in range(2)]
        dsum = [P.ps(f"dsum{u}", [128, 512]) for u in range(2)]
        kq = [P.ps(f"kq{u}", [128, 2, 2, 128]) for u in range(4)]
        c_in = P.sems("c_in", JB)
        kb_ready, gu_ready = P.sem("kb_ready"), P.sem("gu_ready")
        tfull, tfree, dfull, dec_ready, dec_cut, dec_free = (P.sem(n) for n in ("tfull", "tfree", "dfull", "dec_ready", "dec_cut", "dec_free"))
        kfull, kfree, p_ready = (P.sem(n) for n in ("kfull", "kfree", "p_ready"))
        out_free, cut, taken = P.sem("out_free"), P.sem("cut"), P.sem("taken")
        p_out, b_out = [P.sems(f"p_out{u}_") for u in range(2)], P.sems("b_out")
        NB = NCH // JB

        def steps(eng, step):
            for j in range(JB):
                step(0, j, True, j >= 1, j >= 2)
            with eng.Fori(0, NB - 1) as i:
                for j in range(JB):
                    step(i + 1, j, True, True, True)
            step(NB, 0, False, True, True)
            step(NB, 1, False, False, True)

        with nc.Block() as block:
            @block.sync
            def _(sp):
                def load(c, j):
                    sp.dma_start(comp[j][:], rows[bass.ds(c * CH, CH), 0:CKQ]).then_inc(c_in[j], 16)

                def leave(c, u):
                    sp.wait_ge(cut, c + 1)
                    sp.dma_start(diag[bass.ds(c, 1), :, :].rearrange("a p n -> p (a n)"), blk[u][:].rearrange("p h i -> p (h i)")).then_inc(b_out[u], 16)
                    for a, n in ((ap, 0), (aq, 1)):
                        sp.dma_start(a[bass.ds(c, 1), :, :].rearrange("a p n -> p (a n)"), prod[u][:, n].rearrange("p h i -> p (h i)")).then_inc(p_out[u][n], 16)

                def left(u, n):
                    sp.wait_ge(b_out[u], n * 16)
                    for half in p_out[u]:
                        sp.wait_ge(half, n * 16)
                    sp.nop().then_inc(out_free, 1)

                def step(i, j, more, e=True, old=True):
                    c = i * JB + j
                    if more:
                        hold(sp, K, tfull, c * 3 + 6)
                        hold(sp, K, dfull, c + 3)
                        load(c + JB, j)
                    if old:
                        left(1 - j % 2, i * (JB // 2) + (j - 1) // 2)
                    if e:
                        leave(c - 2, j % 2)

                for j in range(JB):
                    load(j, j)
                for j in range(JB):
                    step(0, j, True, j >= 2, j >= 3)
                with sp.Fori(0, NB - 2) as i:
                    for j in range(JB):
                        step(i + 1, j, True)
                for j in range(JB):
                    step(NB - 1, j, False)
                step(NB, 0, False)
                step(NB, 1, False)
                left(1, NCH // 2)

            @block.gpsimd
            def _(pool):
                def step(i, j, a, b, e):
                    c, u = i * JB + j, j % 2
                    if a:
                        hold(pool, K, dec_ready, c + 2)
                        pool.affine_select(out=dec[u][:], in_=dec[u][:], compare_op=ALU.is_ge, fill=0.0, base=0,
                                           pattern=[[0, H], [1, 128]], channel_multiplier=-1).then_inc(dec_cut, 1)
                        pool.drain()
                    if e:
                        hold(pool, K, taken, c - 1)
                        for q in range(4):
                            s = slice(32 * q, 32 * q + 32)
                            pool.memset(prod[u][s, 0, :, s], 0.0)
                        pool.drain().then_inc(cut, 1)
                steps(pool, step)

            @block.tensor
            def _(pe):
                def step(i, j, a, b, e):
                    c, u = i * JB + j, j % 2

                    def turn(n, src):
                        pe.wait_ge(tfree, c * 3 + n + 1)
                        for p in range(4):
                            m = pe.transpose(turned[(u + n) % 2][:, p * 128:(p + 1) * 128], src[:, p * 128:(p + 1) * 128], K.ident[:])
                        m.then_inc(tfull, 1)

                    if a:
                        pe.wait_ge(c_in[j], (i + 1) * 16)
                        turn(0, comp[j][:, 0:D])
                        turn(1, comp[j][:, D:2 * D])
                        pe.wait_ge(kb_ready, c + 1)
                        turn(2, kb[u][:])
                        pe.wait_ge(gu_ready, c + 1)
                        pe.wait_ge(dec_ready, c + 1)
                        for n in range(2):
                            m = pe.matmul(dsum[n][:], K.later[:], gu[u][:, 4 * n:4 * n + 4, :].rearrange("p h i -> p (h i)"), start=True, stop=True)
                        m.then_inc(dfull, 1)
                    if b:
                        pe.wait_ge(tfree, c * 3 + 2)
                        for p in range(4):
                            if p % 2 == 0:
                                pe.wait_ge(kfree, c * 4 - 2 + 2 * (p // 2))
                            for hh in range(2):
                                s = slice(64 * hh, 64 * hh + 64)
                                m = pe.matmul(kq[p // 2 * 2 + hh][:, p % 2].rearrange("p s i -> p (s i)"), kT[1 - u][s, p, :],
                                              bq[1 - u][s, p].rearrange("p s i -> p (s i)"), start=True, stop=True)
                            if p % 2:
                                m.then_inc(kfull, 2)
                steps(pe, step)

            @block.scalar
            def _(act):
                def step(i, j, a, b, e):
                    c, u = i * JB + j, j % 2
                    if a:
                        act.wait_ge(kfull, c * 4 + 4)
                        for n, dst in ((0, kT[u][:]), (1, bq[u][:, :, 1, :]), (2, bq[u][:, :, 0, :])):
                            act.wait_ge(tfull, c * 3 + n + 4)
                            act.activation(dst, turned[(u + n) % 2][:].rearrange("p (a b) -> p a b", a=4), ACT.Copy).then_inc(tfree, 1)
                        act.wait_ge(dec_free, c + 1)
                        act.wait_ge(dfull, c + 3)
                        for n in range(2):
                            m = act.activation(dec[u][:, 4 * n:4 * n + 4, :], dsum[n][:].rearrange("p (h i) -> p h i", h=4), ACT.Exp)
                        m.then_inc(dec_ready, 1)
                    if e:
                        act.wait_ge(p_ready, c - 1)
                        for q in range(4):
                            s = slice(32 * q, 32 * q + 32)
                            m = act.activation(blk[u][s], prod[u][s, 0, :, s], ACT.Copy)
                        m.then_inc(taken, 1)
                steps(act, step)

            @block.vector
            def _(dve):
                for s, n in ((tfree, 2), (tfull, 3), (kfree, 4), (kfull, 8), (dfull, 2), (out_free, 2), (dec_ready, 1), (dec_free, 2)):
                    dve.drain().then_inc(s, n)

                def prepare(i, j, c):
                    u = j % 2
                    dve.wait_ge(c_in[j], (i + 1) * 16)
                    dve.wait_ge(dfull, c + 1)
                    dve.tensor_tensor(kb[u][:].rearrange("p (h d) -> p h d", h=H), comp[j][:, 0:D].rearrange("p (h d) -> p h d", h=H),
                                      comp[j][:, BETA:BETA + H].unsqueeze(2).to_broadcast([128, H, DK]), ALU.mult).then_inc(kb_ready, 1)
                    dve.tensor_tensor(gu[u][:], K.upto[:].unsqueeze(1).to_broadcast([128, H, 128]),
                                      comp[j][:, DECAY:DECAY + H].unsqueeze(2).to_broadcast([128, H, 128]), ALU.mult).then_inc(gu_ready, 1)

                def step(i, j, b, more):
                    c, u = i * JB + j, j % 2
                    if more:
                        if j + 1 < JB:
                            prepare(i, j + 1, c + 1)
                        else:
                            prepare(i + 1, 0, c + 1)
                    if b:
                        dve.wait_ge(dec_cut, c)
                        dve.wait_ge(out_free, c)
                        for p in range(4):
                            dve.wait_ge(kfull, c * 4 + 2 * (p // 2) + 6)
                            two = slice(4 * (p // 2) + p % 2, 4 * (p // 2) + p % 2 + 3, 2)
                            dve.tensor_tensor(prod[1 - u][:, :, two, :].rearrange("p s h i -> p h s i"), kq[p][:],
                                              dec[1 - u][:, two, :].unsqueeze(2).to_broadcast([128, 2, 2, 128]), ALU.mult).then_inc(kfree, 1)
                        dve.drain().then_inc(p_ready, 1)
                        dve.nop().then_inc(dec_free, 1)

                prepare(0, 0, 0)
                for j in range(JB):
                    step(0, j, j >= 1, True)
                with dve.Fori(0, NB - 2) as i:
                    for j in range(JB):
                        step(i + 1, j, True, True)
                for j in range(JB):
                    step(NB - 1, j, True, j < JB - 1)
                step(NB, 0, True, False)


def take_off(eng, B, r, tmp, h0, h1, m):
    n = h1 - h0
    shape = [128, m, n, 32 - m]
    t = tmp[:, 256 * h0:256 * h0 + m * n * (32 - m)].rearrange("p (j h i) -> p j h i", j=m, h=n)
    eng.tensor_tensor(t, B[:, 0:m, h0:h1, m:m + 1].to_broadcast(shape), r[:, m:m + 1, h0:h1, m:32].to_broadcast(shape), ALU.mult)
    eng.drain()
    eng.tensor_tensor(r[:, 0:m, h0:h1, m:32], r[:, 0:m, h0:h1, m:32], t, ALU.subtract)
    eng.drain()


def solve_first(nc, K, diag, inv):
    PH = 3
    with ExitStack() as ctx:
        P = Pools(nc, ctx, "s")
        b, r = P.sb("b", [128, 32, H, 32]), P.sb("r", [128, 32, H, 32])
        tmp = P.sb("tmp", [128, 16 * 16 * H])
        b_in, r_out, done, begun = P.sem("b_in"), P.sem("r_out"), P.sem("done"), P.sem("begun")
        with nc.Block() as block:
            @block.sync
            def _(sp):
                sp.dma_start(b[:].rearrange("p j h i -> p (j h i)"), grouped(diag)[0]).then_inc(b_in, 16)
                sp.wait_ge(done, 2)
                sp.dma_start(grouped(inv)[0], r[:].rearrange("p j h i -> p (j h i)")).then_inc(r_out, 16)
                sp.wait_ge(r_out, 16)

            @block.gpsimd
            def _(pool):
                unit(pool, r)
                pool.drain().then_inc(begun, 1)
                pool.wait_ge(b_in, 16)
                for m in range(31, 0, -1):
                    take_off(pool, b, r, tmp, H - PH, H, m)
                pool.drain().then_inc(done, 1)

            @block.vector
            def _(dve):
                dve.wait_ge(b_in, 16)
                dve.wait_ge(begun, 1)
                for m in range(31, 0, -1):
                    take_off(dve, b, r, tmp, 0, H - PH, m)
                dve.drain().then_inc(done, 1)


def grouped(a):
    return a.rearrange("(g c) (b j) n -> g (c b) (j n)", c=CG, b=4)


def unit(pool, r):
    pool.memset(r[:], 0.0)
    pool.drain()
    pool.affine_select(out=r[:], in_=r[:], compare_op=ALU.not_equal, fill=1.0, base=0,
                       pattern=[[1, 32], [0, H], [-1, 32]], channel_multiplier=0)


def recur(nc, K, rows, ap, aq, diag, inv, keep, orows):
    with ExitStack() as ctx:
        P = Pools(nc, ctx, "c")
        two = lambda name, shape: [P.sb(f"{name}{u}", shape) for u in range(2)]
        comp = two("comp", [128, ROW])
        np_, qk = two("np", [128, H, 128]), two("qk", [128, H, 128])
        tt = two("tt", [128, H, 32])
        td, tu = two("td", [128, H, 128]), two("tu", [128, H, 128])
        gam, gk = two("gam", [128, 3, H]), two("gk", [128, 4])
        bg = P.sb("bg", [128, H])
        X = two("X", [128, H, 128])
        kd, qg = two("kd", [128, H, DK]), two("qg", [128, H, DK])
        pt, ya, yb = P.sb("pt", [128, H, 128]), P.sb("ya", [128, H, 128]), P.sb("yb", [128, H, 128])
        uw = P.sb("uw", [128, 2, H, DK])
        wtn, qgT = P.sb("wtn", [128, 4, 128]), two("qgT", [128, 4, 128])
        U = P.sb("U", [128, H, DK])
        O = two("O", [128, D])
        S = two("S", [128, 4, 2, DK])
        sd = P.sb("sd", [128, 4, DK])
        blocks, inverse = P.sb("blocks", [128, 32, H, 32]), P.sb("inverse", [128, 32, H, 32])
        tmp = P.sb("tmp", [128, 16 * 16 * H])
        sets = [[P.ps(f"set{v}{j}", [128, 4, 128]) for j in range(2)] for v in range(2)]
        qw, ub, ob = P.ps("qw", [128, 4, 128]), P.ps("ub", [128, D]), P.ps("ob", [128, D])
        sg = P.ps("sg", [128, 4, 2, DK])
        c_in, p_in, q_in, t_in = P.sems("c_in"), P.sems("p_in"), P.sems("q_in"), P.sems("t_in")
        names = ("gfull", "gready", "pool_ready", "xv_ready", "tu_ready", "td_ready", "ptfull", "ptready", "yfull", "yready", "uwfull", "uwready",
                 "qfull", "qready", "wfull", "wready", "ufull", "uready", "ofull", "oready", "sfull", "sready", "o_free", "zeroed")
        (gfull, gready, pool_ready, xv_ready, tu_ready, td_ready, ptfull, ptready, yfull, yready, uwfull, uwready, qfull, qready, wfull, wready,
         ufull, uready, ofull, oready, sfull, sready, o_free, zeroed) = (P.sem(n) for n in names)
        o_out, dumped = P.sems("o_out"), P.sem("dumped")
        b_in, r_out, r_free, solved = (P.sem(n) for n in ("b_in", "r_out", "r_free", "solved"))
        NB = NCH // 2
        NGR, GB = NCH // CG, CG // 2
        parts = [(31, 30, 29), (28, 27)] + [(m,) for m in range(26, 5, -1)] + [(5, 4), (3, 2, 1)]
        half = [slice(0, 64), slice(64, 128)]
        flat = lambda a: a.rearrange("p h i -> p (h i)")
        line = lambda a: a.rearrange("a p n -> p (a n)")
        pair = lambda a, p: a[:, 2 * p:2 * p + 2, :].rearrange("p h d -> p (h d)")

        def bank(u, k, j):
            return sets[(u + k) % 2][j]

        def steps(eng, step):
            step(0, 0, True, False, False)
            step(0, 1, True, True, False)
            with eng.Fori(0, NB - 1) as i:
                for u in range(2):
                    step(i + 1, u, True, True, True)
            step(NB, 0, False, True, True)
            step(NB, 1, False, False, True)

        with nc.Block() as block:
            @block.sync
            def _(sp):
                def load_q(c, u):
                    sp.dma_start(flat(qk[u][:]), line(aq[bass.ds(c, 1), :, :])).then_inc(q_in[u], 16)

                def load(c, u):
                    sp.dma_start(comp[u][:], rows[bass.ds(c * CH, CH), :]).then_inc(c_in[u], 16)
                    sp.dma_start(flat(tt[u][:]), line(inv[bass.ds(c, 1), :, :])).then_inc(t_in[u], 16)
                    sp.dma_start(flat(np_[u][:]), line(ap[bass.ds(c, 1), :, :])).then_inc(p_in[u], 16)

                def step(i, u, a, b, more):
                    s = i * 2 + u
                    if b:
                        hold(sp, K, oready, s)
                        sp.dma_start(orows[bass.ds(s * CH - 2 * CH, CH), :], O[u][:]).then_inc(o_out[u], 16)
                        if a:
                            load_q(s, u)
                    if more:
                        hold(sp, K, qfull, s + 1)
                        hold(sp, K, xv_ready, s + 1)
                        hold(sp, K, td_ready, s + 1)
                        load(s + 2, u)
                    if b:
                        sp.wait_ge(o_out[u], i * 16)
                        sp.nop().then_inc(o_free, 1)

                sp.dma_start(orows[NP:NP + 128, :], K.zero[:, 0:D]).then_inc(dumped, 16)
                big = lambda x: x[:].rearrange("p j h i -> p (j h i)")
                sp.dma_start(big(blocks), grouped(diag)[1]).then_inc(b_in, 16)
                for u in range(2):
                    load(u, u)
                    load_q(u, u)
                for u in range(2):
                    step(0, u, True, False, True)
                for g in range(NGR):
                    lo = 1 if g == 0 else 0
                    with sp.Fori(0, GB - 2 - lo) as i:
                        for u in range(2):
                            step(i + (g * GB + lo), u, True, True, True)
                    if g + 1 < NGR:
                        sp.wait_ge(solved, g + 1)
                        sp.dma_start(grouped(inv)[g + 1], big(inverse)).then_inc(r_out, 16)
                        if g + 2 < NGR:
                            sp.dma_start(big(blocks), grouped(diag)[g + 2]).then_inc(b_in, 16)
                    for u in range(2):
                        step(g * GB + GB - 2, u, True, True, True)
                    if g + 1 < NGR:
                        sp.wait_ge(r_out, 16 * (g + 1))
                        sp.nop().then_inc(r_free, 1)
                    for u in range(2):
                        step(g * GB + GB - 1, u, True, True, g + 1 < NGR)
                for u in range(2):
                    step(NB, u, False, True, False)
                sp.wait_ge(dumped, 16)

            @block.gpsimd
            def _(pool):
                for u in range(2):
                    pool.memset(td[u][:], 0.0)
                    pool.memset(tu[u][:], 0.0)
                    pool.memset(S[u][:], 0.0)
                pool.drain().then_inc(zeroed, 1)

                def prepare(i, u):
                    hold(pool, K, gready, i * 2 + u + 1)
                    k, q = (comp[u][:, j * D:(j + 1) * D].rearrange("p (h d) -> p h d", h=H) for j in range(2))
                    wide = lambda x: x.unsqueeze(2).to_broadcast([128, H, DK])
                    pool.tensor_tensor(bg[:], comp[u][:, BETA:BETA + H], gam[u][:, 0, :], ALU.mult)
                    pool.drain()
                    pool.tensor_tensor(qg[u][:], q, wide(gam[u][:, 0, :]), ALU.mult)
                    pool.tensor_tensor(X[u][:, :, DK:2 * DK], k, wide(bg[:]), ALU.mult)
                    pool.tensor_tensor(kd[u][:], k, wide(gam[u][:, 1, :]), ALU.mult)
                    pool.drain().then_inc(pool_ready, 1)

                with pool.Fori(0, NGR - 1) as g:
                    for n in range(CG):
                        prepare(g * GB + n // 2, n % 2)
                        if n == 0:
                            hold(pool, K, r_free, g + 1)
                            unit(pool, inverse)
                            pool.drain()
                        elif n <= len(parts):
                            if n == 1:
                                hold(pool, K, b_in, (g + 1) * 16)
                            for m in parts[n - 1]:
                                take_off(pool, blocks, inverse, tmp, 0, H, m)
                            if n == len(parts):
                                pool.drain().then_inc(solved, 1)
                with pool.Fori(0, GB) as i:
                    for u in range(2):
                        prepare(i + (NGR - 1) * GB, u)

            @block.tensor
            def _(pe):
                pe.wait_ge(zeroed, 1)

                def step(i, u, a, m, b):
                    s, w = i * 2 + u, 1 - u

                    def solve(k, y):
                        for j in range(2):
                            if k == 1:
                                pe.wait_ge(ptready, s * 2 - 1 + j)
                                if b:
                                    pe.wait_ge(uwready, s * 2 - 3 + j)
                            else:
                                pe.wait_ge(yready, s * 6 - 6 + 2 * (k - 2) + j + 1)
                            for h in range(4 * j, 4 * j + 4):
                                mm = pe.matmul(bank(w, k, j)[:, h % 4, :], pt[:, h, :], y[:, h, :], start=True, stop=True)
                            mm.then_inc(yfull, 1)

                    if m:
                        pe.wait_ge(pool_ready, s)
                        pe.wait_ge(xv_ready, s)
                        solve(1, X[w])
                    if b:
                        pe.wait_ge(uwready, s * 2 - 2)
                        if m:
                            pe.wait_ge(qready, s)
                        for p in range(4):
                            mm = pe.transpose(qw[:, p, :], pair(uw[:, 1], p), K.ident[:])
                        mm.then_inc(wfull, 1)
                    if m:
                        solve(2, ya)
                    if b:
                        pe.wait_ge(sready, s - 1)
                        pe.wait_ge(wready, s - 1)
                        if m:
                            pe.wait_ge(gready, s)
                        for p in range(4):
                            mm = pe.matmul(ub[:, p * 128:(p + 1) * 128], wtn[:, p, :], S[u][:, p].rearrange("p a d -> p (a d)"), start=True, stop=True)
                        mm.then_inc(ufull, 1)
                    if m:
                        solve(3, yb)
                    if b:
                        pe.wait_ge(uready, s - 1)
                        for p in range(4):
                            mm = pe.matmul(sg[:, p].rearrange("p a d -> p (a d)"), pair(kd[u], p), pair(U, p), start=True, stop=True)
                        mm.then_inc(sfull, 1)
                    if a:
                        pe.wait_ge(c_in[u], (i + 1) * 16)
                        for j, mask in enumerate((K.upto, K.later, K.ones)):
                            mm = pe.matmul(ub[:, j * H:(j + 1) * H], mask[:], comp[u][:, DECAY:DECAY + H], start=True, stop=True)
                        mm.then_inc(gfull, 1)
                    if b:
                        pe.wait_ge(oready, s - 1)
                        pe.wait_ge(q_in[u], i * 16)
                        for p in range(4):
                            pe.matmul(ob[:, p * 128:(p + 1) * 128], qgT[u][:, p, :], S[u][:, p].rearrange("p a d -> p (a d)"),
                                      start=(p == 0), stop=False, skip_group_check=True)
                        for h in range(H):
                            mm = pe.matmul(ob[:, h * DK:(h + 1) * DK], qk[u][:, h, :], U[:, h, :], start=False, stop=True, skip_group_check=True)
                        mm.then_inc(ofull, 1)
                    if m:
                        pe.wait_ge(td_ready, s)
                        for j in range(2):
                            pe.wait_ge(yready, s * 6 - 1 + j)
                            for h in range(4 * j, 4 * j + 4):
                                mm = pe.matmul(bank(w, 4, j)[:, h % 4, :], td[w][:, h, :], ya[:, h, :], start=True, stop=True)
                            mm.then_inc(uwfull, 1)
                    if a:
                        pe.wait_ge(p_in[u], (i + 1) * 16)
                        pe.wait_ge(tu_ready, s + 1)
                        for j in range(2):
                            for h in range(4 * j, 4 * j + 4):
                                mm = pe.matmul(bank(u, 0, j)[:, h % 4, :], tu[u][:, h, :], np_[u][:, h, :], start=True, stop=True)
                            mm.then_inc(ptfull, 1)
                        pe.wait_ge(pool_ready, s + 1)
                        for p in range(4):
                            mm = pe.transpose(qw[:, p, :], pair(qg[u], p), K.ident[:])
                        mm.then_inc(qfull, 1)
                steps(pe, step)

            @block.scalar
            def _(act):
                act.wait_ge(zeroed, 1)

                def step(i, u, a, m, b):
                    s, w = i * 2 + u, 1 - u
                    if b:
                        act.wait_ge(wfull, s - 1)
                        act.activation(wtn[:], qw[:], ACT.Copy, scale=-1.0).then_inc(wready, 1)
                    if a:
                        act.wait_ge(gfull, s + 1)
                        act.activation(gam[u][:].rearrange("p j h -> p (j h)"), ub[:, 0:3 * H], ACT.Exp).then_inc(gready, 1)
                        act.wait_ge(t_in[u], (i + 1) * 16)
                        for q in range(4):
                            r = slice(32 * q, 32 * q + 32)
                            mm = act.activation(td[u][r, :, r], tt[u][r], ACT.Copy)
                        mm.then_inc(td_ready, 1)
                    if b:
                        act.wait_ge(ofull, s - 1)
                        act.wait_ge(o_free, s - 1)
                        act.activation(O[u][:], ob[:], ACT.Copy).then_inc(oready, 1)
                    if m:
                        for j in range(2):
                            act.wait_ge(uwfull, s * 2 - 1 + j)
                            act.activation(uw[:, :, 4 * j:4 * j + 4, :].rearrange("p v h d -> p h v d"),
                                           bank(w, 4, j)[:].rearrange("p h (v d) -> p h v d", v=2), ACT.Copy).then_inc(uwready, 1)
                    if a:
                        for j in range(2):
                            act.wait_ge(ptfull, s * 2 + j + 1)
                            act.activation(pt[:, 4 * j:4 * j + 4, :], bank(u, 0, j)[:], ACT.Copy).then_inc(ptready, 1)
                        act.wait_ge(qfull, s + 1)
                        act.activation(qgT[u][:], qw[:], ACT.Copy).then_inc(qready, 1)
                steps(act, step)

            @block.vector
            def _(dve):
                dve.wait_ge(zeroed, 1)
                for sem, n in ((sready, 1), (oready, 1), (o_free, 2), (r_free, 1)):
                    dve.drain().then_inc(sem, n)

                def step(i, u, a, m, b):
                    s, w = i * 2 + u, 1 - u

                    def subtract(k, y):
                        for j in range(2):
                            dve.wait_ge(yfull, s * 6 - 6 + (k - 1) * 2 + j + 1)
                            dve.tensor_tensor(y[:, 4 * j:4 * j + 4, :], X[w][:, 4 * j:4 * j + 4, :], bank(w, k, j)[:], ALU.subtract).then_inc(yready, 1)

                    if m:
                        subtract(1, ya)
                        subtract(2, yb)
                    if b:
                        for v in range(2):
                            dve.tensor_tensor(sd[half[v]], S[u][half[v], :, v, :], gk[u][half[v]].unsqueeze(2).to_broadcast([64, 4, DK]), ALU.mult)
                        dve.wait_ge(ufull, s - 1)
                        dve.tensor_tensor(U[:].rearrange("p h d -> p (h d)"), uw[:, 0].rearrange("p h d -> p (h d)"), ub[:], ALU.add).then_inc(uready, 1)
                    if m:
                        subtract(3, ya)
                    if b:
                        dve.wait_ge(sfull, s - 1)
                        for v in range(2):
                            dve.scalar_tensor_tensor(S[w][half[v], :, v, :], sg[half[v], :, v, :], keep[half[v], bass.ds(s - 1, 1)], sd[half[v]],
                                                     ALU.mult, ALU.add)
                        dve.drain().then_inc(sready, 1)
                    if a:
                        dve.wait_ge(t_in[u], (i + 1) * 16)
                        for q in range(4):
                            r = slice(32 * q, 32 * q + 32)
                            mm = dve.transpose(tu[u][r, :, r], tt[u][r])
                        mm.then_inc(tu_ready, 1)
                        dve.wait_ge(c_in[u], (i + 1) * 16)
                        dve.tensor_tensor(X[u][:, :, 0:DK], comp[u][:, V:V + D].rearrange("p (h d) -> p h d", h=H),
                                          comp[u][:, BETA:BETA + H].unsqueeze(2).to_broadcast([128, H, DK]), ALU.mult)
                        dve.wait_ge(gready, s + 1)
                        for v in range(2):
                            mm = dve.tensor_scalar(gk[u][half[v]], gam[u][half[v], 2, v:H:2], keep[half[v], bass.ds(s + 1, 1)], None, ALU.mult)
                        mm.then_inc(xv_ready, 1)
                steps(dve, step)


def finish(nc, K, h3T, x3, orows, w, weights, pos, out):
    with ExitStack() as ctx:
        P = Pools(nc, ctx, "g")
        wg, wo = P.sb("wg", [128, KC, D]), P.sb("wo", [128, KC, D])
        nw = P.sb("nw", [128, 1])
        feat = [P.sb(f"feat{u}", [128, KC, GR]) for u in range(2)]
        xin = [P.sb(f"xin{u}", [R, G, D]) for u in range(2)]
        ix = [[P.sb(f"ix{v}{s}", [R, 1], I32) for s in range(2)] for v in range(2)]
        o = [[P.sb(f"o{v}{s}", [R, D]) for s in range(2)] for v in range(2)]
        gate = [P.sb(f"gate{v}", [R, D]) for v in range(2)]
        core = P.sb("core", [R, D])
        gated = [P.sb(f"gated{v}", [R, D]) for v in range(2)]
        sq = P.sb("sq", [R, D])
        cT = [P.sb(f"cT{v}", [128, KC, R]) for v in range(2)]
        ss, inv, tmp = P.sb("ss", [R, H]), P.sb("inv", [R, H]), P.sb("tmp", [R, H])
        pg = [P.ps(f"pg{v}", [R, 512]) for v in range(2)]
        pt = [P.ps(f"pt{v}", [128, KC, R]) for v in range(2)]
        po = [P.ps(f"po{v}", [R, 512]) for v in range(2)]
        wld = P.sem("wld")
        f_in, x_in, x_out = P.sems("f_in"), P.sems("x_in"), P.sems("x_out")
        got = [[P.sem(f"got{v}{s}") for s in range(2)] for v in range(2)]
        wo_ready, core_made, squared = P.sem("wo_ready"), P.sem("core_made"), P.sem("squared")
        gfull, gready, cready, tfull, tready, pfull, pfree, group, o_free = (P.sem(n) for n in (
            "gfull", "gready", "cready", "tfull", "tready", "pfull", "pfree", "group", "o_free"))
        xrows, outrows = (a.rearrange("(n r) d -> r n d", r=R) for a in (x3, out))
        NB = NG // 2
        TB = 2 * G

        def steps(eng, step):
            for j in range(TB):
                step(0, j, True, j >= 1, j >= 2)
            with eng.Fori(0, NB - 1) as i:
                for j in range(TB):
                    step(i + 1, j, True, True, True)
            step(NB, 0, False, True, True)
            step(NB, 1, False, False, True)

        with nc.Block() as block:
            @block.sync
            def _(sp):
                sp.dma_start(wg[:], w["wg"].rearrange("(k p) n -> p k n", p=128)).then_inc(wld, 16)
                sp.dma_start(wo[:], w["wo"].rearrange("(k p) n -> p k n", p=128)).then_inc(wld, 16)
                for n in range(128 // DK):
                    sp.dma_start(nw[n * DK:(n + 1) * DK, :], w["nw"]).then_inc(wld, 16)

                def load_f(ig, u):
                    sp.dma_start(feat[u][:].rearrange("p k n -> p (k n)"), h3T[bass.ds(ig, 1), :, :].rearrange("a p n -> p (a n)")).then_inc(f_in[u], 16)

                def load_x(ig, u):
                    sp.dma_start(xin[u][:], xrows[:, bass.ds(ig * G, G), :]).then_inc(x_in[u], 16)

                def leave(i, u, more):
                    ig = i * 2 + u
                    if more:
                        sp.wait_ge(gfull, ig * G + G)
                        load_f(ig + 2, u)
                    sp.wait_ge(pfree, ig * G + G + 2)
                    sp.dma_start(outrows[:, bass.ds(ig * G, G), :], xin[u][:]).then_inc(x_out[u], 16)
                    sp.wait_ge(x_out[u], (i + 1) * 16)
                    if more:
                        load_x(ig + 2, u)
                for u in range(2):
                    load_f(u, u)
                    load_x(u, u)
                with sp.Fori(0, NB - 1) as i:
                    for u in range(2):
                        leave(i, u, True)
                for u in range(2):
                    leave(NB - 1, u, False)

            @block.gpsimd
            def _(pool):
                with pool.Fori(0, T // 2) as i:
                    for v in range(2):
                        t = i * 2 + v
                        hold(pool, K, cready, t + 1)
                        for s in range(2):
                            pool.tensor_copy(ix[v][s][:], pos[:, s, bass.ds(t, 1)])
                        pool.drain()
                        for s in range(2):
                            pool.indirect_dma_start(o[v][s][:], None, orows, bass.IndirectOffsetOnAxis(ap=ix[v][s][:, 0:1], axis=0),
                                                    bounds_check=NP + 127, oob_is_err=True).then_inc(got[v][s], 16)

            @block.tensor
            def _(pe):
                pe.wait_ge(wld, 16 * (2 + 128 // DK))
                pe.wait_ge(wo_ready, 1)
                def step(i, j, a, m, b):
                    t, v = i * TB + j, j % 2
                    if b:
                        pe.wait_ge(cready, t + 1)
                        for k in range(KC):
                            mm = pe.transpose(pt[v][:, k, :], gated[v][:, k * 128:(k + 1) * 128], K.ident[0:R, 0:R])
                        mm.then_inc(tfull, 1)
                    if a:
                        if j % G == 0:
                            pe.wait_ge(f_in[j // G], (i + 1) * 16)
                        pe.wait_ge(gready, t + 1)
                        g = j % G
                        for k in range(KC):
                            mm = pe.matmul(pg[v][:], feat[j // G][:, k, g * R:(g + 1) * R], wg[:, k, :], start=(k == 0), stop=(k == KC - 1))
                        mm.then_inc(gfull, 1)
                    if b:
                        pe.wait_ge(tready, t - 1)
                        pe.wait_ge(pfree, t - 1)
                        for k in range(KC):
                            mm = pe.matmul(po[v][:], cT[v][:, k, :], wo[:, k, :], start=(k == 0), stop=(k == KC - 1))
                        mm.then_inc(pfull, 1)
                steps(pe, step)

            @block.scalar
            def _(act):
                def step(i, j, a, m, b):
                    t, v = i * TB + j, j % 2
                    if b:
                        act.wait_ge(tfull, t - 1)
                        act.activation(cT[v][:], pt[v][:], ACT.Copy).then_inc(tready, 1)
                    if m:
                        act.wait_ge(core_made, t)
                        act.activation(sq[:], core[:], ACT.Square).then_inc(squared, 1)
                    if a:
                        act.wait_ge(gfull, t + 1)
                        act.wait_ge(cready, t + 1)
                        act.activation(gate[v][:], pg[v][:], ACT.Silu).then_inc(gready, 1)
                steps(act, step)

            @block.vector
            def _(dve):
                for s, n in ((gready, 2), (cready, 2), (pfree, 2)):
                    dve.drain().then_inc(s, n)
                dve.wait_ge(wld, 16 * (2 + 128 // DK))
                dve.tensor_scalar(wo[:], wo[:], nw[:, 0:1], None, ALU.mult)
                dve.drain().then_inc(wo_ready, 1)
                heads = lambda a: a.rearrange("p (h d) -> p h d", h=H)

                def step(i, j, a, m, b):
                    t, v = i * TB + j, j % 2
                    if m:
                        w = 1 - v
                        dve.wait_ge(got[w][0], (i * (TB // 2) + (j + 1) // 2) * 16)
                        dve.wait_ge(got[w][1], (i * (TB // 2) + (j + 1) // 2) * 16)
                        dve.tensor_scalar(o[w][0][:], o[w][0][:], weights[:, 0, bass.ds(t - 1, 1)], None, ALU.mult)
                        dve.drain()
                        dve.scalar_tensor_tensor(core[:], o[w][1][:], weights[:, 1, bass.ds(t - 1, 1)], o[w][0][:], ALU.mult, ALU.add)
                        dve.drain().then_inc(core_made, 1)
                        dve.wait_ge(gready, t + 2)
                        dve.tensor_tensor(gated[w][:], core[:], gate[w][:], ALU.mult)
                        dve.wait_ge(squared, t)
                        dve.tensor_reduce(ss[:], heads(sq[:]), AX.X, ALU.add)
                        dve.drain()
                        dve.tensor_scalar(ss[:], ss[:], 1.0 / DK, 1e-5, ALU.mult, ALU.add)
                        dve.drain()
                        rsqrt(dve, inv[:], ss[:], tmp[:])
                        dve.tensor_tensor(heads(gated[w][:]), heads(gated[w][:]), inv[:].unsqueeze(2).to_broadcast([R, H, DK]), ALU.mult)
                        dve.drain().then_inc(cready, 1)
                    if b:
                        u, g = (j - 2) // G % 2, (j - 2) % G
                        if g == 0:
                            dve.wait_ge(x_in[u], (i + 1) * 16)
                        dve.wait_ge(pfull, t - 1)
                        dve.tensor_tensor(xin[u][:, g, :], po[v][:], xin[u][:, g, :], ALU.add)
                        dve.drain().then_inc(pfree, 1)
                steps(dve, step)


INS = ("x", "src", "dst", "dstrows", "g1", "g2", "gb1", "gb2", "up", "gate", "gateb", "bup", "down", "bdown", "n1", "n2", "nb1", "nb2",
       "wl", "dtb", "alog", "wk", "wq", "wv", "wg", "wo", "nw")


def program(nc, a, out):
    def scratch(name, shape):
        return nc.dram_tensor(name, list(shape), F32, kind="Internal").ap()

    tables0 = [scratch(f"tables0{t}", (N + R, D + 1)) for t in range(2)]
    tables1 = [scratch(f"tables1{t}", (N + R, D)) for t in range(2)]
    x2, h2, x3, h3T = scratch("x2", (N, D)), scratch("h2", (N, D)), scratch("x3", (N, D)), scratch("h3T", (NG, 128, KC * GR))
    rows, orows = scratch("rows", (NP + 128, ROW)), scratch("orows", (NP + 128, D))
    ap, aq = scratch("ap", (NCH, 128, H * CH)), scratch("aq", (NCH, 128, H * CH))
    diag, inv = scratch("diag", (NCH, 128, H * 32)), scratch("inv", (NCH, 128, H * 32))
    with ExitStack() as ctx:
        K = Consts()
        K.pool = Pools(nc, ctx, "k")
        constants(nc, K)
        aggregate(nc, K, "a", a["src"], a["dst"], a["dstrows"], a["x"], tables0, True)
        first_layer(nc, K, a["x"], tables0, a, x2, h2, rows, tables1)
        aggregate(nc, K, "n", a["src"], a["dst"], a["dstrows"], h2, tables1, False)
        weights, pos = K.pool.sb("weights", [R, 2, T]), K.pool.sb("pos", [R, 2, T], I32)
        keep = K.pool.sb("keep", [128, NCH + 1])
        with ExitStack() as until_rows:
            P = Pools(nc, until_rows, "kr")
            beta, decay, logits = P.sb("beta", [R, T, H]), P.sb("decay", [R, T, H]), P.sb("logits", [R, T, NL])
            second_gnn(nc, K, h2, tables1, x2, a, x3, h3T, logits)
            route(nc, K, logits, a, weights, pos, beta, decay, keep)
            project(nc, K, h3T, a, pos, beta, decay, rows)
        chunk_products(nc, K, rows, ap, aq, diag)
        solve_first(nc, K, diag, inv)
        recur(nc, K, rows, ap, aq, diag, inv, keep, orows)
        finish(nc, K, h3T, x3, orows, a, weights, pos, out)


def kernel(**inputs):
    import numpy as np
    import concourse.bacc as bacc
    from concourse.bass_utils import run_bass_kernel_spmd

    v = {k: np.asarray(a) for k, a in inputs.items()}
    f = lambda name: v["L0_ffn_" + name]
    g = lambda name: v["L1_ffn_" + name]
    laid = {
        "x": v["x"], "src": v["src"].reshape(T // V4, V4, R).transpose(0, 2, 1), "dst": v["dst"].reshape(T // V4, V4, R).transpose(0, 2, 1),
        "dstrows": v["dst"].reshape(T, R),
        "g1": v["L0_gnn_W1"].T, "g2": v["L0_gnn_W2"].T, "gb1": v["L0_gnn_b1"][None], "gb2": v["L0_gnn_b2"][None],
        "up": np.concatenate([f("sw1").reshape(-1, D), f("rw1").reshape(-1, D)]).T, "gate": f("gate_w").T,
        "gateb": f("gate_b")[None], "bup": np.concatenate([f("sb1").ravel(), f("rb1").ravel()]).reshape(HC, 128).T,
        "down": np.concatenate([f("sw2").transpose(0, 2, 1).reshape(-1, D), f("rw2").transpose(0, 2, 1).reshape(-1, D)]),
        "bdown": np.concatenate([f("rb2"), f("sb2")]),
        "n1": v["L1_gnn_W1"], "n2": v["L1_gnn_W2"], "nb1": v["L1_gnn_b1"].reshape(KC, 128).T, "nb2": v["L1_gnn_b2"][None],
        "wl": np.concatenate([g("Wgate"), g("Wb"), g("Wa")], axis=1), "dtb": g("dt_bias")[None], "alog": g("A_log")[None],
        "wk": g("Wk"), "wq": g("Wq"), "wv": g("Wv"), "wg": g("Wg"), "wo": g("Wo"), "nw": g("o_norm_weight")[:, None],
    }
    nc = bacc.Bacc("TRN2", target_bir_lowering=False, num_devices=1)
    arrays, aps = {}, {}
    for name in INS:
        a = np.ascontiguousarray(laid[name])
        arrays[f"in_{name}"] = a
        aps[name] = nc.dram_tensor(f"in_{name}", a.shape, mybir.dt.from_np(a.dtype), kind="ExternalInput").ap()
    out = nc.dram_tensor("out", (N, D), F32, kind="ExternalOutput").ap()
    program(nc, aps, out)
    return run_bass_kernel_spmd(nc, [arrays], core_ids=[0]).results[0]["out"]
```
